# Optimizing a Trainium2 kernel written in Bass

```python
import numpy as np
import jax
import jax.numpy as jnp

def _softmax(x, axis=-1):
    return jax.nn.softmax(x, axis=axis)

def _gelu(x):
    return jax.nn.gelu(x, approximate=True)

def _silu(x):
    return jax.nn.silu(x)

def _sigmoid(x):
    return jax.nn.sigmoid(x)

def _layernorm(x, axis=-1, eps=1e-05):
    m = jnp.mean(x, axis=axis, keepdims=True)
    v = jnp.var(x, axis=axis, keepdims=True)
    return (x - m) / jnp.sqrt(v + eps)

def _scatter_add(tgt, idx, src, axis=0):
    return tgt.at[idx].add(src)

def _segment_sum(src, seg, n):
    return jax.ops.segment_sum(src, seg, n)
kernel_name = 'mk_lm_tower_d2_tok_ids256_r4_2b14bd'

def setup_inputs(seed: int=0):
    np.random.seed(seed)
    _w = jnp.asarray

    def _rec_inputs():
        import jax
        import jax.numpy as jnp
        _rk = jax.random.key(seed)
        x = jax.random.randint(jax.random.fold_in(_rk, 1), (16, 1024), 0, 64, jnp.int32)
        itok_BS_0_255 = jax.random.randint(jax.random.fold_in(_rk, 21), (16, 1024), 0, 64, jnp.int32)
        itok_BS_0_511 = jax.random.randint(jax.random.fold_in(_rk, 22), (16, 1024), 0, 128, jnp.int32)
        itok_BS_0_127 = jax.random.randint(jax.random.fold_in(_rk, 23), (16, 1024), 0, 128, jnp.int32)
        itok_BS_0_63 = jax.random.randint(jax.random.fold_in(_rk, 24), (16, 1024), 0, 64, jnp.int32)
        itok_BS_0_3 = jax.random.randint(jax.random.fold_in(_rk, 25), (16, 1024), 0, 4, jnp.int32)
        return (x, itok_BS_0_255, itok_BS_0_511, itok_BS_0_127, itok_BS_0_63, itok_BS_0_3)
    x, itok_BS_0_255, itok_BS_0_511, itok_BS_0_127, itok_BS_0_63, itok_BS_0_3 = _rec_inputs()

    def _L0_tok_setup():
        import jax, jax.numpy as jnp
        import numpy as np
        B, S = (128, 512)
        D_OUT = 64
        EMB = 16
        EPS_W = 1e-08
        EPS_LN = 1e-05

        def ternary_linear(x, W, b):
            scale = jnp.mean(jnp.abs(W))
            w_q = jnp.clip(jnp.round(W / (scale + EPS_W)), -1.0, 1.0) * scale
            w_eff = W + jax.lax.stop_gradient(w_q - W)
            return jnp.einsum('bsk,ok->bso', x, w_eff) + b

        def layer_norm(x, gamma, beta):
            mu = jnp.mean(x, axis=-1, keepdims=True)
            var = jnp.mean(jnp.square(x - mu), axis=-1, keepdims=True)
            return (x - mu) * jax.lax.rsqrt(var + EPS_LN) * gamma + beta
        key = jax.random.key(seed)
        ks = jax.random.split(key, 16)
        vocabs = {'event_type': 64, 'fault_class': 64, 'syscall_class': 128, 'opcode_family': 128, 'transition_type': 64, 'result_class': 4}
        inp = {}
        for i, (name, v) in enumerate(vocabs.items()):
            inp[name] = jax.random.randint(ks[i], (B, S), 0, v, dtype=jnp.int64)
        inp['E_et'] = jax.random.normal(ks[6], (64, EMB), dtype=jnp.float32)
        inp['E_fc'] = jax.random.normal(ks[7], (64, EMB), dtype=jnp.float32)
        inp['E_sc'] = jax.random.normal(ks[8], (128, EMB), dtype=jnp.float32)
        inp['E_of'] = jax.random.normal(ks[9], (128, EMB), dtype=jnp.float32)
        inp['E_tt'] = jax.random.normal(ks[10], (64, EMB), dtype=jnp.float32)
        inp['E_rc'] = jax.random.normal(ks[11], (4, EMB), dtype=jnp.float32)
        inp['W'] = jax.random.normal(ks[12], (D_OUT, 96), dtype=jnp.float32) * 0.1
        inp['b'] = jnp.zeros((D_OUT,), dtype=jnp.float32)
        inp['gamma'] = jnp.ones((D_OUT,), dtype=jnp.float32)
        inp['beta'] = jnp.zeros((D_OUT,), dtype=jnp.float32)
        return inp
    _L0_tok_all = _L0_tok_setup()
    _L0_tok_in = {k: v for k, v in _L0_tok_all.items() if k in ('E_et', 'E_fc', 'E_sc', 'E_of', 'E_tt', 'E_rc', 'W', 'b', 'gamma', 'beta')}
    del _L0_tok_all

    def _L0_attn_setup():
        import jax, jax.numpy as jnp
        import numpy as np
        NUM_HEADS = 8
        key = jax.random.key(seed)
        ks = jax.random.split(key, 5)
        B, N, C = (8, 4096, 64)
        x = jax.random.normal(ks[0], (B, N, C), dtype=jnp.float32)
        Wq = jax.random.normal(ks[1], (C, C), dtype=jnp.float32) * 0.02
        Wkv = jax.random.normal(ks[2], (2 * C, C), dtype=jnp.float32) * 0.02
        Wproj = jax.random.normal(ks[3], (C, C), dtype=jnp.float32) * 0.02
        bproj = jnp.zeros((C,), dtype=jnp.float32)
        return {'x': x, 'Wq': Wq, 'Wkv': Wkv, 'Wproj': Wproj, 'bproj': bproj}
    _L0_attn_all = _L0_attn_setup()
    _L0_attn_in = {k: v for k, v in _L0_attn_all.items() if k in ('Wq', 'Wkv', 'Wproj', 'bproj')}
    del _L0_attn_all

    def _L0_ffn_setup():
        import jax, jax.numpy as jnp
        import numpy as np
        C = 64
        HID = 256
        E = 8
        TEMP = 1.0
        key = jax.random.key(seed)
        ks = jax.random.split(key, 7)
        x = jax.random.normal(ks[0], (8, 4096, C), dtype=jnp.float32)
        W1 = jax.random.normal(ks[1], (C, HID), dtype=jnp.float32) * 0.02
        b1 = jnp.zeros((HID,), dtype=jnp.float32)
        Wg = jax.random.normal(ks[2], (HID, E), dtype=jnp.float32) * 0.02
        bg = jnp.zeros((E,), dtype=jnp.float32)
        Wd = jax.random.normal(ks[3], (E, HID, C), dtype=jnp.float32) * 0.02
        bd = jnp.zeros((E, C), dtype=jnp.float32)
        return {'x': x, 'W1': W1, 'b1': b1, 'Wg': Wg, 'bg': bg, 'Wd': Wd, 'bd': bd}
    _L0_ffn_all = _L0_ffn_setup()
    _L0_ffn_in = {k: v for k, v in _L0_ffn_all.items() if k in ('W1', 'b1', 'Wg', 'bg', 'Wd', 'bd')}
    del _L0_ffn_all

    def _L1_attn_setup():
        import jax, jax.numpy as jnp
        import numpy as np
        IN_C = 64
        HID_C = 64
        HEADS = 8
        SCALE = 1.0 / np.sqrt(HID_C / HEADS).astype(np.float32)
        key = jax.random.key(seed)
        k_v, k_q, k_k, k_w, k_o, k_b = jax.random.split(key, 6)
        B, S = (4, 512)
        lim_in = 1.0 / np.sqrt(IN_C)
        lim_out = 1.0 / np.sqrt(IN_C * HEADS)
        v = jax.random.normal(k_v, (B, S, IN_C), dtype=jnp.float32)
        WQ = jax.random.uniform(k_q, (IN_C, IN_C * HEADS), jnp.float32, -lim_in, lim_in)
        WK = jax.random.uniform(k_k, (IN_C, IN_C * HEADS), jnp.float32, -lim_in, lim_in)
        WV = jax.random.uniform(k_w, (IN_C, IN_C * HEADS), jnp.float32, -lim_in, lim_in)
        Wout = jax.random.uniform(k_o, (IN_C * HEADS, HID_C), jnp.float32, -lim_out, lim_out)
        bout = jax.random.uniform(k_b, (HID_C,), jnp.float32, -lim_out, lim_out)
        return {'v': v, 'WQ': WQ, 'WK': WK, 'WV': WV, 'Wout': Wout, 'bout': bout}
    _L1_attn_all = _L1_attn_setup()
    _L1_attn_in = {k: v for k, v in _L1_attn_all.items() if k in ('WQ', 'WK', 'WV', 'Wout', 'bout')}
    del _L1_attn_all

    def _L1_ffn_setup():
        import jax, jax.numpy as jnp
        import numpy as np
        B, S, H, NH, NE = (4, 256, 64, 4, 4)
        D = H // NH
        EPS = 1e-08

        def layernorm(x, g, b):
            m = jnp.mean(x, axis=-1, keepdims=True)
            v = jnp.mean((x - m) ** 2, axis=-1, keepdims=True)
            return (x - m) / jnp.sqrt(v + EPS) * g + b
        key = jax.random.key(seed)
        ks = jax.random.split(key, 18)
        sc = 0.05
        return {'x': jax.random.normal(ks[0], (B, S, H), jnp.float32), 'hl_w': jax.random.normal(ks[1], (NH, D, H), jnp.float32) * sc, 'hl_b': jax.random.normal(ks[2], (NH, D), jnp.float32) * sc, 'wq': jax.random.normal(ks[3], (NH, NE, D, D), jnp.float32) * sc, 'wk': jax.random.normal(ks[4], (NH, D, D), jnp.float32) * sc, 'wv': jax.random.normal(ks[5], (NH, D, D), jnp.float32) * sc, 'gate_w': jax.random.normal(ks[6], (NH, NE, NE * D), jnp.float32) * sc, 'gate_b': jax.random.normal(ks[7], (NH, NE), jnp.float32) * sc, 'ln_g': jnp.ones((D,), jnp.float32), 'ln_b': jnp.zeros((D,), jnp.float32), 'fc1_w': jax.random.normal(ks[8], (D, D), jnp.float32) * sc, 'fc1_b': jax.random.normal(ks[9], (D,), jnp.float32) * sc, 'fc2_w': jax.random.normal(ks[10], (D, D), jnp.float32) * sc, 'fc2_b': jax.random.normal(ks[11], (D,), jnp.float32) * sc, 'fnorm_g': jnp.ones((D,), jnp.float32), 'fnorm_b': jnp.zeros((D,), jnp.float32), 'fgate_w': jax.random.normal(ks[12], (NH, H), jnp.float32) * sc}
    _L1_ffn_all = _L1_ffn_setup()
    _L1_ffn_in = {k: v for k, v in _L1_ffn_all.items() if k in ('hl_w', 'hl_b', 'wq', 'wk', 'wv', 'gate_w', 'gate_b', 'ln_g', 'ln_b', 'fc1_w', 'fc1_b', 'fc2_w', 'fc2_b', 'fnorm_g', 'fnorm_b', 'fgate_w')}
    del _L1_ffn_all
    return {'x': x, 'itok_BS_0_255': itok_BS_0_255, 'itok_BS_0_511': itok_BS_0_511, 'itok_BS_0_127': itok_BS_0_127, 'itok_BS_0_63': itok_BS_0_63, 'itok_BS_0_3': itok_BS_0_3, 'L0_tok_E_et': _L0_tok_in['E_et'], 'L0_tok_E_fc': _L0_tok_in['E_fc'], 'L0_tok_E_sc': _L0_tok_in['E_sc'], 'L0_tok_E_of': _L0_tok_in['E_of'], 'L0_tok_E_tt': _L0_tok_in['E_tt'], 'L0_tok_E_rc': _L0_tok_in['E_rc'], 'L0_tok_W': _L0_tok_in['W'], 'L0_tok_b': _L0_tok_in['b'], 'L0_tok_gamma': _L0_tok_in['gamma'], 'L0_tok_beta': _L0_tok_in['beta'], 'L0_attn_Wq': _L0_attn_in['Wq'], 'L0_attn_Wkv': _L0_attn_in['Wkv'], 'L0_attn_Wproj': _L0_attn_in['Wproj'], 'L0_attn_bproj': _L0_attn_in['bproj'], 'L0_ffn_W1': _L0_ffn_in['W1'], 'L0_ffn_b1': _L0_ffn_in['b1'], 'L0_ffn_Wg': _L0_ffn_in['Wg'], 'L0_ffn_bg': _L0_ffn_in['bg'], 'L0_ffn_Wd': _L0_ffn_in['Wd'], 'L0_ffn_bd': _L0_ffn_in['bd'], 'L1_attn_WQ': _L1_attn_in['WQ'], 'L1_attn_WK': _L1_attn_in['WK'], 'L1_attn_WV': _L1_attn_in['WV'], 'L1_attn_Wout': _L1_attn_in['Wout'], 'L1_attn_bout': _L1_attn_in['bout'], 'L1_ffn_hl_w': _L1_ffn_in['hl_w'], 'L1_ffn_hl_b': _L1_ffn_in['hl_b'], 'L1_ffn_wq': _L1_ffn_in['wq'], 'L1_ffn_wk': _L1_ffn_in['wk'], 'L1_ffn_wv': _L1_ffn_in['wv'], 'L1_ffn_gate_w': _L1_ffn_in['gate_w'], 'L1_ffn_gate_b': _L1_ffn_in['gate_b'], 'L1_ffn_ln_g': _L1_ffn_in['ln_g'], 'L1_ffn_ln_b': _L1_ffn_in['ln_b'], 'L1_ffn_fc1_w': _L1_ffn_in['fc1_w'], 'L1_ffn_fc1_b': _L1_ffn_in['fc1_b'], 'L1_ffn_fc2_w': _L1_ffn_in['fc2_w'], 'L1_ffn_fc2_b': _L1_ffn_in['fc2_b'], 'L1_ffn_fnorm_g': _L1_ffn_in['fnorm_g'], 'L1_ffn_fnorm_b': _L1_ffn_in['fnorm_b'], 'L1_ffn_fgate_w': _L1_ffn_in['fgate_w']}

def reference(x, itok_BS_0_255, itok_BS_0_511, itok_BS_0_127, itok_BS_0_63, itok_BS_0_3, L0_tok_E_et, L0_tok_E_fc, L0_tok_E_sc, L0_tok_E_of, L0_tok_E_tt, L0_tok_E_rc, L0_tok_W, L0_tok_b, L0_tok_gamma, L0_tok_beta, L0_attn_Wq, L0_attn_Wkv, L0_attn_Wproj, L0_attn_bproj, L0_ffn_W1, L0_ffn_b1, L0_ffn_Wg, L0_ffn_bg, L0_ffn_Wd, L0_ffn_bd, L1_attn_WQ, L1_attn_WK, L1_attn_WV, L1_attn_Wout, L1_attn_bout, L1_ffn_hl_w, L1_ffn_hl_b, L1_ffn_wq, L1_ffn_wk, L1_ffn_wv, L1_ffn_gate_w, L1_ffn_gate_b, L1_ffn_ln_g, L1_ffn_ln_b, L1_ffn_fc1_w, L1_ffn_fc1_b, L1_ffn_fc2_w, L1_ffn_fc2_b, L1_ffn_fnorm_g, L1_ffn_fnorm_b, L1_ffn_fgate_w):
    import jax
    import jax.numpy as jnp

    def _L0_tok_ref(event_type, fault_class, syscall_class, opcode_family, transition_type, result_class, E_et, E_fc, E_sc, E_of, E_tt, E_rc, W, b, gamma, beta):
        import jax, jax.numpy as jnp
        import numpy as np
        B, S = (128, 512)
        D_OUT = 64
        EMB = 16
        EPS_W = 1e-08
        EPS_LN = 1e-05

        def ternary_linear(x, W, b):
            scale = jnp.mean(jnp.abs(W))
            w_q = jnp.clip(jnp.round(W / (scale + EPS_W)), -1.0, 1.0) * scale
            w_eff = W + jax.lax.stop_gradient(w_q - W)
            return jnp.einsum('bsk,ok->bso', x, w_eff) + b

        def layer_norm(x, gamma, beta):
            mu = jnp.mean(x, axis=-1, keepdims=True)
            var = jnp.mean(jnp.square(x - mu), axis=-1, keepdims=True)
            return (x - mu) * jax.lax.rsqrt(var + EPS_LN) * gamma + beta
        combined = jnp.concatenate([E_et[event_type], E_fc[fault_class], E_sc[syscall_class], E_of[opcode_family], E_tt[transition_type], E_rc[result_class]], axis=-1)
        z = ternary_linear(combined, W, b)
        return layer_norm(z, gamma, beta)

    def _L0_attn_ref(x, Wq, Wkv, Wproj, bproj):
        import jax, jax.numpy as jnp
        import numpy as np
        NUM_HEADS = 8
        B, N, C = x.shape
        h = NUM_HEADS
        d = C // h
        q = jnp.einsum('bnc,oc->bno', x, Wq).reshape(B, N, h, d).transpose(0, 2, 1, 3)
        kv = jnp.einsum('bnc,oc->bno', x, Wkv).reshape(B, N, 2, h, d)
        k = kv[:, :, 0].transpose(0, 2, 1, 3)
        v = kv[:, :, 1].transpose(0, 2, 1, 3)
        q = jax.nn.elu(q) + 1.0
        k = jax.nn.elu(k) + 1.0
        k_sum = k.sum(axis=2)
        D_inv = 1.0 / jnp.maximum(jnp.einsum('bhnd,bhd->bhn', q, k_sum), 1e-06)
        context = jnp.einsum('bhnd,bhne->bhde', k, v)
        attn = jnp.einsum('bhnd,bhde->bhne', q, context) * D_inv[..., None]
        out = attn.transpose(0, 2, 1, 3).reshape(B, N, C)
        out = jnp.einsum('bnc,oc->bno', out, Wproj) + bproj
        return out

    def _L0_ffn_ref(x, W1, b1, Wg, bg, Wd, bd):
        import jax, jax.numpy as jnp
        import numpy as np
        C = 64
        HID = 256
        E = 8
        TEMP = 1.0
        orig_shape = x.shape
        xf = x.reshape(-1, orig_shape[-1])
        H = jax.nn.gelu(xf @ W1 + b1, approximate=False)
        probs = jax.nn.softmax((H @ Wg + bg) / TEMP, axis=-1)
        assign = jnp.argmax(probs, axis=-1)
        out = jnp.zeros_like(xf)
        for e in range(Wd.shape[0]):
            y = H @ Wd[e] + bd[e]
            sel = (assign == e)[:, None]
            out = out + jnp.where(sel, probs[:, e:e + 1] * y, 0.0)
        return out.reshape(orig_shape)

    def _L1_attn_ref(v, WQ, WK, WV, Wout, bout):
        import jax, jax.numpy as jnp
        import numpy as np
        IN_C = 64
        HID_C = 64
        HEADS = 8
        SCALE = 1.0 / np.sqrt(HID_C / HEADS).astype(np.float32)
        B, S, C = v.shape
        H = HEADS
        q = (v @ WQ).reshape(B, S, H, C)
        k = (v @ WK).reshape(B, S, H, C)
        val = (v @ WV).reshape(B, S, H, C)
        scores = jnp.einsum('bshc,bthc->bsth', q, k) * SCALE
        A = jax.nn.softmax(scores, axis=2)
        u = jnp.einsum('bsth,bthc->bshc', A, val).reshape(B, S, H * C)
        return u @ Wout + bout

    def _L1_ffn_ref(x, hl_w, hl_b, wq, wk, wv, gate_w, gate_b, ln_g, ln_b, fc1_w, fc1_b, fc2_w, fc2_b, fnorm_g, fnorm_b, fgate_w):
        import jax, jax.numpy as jnp
        import numpy as np
        B, S, H, NH, NE = (4, 256, 64, 4, 4)
        D = H // NH
        EPS = 1e-08

        def layernorm(x, g, b):
            m = jnp.mean(x, axis=-1, keepdims=True)
            v = jnp.mean((x - m) ** 2, axis=-1, keepdims=True)
            return (x - m) / jnp.sqrt(v + EPS) * g + b
        b, s, h = x.shape
        nh, d, _ = wk.shape
        ne = wq.shape[1]
        sx = jnp.einsum('bsh,ndh->bnsd', x, hl_w) + hl_b[None, :, None, :]
        pad = sx == 0
        q = jnp.einsum('bnsd,neod->bneso', sx, wq)
        k = jnp.einsum('bnsd,nod->bnso', sx, wk)
        v = jnp.einsum('bnsd,nod->bnso', sx, wv)
        causal = jnp.where(jnp.tril(jnp.ones((s, s), bool)), 0.0, -jnp.inf).astype(x.dtype)
        scores = jnp.einsum('bnesd,bntd->bnest', q, k) * d ** 0.5 + causal
        att = jax.nn.softmax(scores, axis=-1)
        qkv = jnp.einsum('bnest,bntd->bnesd', att, v)
        qkv = jnp.where(pad[:, :, None], 0.0, qkv)
        out = jnp.transpose(qkv, (0, 1, 3, 2, 4)).reshape(b, nh, s, ne * d)
        gs = jax.nn.softmax(jnp.einsum('bnsf,nef->bnse', out, gate_w) + gate_b[None, :, None, :], axis=-1)
        mixed = jnp.einsum('bnsed,bnse->bnsd', out.reshape(b, nh, s, ne, d), gs)
        resid = sx[jnp.arange(nh), jnp.arange(nh)]
        hn = layernorm(mixed + resid, ln_g, ln_b)
        f_n = jnp.transpose(hn, (0, 2, 1, 3)).reshape(b, s, h)
        fx = f_n.reshape(b, s, nh, d)
        pm = fx == 0
        hx = jnp.where(pm, 0.0, fx @ fc1_w.T + fc1_b)
        hx = jax.nn.relu(hx)
        hx = jnp.where(pm, 0.0, hx @ fc2_w.T + fc2_b)
        hx = layernorm(hx + fx, fnorm_g, fnorm_b)
        fout = hx.reshape(b, s, h)
        fg = jax.nn.softmax(fout @ fgate_w.T, axis=-1)
        return (fout.reshape(b, s, nh, d) * fg[..., None]).reshape(b, s, h)
    h = _L0_tok_ref(x, itok_BS_0_255, itok_BS_0_511, itok_BS_0_127, itok_BS_0_63, itok_BS_0_3, L0_tok_E_et, L0_tok_E_fc, L0_tok_E_sc, L0_tok_E_of, L0_tok_E_tt, L0_tok_E_rc, L0_tok_W, L0_tok_b, L0_tok_gamma, L0_tok_beta)
    h = h + _L0_attn_ref(_layernorm(h, axis=-1), L0_attn_Wq, L0_attn_Wkv, L0_attn_Wproj, L0_attn_bproj)
    h = h + _L0_ffn_ref(_layernorm(h, axis=-1), L0_ffn_W1, L0_ffn_b1, L0_ffn_Wg, L0_ffn_bg, L0_ffn_Wd, L0_ffn_bd)
    h = h + _L1_attn_ref(_layernorm(h, axis=-1), L1_attn_WQ, L1_attn_WK, L1_attn_WV, L1_attn_Wout, L1_attn_bout)
    h = h + _L1_ffn_ref(_layernorm(h, axis=-1), L1_ffn_hl_w, L1_ffn_hl_b, L1_ffn_wq, L1_ffn_wk, L1_ffn_wv, L1_ffn_gate_w, L1_ffn_gate_b, L1_ffn_ln_g, L1_ffn_ln_b, L1_ffn_fc1_w, L1_ffn_fc1_b, L1_ffn_fc2_w, L1_ffn_fc2_b, L1_ffn_fnorm_g, L1_ffn_fnorm_b, L1_ffn_fgate_w)
    return h

_drawn_inputs = setup_inputs


def setup_inputs(seed=0):
    import zlib

    import numpy as np

    out = dict(_drawn_inputs(seed))
    spreads = {'L0_tok_b': (0.0, 0.1),
     'L0_tok_gamma': (1.0, 0.2),
     'L0_tok_beta': (0.0, 0.1),
     'L0_attn_bproj': (0.0, 0.1),
     'L0_ffn_b1': (0.0, 0.8),
     'L0_ffn_bg': (0.0, 0.429),
     'L0_ffn_bd': (0.0, 0.618),
     'L1_ffn_ln_g': (1.0, 0.6),
     'L1_ffn_ln_b': (0.0, 0.339),
     'L1_ffn_fnorm_g': (1.0, 0.574),
     'L1_ffn_fnorm_b': (0.0, 0.318)}
    factors = {'L0_attn_Wq': 8.0,
     'L0_attn_Wkv': 6.29,
     'L0_attn_Wproj': 6.472,
     'L0_ffn_W1': 8.0,
     'L0_ffn_Wg': 8.0,
     'L0_ffn_Wd': 8.0,
     'L1_ffn_wq': 34.215,
     'L1_ffn_wk': 38.063,
     'L1_ffn_gate_w': 64.0,
     'L1_ffn_gate_b': 64.0,
     'L1_ffn_fc1_w': 8.0,
     'L1_ffn_fc1_b': 8.0,
     'L1_ffn_fc2_w': 6.227,
     'L1_ffn_fc2_b': 10.852,
     'L1_attn_bout': 4.18,
     'L1_ffn_hl_b': 3.456,
     'L1_ffn_wv': 3.548}
    for name, (base, spread) in spreads.items():
        noise = np.random.default_rng([zlib.crc32(name.encode()), seed]).standard_normal(out[name].shape)
        drawn = base * np.exp(spread * noise) if base else spread * noise
        out[name] = jnp.asarray(drawn.astype(out[name].dtype))
    for name, factor in factors.items():
        out[name] = (out[name] * factor).astype(out[name].dtype)
    return out
```

```python
from contextlib import ExitStack

import numpy as np

import concourse.bass as bass
from concourse import mybir

F32 = mybir.dt.float32
BF16 = mybir.dt.bfloat16
FP16 = mybir.dt.float16
I32 = mybir.dt.int32
ACT = mybir.ActivationFunctionType
ALU = mybir.AluOpType
X = mybir.AxisListType.X
XY = mybir.AxisListType.XY
ds = bass.ds

P = 128
S = 1024
T = S // P
HALF = 512
C = 64
HEADS = 8
HID = 256
EXPERTS = 8
NH, NE, D = 4, 4, 16
VR = 96
SLOTS = 8
BIG = -1.0e30
WSPAN = 512.0
MSPAN = 32768.0
EPS_W, EPS_LN, EPS_FFN = 1e-8, 1e-5, 1e-8


class Parts:
    pass


def load_weights(k, nc, a):
    sb = k.sb
    k.ident = sb("ident", [P, P], F32)
    k.identb = sb("identb", [P, P], BF16)
    k.identh = sb("identh", [P, P], FP16)
    k.ones = sb("ones", [P, P], F32)
    k.onesb = sb("onesb", [P, P], BF16)
    k.tab3 = sb("tab3", [P, 4, 3, C], BF16)
    k.sel = sb("sel", [6, 8, C], BF16)
    k.vcol = sb("vcol", [P, 4], F32)
    k.tok_b = sb("tok_b", [P, C], F32)
    k.tok_g = sb("tok_g", [P, C], F32)
    k.tok_beta = sb("tok_beta", [P, C], F32)
    k.eps_ln = sb("eps_ln", [P, 1], F32)
    k.eps_ffn = sb("eps_ffn", [P, 1], F32)
    k.wqT = sb("wqT", [C, C], F32)
    k.wkvT = sb("wkvT", [C, 2 * C], F32)
    k.wpT = sb("wpT", [C, C], F32)
    k.bproj = sb("bproj", [P, C], F32)
    k.blk8 = sb("blk8", [C, C], F32)
    k.w1 = sb("w1", [C, HID], F32)
    k.b1 = sb("b1", [P, 2], F32)
    k.wg = sb("wg", [P, 2, EXPERTS], F32)
    k.bg = sb("bg", [P, EXPERTS], F32)
    k.wd = sb("wd", [P, 2, EXPERTS, C], F32)
    k.bd3 = sb("bd3", [3, EXPERTS * C], BF16)
    k.rank = sb("rank", [P, EXPERTS], F32)
    k.escale = sb("escale", [P, 1], F32)
    k.vscale = sb("vscale", [P, 1], F32)
    k.wqk_hi = sb("wqk_hi", [P, 2, HEADS, 2, C], FP16)
    k.wqk_lo = sb("wqk_lo", [P, 2, HEADS, 2, C], FP16)
    k.wvo_hi = sb("wvo_hi", [P, HEADS * C], FP16)
    k.wvo_lo = sb("wvo_lo", [P, HEADS * C], FP16)
    k.bout = sb("bout", [P, C], F32)
    k.gq = sb("gq", [C + 1, NH, NE, SLOTS, D], F32)
    k.gk = sb("gk", [C + 1, NH, SLOTS, D], F32)
    k.gsv = sb("gsv", [C + 1, 2 * C], F32)
    k.gatew = sb("gatew", [P, NH, NE, NE * D], F32)
    k.gateb = sb("gateb", [P, NH, NE], F32)
    k.lnp = sb("lnp", [P, 4, D], F32)
    k.fcT = sb("fcT", [C, 2, C], F32)
    k.fcb = sb("fcb", [C, 2], F32)
    k.fgT = sb("fgT", [C, NH], F32)
    k.mask_q = sb("mask_q", [P, P], BF16)
    k.mask_k = sb("mask_k", [P, P], BF16)
    k.part = sb("part", [P, 4], F32)
    tmp = k.tmp
    k.eblk = tmp("eblk", [P, 4, VR], F32)
    k.eblkT = tmp("eblkT", [VR, 4, P], F32)
    k.w = tmp("w", [C, VR], F32)
    k.wtmp = tmp("wtmp", [C, 4, VR], F32)
    k.wcol = tmp("wcol", [C, 4], F32)
    k.weffT = tmp("weffT", [VR, C], F32)
    k.tab = tmp("tab", [P, 4, C], F32)
    k.tabr = tmp("tabr", [P, 4, C], F32)
    k.vint = tmp("vint", [P, 1], I32)
    k.wqn = tmp("wqn", [C, C], F32)
    k.wkvn = tmp("wkvn", [2 * C, C], F32)
    k.wpn = tmp("wpn", [C, C], F32)
    k.bd1 = tmp("bd1", [1, EXPERTS * C], F32)
    k.bds = tmp("bds", [1, 3, EXPERTS * C], BF16)
    k.bdr = tmp("bdr", [1, EXPERTS * C], F32)
    k.ranki = tmp("ranki", [P, EXPERTS], I32)
    k.aq = tmp("aq", [P, 2, HEADS * C], F32)
    k.av = tmp("av", [C, HEADS * C], F32)
    k.avT = tmp("avT", [C, HEADS, 2, C], F32)
    k.ao = tmp("ao", [C, HEADS, C], F32)
    k.avo = tmp("avo", [P, HEADS * C], F32)
    k.amax = tmp("amax", [P, 3], F32)
    k.amaxr = tmp("amaxr", [P, 3], F32)
    k.ainv = tmp("ainv", [P, 3], F32)
    k.an = tmp("an", [P, 3, HEADS * C], F32)
    k.hld = tmp("hld", [D, NH, C + 1], F32)
    k.hln = tmp("hln", [C, C + 1], F32)
    k.fq = tmp("fq", [C, NH, D], F32)
    k.fk = tmp("fk", [C, D], F32)
    k.fv = tmp("fv", [C, D], F32)
    k.fqT = tmp("fqT", [D, NH, C], F32)
    k.fkT = tmp("fkT", [D, C], F32)
    k.fvT = tmp("fvT", [D, C], F32)
    k.fc = tmp("fc", [C, 2, C], F32)
    k.fgn = tmp("fgn", [NH, C], F32)

    loaded, cleared = k.sem("loaded"), k.sem("cleared")
    k.loaded = loaded
    loads = [
        (k.w[:], a["W"]), (k.wqn[:], a["Wq"]), (k.wkvn[:], a["Wkv"]), (k.wpn[:], a["Wproj"]),
        (k.tok_b[:], a["b"].partition_broadcast(P)), (k.tok_g[:], a["gamma"].partition_broadcast(P)),
        (k.tok_beta[:], a["beta"].partition_broadcast(P)), (k.bproj[:], a["bproj"].partition_broadcast(P)),
        (k.w1[:], a["W1"]), (k.b1[:], a["b1"].rearrange("(c p) -> p c", p=P)),
        (k.wg[:], a["Wg"].rearrange("(c p) e -> p c e", p=P)), (k.bg[:], a["bg"].partition_broadcast(P)),
        (k.wd[:, 0], a["Wd"][:, 0:P, :].rearrange("e p c -> p e c")),
        (k.wd[:, 1], a["Wd"][:, P:HID, :].rearrange("e p c -> p e c")),
        (k.bd1[:], a["bd"].rearrange("(o e) c -> o (e c)", o=1)),
        (k.aq[0:C, 0], a["WQ"]), (k.aq[C:P, 0], a["WQ"]), (k.aq[0:C, 1], a["WK"]), (k.aq[C:P, 1], a["WK"]),
        (k.av[:], a["WV"]), (k.ao[:], a["Wout"].rearrange("(h c) o -> c h o", h=HEADS)),
        (k.bout[:], a["bout"].partition_broadcast(P)),
        (k.hld[:, :, 0:C], a["hl_w"].rearrange("n d h -> d n h")),
        (k.hld[:, :, C], a["hl_b"].rearrange("n d -> d n")),
        (k.hln[:, 0:C], a["hl_w"].rearrange("n d h -> (n d) h")),
        (k.hln[:, C:C + 1], a["hl_b"].rearrange("n (d o) -> (n d) o", o=1)),
        (k.fq[:], a["wq"].rearrange("n e o d -> (e o) n d")),
        (k.fk[:], a["wk"].rearrange("n o d -> (n o) d")), (k.fv[:], a["wv"].rearrange("n o d -> (n o) d")),
        (k.gatew[:], a["gate_w"].partition_broadcast(P)), (k.gateb[:], a["gate_b"].partition_broadcast(P)),
        (k.lnp[:, 0], a["ln_g"].partition_broadcast(P)), (k.lnp[:, 1], a["ln_b"].partition_broadcast(P)),
        (k.lnp[:, 2], a["fnorm_g"].partition_broadcast(P)), (k.lnp[:, 3], a["fnorm_b"].partition_broadcast(P)),
        (k.fgn[:], a["fgate_w"]),
    ]
    diagonal = [
        (k.eblk[0:64, 0, 0:16], a["E_et"]), (k.eblk[64:128, 0, 16:32], a["E_fc"]),
        (k.eblk[:, 1, 32:48], a["E_sc"]), (k.eblk[:, 2, 48:64], a["E_of"]),
        (k.eblk[0:64, 3, 64:80], a["E_tt"]), (k.eblk[64:68, 3, 80:96], a["E_rc"]),
    ]
    for n in range(NH):
        at = slice(n * D, n * D + D)
        diagonal += [(k.fc[at, 0, at], a["fc1_w"]), (k.fc[at, 1, at], a["fc2_w"]),
                     (k.fcb[at, 0:1], a["fc1_b"].unsqueeze(1)), (k.fcb[at, 1:2], a["fc2_b"].unsqueeze(1))]
    k.n_loads = 16 * (len(loads) + len(diagonal))

    with nc.allow_non_contiguous_dma(reason="small weights, once"), nc.Block() as block:
        @block.sync
        def _(sp):
            for dst, src in loads[::2]:
                sp.dma_start(dst, src).then_inc(loaded, 16)
            sp.wait_ge(cleared, 2)
            for dst, src in diagonal:
                sp.dma_start(dst, src).then_inc(loaded, 16)
            sp.wait_ge(loaded, k.n_loads)

        @block.scalar
        def _(act):
            for dst, src in loads[1::2]:
                act.dma_start(dst, src).then_inc(loaded, 16)

        @block.vector
        def _(dve):
            dve.memset(k.eblk[:], 0.0).then_inc(cleared, 1)
            dve.memset(k.fc[:], 0.0).then_inc(cleared, 1)


def constants(k, nc):
    c = k.sem("const")
    with nc.Block() as block:
        @block.gpsimd
        def _(pool):
            n = 0

            def link(ins):
                nonlocal n
                n += 1
                ins.then_inc(c, 1)
                pool.wait_ge(c, n)

            def cut(t, x, v, size=1):
                link(pool.affine_select(out=t, in_=t, pattern=[[0, size]], compare_op=ALU.is_gt, fill=v,
                                        base=x, channel_multiplier=-1))

            link(pool.memset(k.ident[:], 0.0))
            link(pool.affine_select(out=k.ident[:], in_=k.ident[:], pattern=[[-1, P]], compare_op=ALU.not_equal,
                                    fill=1.0, base=0, channel_multiplier=1))
            link(pool.tensor_copy(k.identb[:], k.ident[:]))
            link(pool.tensor_copy(k.identh[:], k.ident[:]))
            link(pool.memset(k.ones[:], 1.0))
            link(pool.memset(k.onesb[:], 1.0))
            link(pool.memset(k.eps_ln[:], EPS_LN))
            link(pool.memset(k.eps_ffn[:], EPS_FFN))
            link(pool.memset(k.mask_q[:], 0.0))
            link(pool.affine_select(out=k.mask_q[:], in_=k.mask_q[:], pattern=[[-1, P]], compare_op=ALU.is_ge,
                                    fill=BIG, base=0, channel_multiplier=1))
            link(pool.memset(k.mask_k[:], 0.0))
            link(pool.affine_select(out=k.mask_k[:], in_=k.mask_k[:], pattern=[[1, P]], compare_op=ALU.is_ge,
                                    fill=BIG, base=0, channel_multiplier=-1))
            b8 = k.blk8[:].rearrange("p (h d) -> p h d", h=HEADS)
            link(pool.memset(k.blk8[:], 1.0))
            link(pool.affine_select(out=b8, in_=b8, pattern=[[-8, HEADS], [0, 8]], compare_op=ALU.is_ge,
                                    fill=0.0, base=0, channel_multiplier=1))
            link(pool.affine_select(out=b8, in_=b8, pattern=[[8, HEADS], [0, 8]], compare_op=ALU.is_ge,
                                    fill=0.0, base=7, channel_multiplier=-1))
            link(pool.memset(k.sel[:], 0.0))
            for view, pattern, base in (
                (k.sel[:, 0:2], [[-1, 2], [0, C]], 0),
                (k.sel[:, 2:6].rearrange("p (a b) c -> p a (b c)", a=2), [[-1, 2], [0, 2 * C]], -2),
                (k.sel[:, 6:8], [[-1, 2], [0, C]], -4),
            ):
                link(pool.affine_select(out=view, in_=view, pattern=pattern, compare_op=ALU.not_equal,
                                        fill=1.0, base=base, channel_multiplier=1))
            link(pool.iota(k.vint[:], pattern=[[0, 1]], base=0, channel_multiplier=1))
            for j in range(4):
                link(pool.tensor_copy(k.vcol[:, j:j + 1], k.vint[:]))
            for j in (0, 3):
                link(pool.tensor_scalar(k.vcol[64:128, j:j + 1], k.vcol[64:128, j:j + 1], -64.0, None, ALU.add))
            link(pool.iota(k.ranki[:], pattern=[[-1, EXPERTS]], base=EXPERTS, channel_multiplier=0))
            link(pool.tensor_copy(k.rank[:], k.ranki[:]))
            link(pool.memset(k.part[:], 0.0))
            link(pool.memset(k.part[64:128, 0:1], 1.0))
            link(pool.memset(k.part[96:128, 1:2], 1.0))
            for x, v in ((16, 1.0), (32, 0.0), (48, 1.0), (64, 0.0), (80, 1.0), (96, 0.0)):
                cut(k.part[:, 2:3], x, v)
            for x, v in ((48, 1.0), (64, 0.0)):
                cut(k.part[:, 3:4], x, v)
            link(pool.memset(k.gq[:], 0.0))
            link(pool.memset(k.gk[:], 0.0))


PREPARE = (
    ["abs_sum", "abs_all", "scale", "scale_eps", "inverse", "ratio", "above", "below", "sign", "ternary",
     "delta", "weff", "weff_turn", "weff_out"]
    + [f"{x}{j}" for j in range(4) for x in ("table_turn", "table_turned")]
    + [f"{x}{j}" for j in range(4) for x in ("table", "table_out")]
    + ["part1", "rest1", "part2", "rest2", "part3"]
    + [f"{w}_{x}" for w in ("wq", "wkv", "wp", "fk", "fv", "fc1", "fc2", "fg", "hl") for x in ("turn", "out")]
    + ["bd1", "bdr1", "bd2", "bdr2", "bd3", "bd_rows"]
    + [f"{x}{h}" for h in range(HEADS) for x in ("av_turn", "av_out")]
    + ["avo", "avo_out", "max_q", "max_k", "max_v", "max_all", "max_least", "max_inverse", "span",
       "escale", "escale2", "vscale", "norm_q", "norm_k", "norm_v", "hi_q", "hi_k", "hi_v", "lo_q", "lo_k", "lo_v"]
    + [f"{x}{n}" for n in range(NH) for x in ("fq_turn", "fq_out")]
    + [f"{x}{n}" for n in range(NH) for x in ("gq", "gq_a", "gq_b", "gq_c", "gk", "gk_a", "gk_b", "gk_c", "gk_one", "gv", "gv_out")]
)


def prepare(k, nc):
    step = k.sem("step")
    ps = k.bank

    def at(eng, name):
        i = PREPARE.index(name)
        if i:
            eng.wait_ge(step, i)

    with nc.Block() as block:
        @block.tensor
        def _(pe):
            def mm(name, out, lhsT, rhs):
                at(pe, name)
                pe.matmul(out, lhsT=lhsT, rhs=rhs, start=True, stop=True).then_inc(step, 1)

            def turn(name, out, in_):
                at(pe, name)
                n = in_.shape[0]
                pe.transpose(out, in_, k.ident[0:n, 0:n]).then_inc(step, 1)

            mm("abs_all", ps[0][0:C, 0:1], k.ones[0:C, 0:C], k.wcol[:, 0:1])
            turn("weff_turn", ps[0][0:VR, 0:C], k.wtmp[:, 3])
            for j in range(4):
                turn(f"table_turn{j}", ps[0][0:VR, 0:P], k.eblk[:, j])
            for j in range(4):
                mm(f"table{j}", ps[0][:, 0:C], k.eblkT[:, j], k.weffT[:])
            turn("wq_turn", ps[0][0:C, 0:C], k.wqn[:])
            turn("wkv_turn", ps[0][0:C, 0:2 * C], k.wkvn[:])
            turn("wp_turn", ps[0][0:C, 0:C], k.wpn[:])
            turn("fk_turn", ps[0][0:D, 0:C], k.fk[:])
            turn("fv_turn", ps[0][0:D, 0:C], k.fv[:])
            turn("fc1_turn", ps[0][0:C, 0:C], k.fc[:, 0])
            turn("fc2_turn", ps[0][0:C, 0:C], k.fc[:, 1])
            turn("fg_turn", ps[0][0:C, 0:NH], k.fgn[:])
            turn("hl_turn", ps[0][0:C + 1, 0:C], k.hln[:])
            for h in range(HEADS):
                turn(f"av_turn{h}", ps[0][0:C, 0:C], k.av[:, h * C:(h + 1) * C])
            at(pe, "avo")
            for h in range(HEADS):
                mm_ = pe.matmul(ps[0][:, h * C:(h + 1) * C], lhsT=k.avT[:, h].rearrange("c a i -> c (a i)"),
                                rhs=k.ao[:, h], start=True, stop=True)
            mm_.then_inc(step, 1)
            for n in range(NH):
                turn(f"fq_turn{n}", ps[0][0:D, 0:C], k.fq[:, n])
            for n in range(NH):
                mm(f"gq{n}", ps[0][0:C + 1, 0:C], k.hld[:, n], k.fqT[:, n])
                mm(f"gk{n}", ps[0][0:C + 1, 0:D], k.hld[:, n], k.fkT[:, n * D:(n + 1) * D])
                mm(f"gv{n}", ps[0][0:C + 1, 0:D], k.hld[:, n], k.fvT[:, n * D:(n + 1) * D])

        @block.gpsimd
        def _(pool):
            at(pool, "max_all")
            pool.partition_all_reduce(k.amaxr[:], k.amax[:], P, bass.bass_isa.ReduceOp.max).then_inc(step, 1)

        @block.sync
        def _(sp):
            at(sp, "bd_rows")
            sp.dma_start(k.bd3[:], k.bds[0:1]).then_inc(k.loaded, 16)
            sp.wait_ge(k.loaded, k.n_loads + 16)
            sp.sem_inc(step, 1)

        @block.vector
        def _(dve):
            def ts(name, out, in0, s1, s2, op0, op1=ALU.bypass):
                at(dve, name)
                dve.tensor_scalar(out, in0, s1, s2, op0, op1).then_inc(step, 1)

            def tt(name, out, in0, in1, op):
                at(dve, name)
                dve.tensor_tensor(out, in0, in1, op).then_inc(step, 1)

            def copy(name, out, in_):
                at(dve, name)
                dve.tensor_copy(out, in_).then_inc(step, 1)

            def biggest(name, out, in_):
                at(dve, name)
                dve.tensor_reduce(out, in_, X, ALU.max, apply_absolute_value=True).then_inc(step, 1)

            w, t, col = k.w[:], k.wtmp, k.wcol
            at(dve, "abs_sum")
            dve.tensor_reduce(col[:, 0:1], w, X, ALU.add, apply_absolute_value=True).then_inc(step, 1)
            ts("scale", col[:, 1:2], ps[0][0:C, 0:1], 1.0 / (C * VR), None, ALU.mult)
            ts("scale_eps", col[:, 2:3], col[:, 1:2], EPS_W, None, ALU.add)
            at(dve, "inverse")
            dve.reciprocal(col[:, 3:4], col[:, 2:3]).then_inc(step, 1)
            ts("ratio", t[:, 0], w, col[:, 3:4], None, ALU.mult)
            ts("above", t[:, 1], t[:, 0], 0.5, None, ALU.is_gt)
            ts("below", t[:, 2], t[:, 0], -0.5, None, ALU.is_lt)
            tt("sign", t[:, 1], t[:, 1], t[:, 2], ALU.subtract)
            ts("ternary", t[:, 1], t[:, 1], col[:, 1:2], None, ALU.mult)
            tt("delta", t[:, 2], t[:, 1], w, ALU.subtract)
            tt("weff", t[:, 3], w, t[:, 2], ALU.add)
            copy("weff_out", k.weffT[:], ps[0][0:VR, 0:C])
            for j in range(4):
                copy(f"table_turned{j}", k.eblkT[:, j], ps[0][0:VR, 0:P])
            for j in range(4):
                copy(f"table_out{j}", k.tab[:, j], ps[0][:, 0:C])
            copy("part1", k.tab3[:, :, 0], k.tab[:])
            tt("rest1", k.tabr[:], k.tab[:], k.tab3[:, :, 0], ALU.subtract)
            copy("part2", k.tab3[:, :, 1], k.tabr[:])
            tt("rest2", k.tab[:], k.tabr[:], k.tab3[:, :, 1], ALU.subtract)
            copy("part3", k.tab3[:, :, 2], k.tab[:])
            copy("wq_out", k.wqT[:], ps[0][0:C, 0:C])
            copy("wkv_out", k.wkvT[:], ps[0][0:C, 0:2 * C])
            copy("wp_out", k.wpT[:], ps[0][0:C, 0:C])
            copy("fk_out", k.fkT[:], ps[0][0:D, 0:C])
            copy("fv_out", k.fvT[:], ps[0][0:D, 0:C])
            copy("fc1_out", k.fcT[:, 0], ps[0][0:C, 0:C])
            copy("fc2_out", k.fcT[:, 1], ps[0][0:C, 0:C])
            copy("fg_out", k.fgT[:], ps[0][0:C, 0:NH])
            copy("hl_out", k.gsv[:, 0:C], ps[0][0:C + 1, 0:C])
            copy("bd1", k.bds[:, 0], k.bd1[:])
            tt("bdr1", k.bdr[:], k.bd1[:], k.bds[:, 0], ALU.subtract)
            copy("bd2", k.bds[:, 1], k.bdr[:])
            tt("bdr2", k.bd1[:], k.bdr[:], k.bds[:, 1], ALU.subtract)
            copy("bd3", k.bds[:, 2], k.bd1[:])
            for h in range(HEADS):
                copy(f"av_out{h}", k.avT[:, h], ps[0][0:C, 0:C].unsqueeze(1).to_broadcast([C, 2, C]))
            copy("avo_out", k.avo[:], ps[0][:, :])
            biggest("max_q", k.amax[:, 0:1], k.aq[:, 0])
            biggest("max_k", k.amax[:, 1:2], k.aq[:, 1])
            biggest("max_v", k.amax[:, 2:3], k.avo[:])
            ts("max_least", k.amax[:], k.amaxr[:], 1e-30, None, ALU.max)
            at(dve, "max_inverse")
            dve.reciprocal(k.ainv[:], k.amax[:]).then_inc(step, 1)
            ts("span", k.ainv[:], k.ainv[:], WSPAN, None, ALU.mult)
            ts("escale", k.escale[:], k.amax[:, 0:1], 1.0 / (WSPAN * WSPAN * float(np.sqrt(C / HEADS))), None, ALU.mult)
            tt("escale2", k.escale[:], k.escale[:], k.amax[:, 1:2], ALU.mult)
            ts("vscale", k.vscale[:], k.amax[:, 2:3], 1.0 / WSPAN, None, ALU.mult)
            ts("norm_q", k.an[:, 0], k.aq[:, 0], k.ainv[:, 0:1], None, ALU.mult)
            ts("norm_k", k.an[:, 1], k.aq[:, 1], k.ainv[:, 1:2], None, ALU.mult)
            ts("norm_v", k.an[:, 2], k.avo[:], k.ainv[:, 2:3], None, ALU.mult)
            twice = [k.an[:, j].rearrange("p (h c) -> p h c", h=HEADS).unsqueeze(2).to_broadcast([P, HEADS, 2, C])
                     for j in range(2)]
            copy("hi_q", k.wqk_hi[:, 0], twice[0])
            copy("hi_k", k.wqk_hi[:, 1], twice[1])
            copy("hi_v", k.wvo_hi[:], k.an[:, 2])
            tt("lo_q", k.wqk_lo[:, 0], twice[0], k.wqk_hi[:, 0], ALU.subtract)
            tt("lo_k", k.wqk_lo[:, 1], twice[1], k.wqk_hi[:, 1], ALU.subtract)
            tt("lo_v", k.wvo_lo[:], k.an[:, 2], k.wvo_hi[:], ALU.subtract)
            for n in range(NH):
                copy(f"fq_out{n}", k.fqT[:, n], ps[0][0:D, 0:C])
            for n in range(NH):
                q = ps[0][0:C + 1, 0:C].rearrange("p (e o) -> p e o", e=NE)
                for x, s0, s1 in (("a", 0, 2), ("b", 3, 6), ("c", 7, 8)):
                    copy(f"gq_{x}{n}", k.gq[:, n, :, s0:s1], q.unsqueeze(2).to_broadcast([C + 1, NE, s1 - s0, D]))
                kk = ps[0][0:C + 1, 0:D]
                for x, s0, s1 in (("a", 0, 2), ("b", 3, 6), ("c", 7, 8)):
                    copy(f"gk_{x}{n}", k.gk[:, n, s0:s1], kk.unsqueeze(1).to_broadcast([C + 1, s1 - s0, D]))
                at(dve, f"gk_one{n}")
                dve.memset(k.gk[C:C + 1, n, 2, 0:2], 1.0).then_inc(step, 1)
                copy(f"gv_out{n}", k.gsv[:, C + n * D:C + (n + 1) * D], kk)


class Chain:

    def __init__(self, eng, sem, turn, steps):
        self.eng, self.sem, self.base, self.steps, self.n = eng, sem, turn * steps, steps, 0

    def __call__(self, ins):
        self.n += 1
        ins.then_inc(self.sem, 1)
        self.eng.wait_ge(self.sem, self.base + self.n)

    def fill(self, eng):
        if self.n < self.steps:
            eng.sem_inc(self.sem, self.steps - self.n)

    def end(self):
        assert self.n == self.steps, (self.n, self.steps)


def passed(eng, seen, sem, value):
    eng.wait_ge(sem, value)
    eng.sem_inc(seen, 1)


def wide(ap, n):
    return ap.unsqueeze(2).to_broadcast([ap.shape[0], ap.shape[1], n])


def rows(ap, n):
    return ap.unsqueeze(1).to_broadcast([ap.shape[0], n, ap.shape[1]])


def normalize(dve, link, x, out, xc, sq, st, size, var_ready, std_ready, turn):
    link(dve.tensor_reduce(st[:, 0], x, X, ALU.add))
    link(dve.tensor_scalar(st[:, 0], st[:, 0], 1.0 / size, None, ALU.mult))
    link(dve.tensor_tensor(xc, x, wide(st[:, 0], size), ALU.subtract))
    link(dve.tensor_tensor(sq, xc, xc, ALU.mult))
    dve.tensor_reduce(st[:, 1], sq, X, ALU.add).then_inc(var_ready, 1)
    dve.wait_ge(std_ready, turn + 1)
    link(dve.reciprocal(st[:, 3], st[:, 2]))
    link(dve.tensor_tensor(out, xc, wide(st[:, 3], size), ALU.mult))


def root(act, st, eps, size, var_ready, std_ready, turn):
    act.wait_ge(var_ready, turn + 1)
    act.activation(st[:, 2], st[:, 1], ACT.Sqrt, bias=eps, scale=1.0 / size).then_inc(std_ready, 1)


def layer0(k, nc, a):
    NB = k.NB
    ps = k.bank
    with ExitStack() as ctx:
        def sb(name, shape, dt):
            return ctx.enter_context(nc.sbuf_tensor(name, shape, dt))

        ids = sb("ids", [6, S], I32)
        idsb = sb("idsb", [6, S], BF16)
        onehot = sb("onehot", [P, 4, S], BF16)
        x = sb("l0_x", [P, T, C], F32)
        xc = sb("l0_xc", [P, T, C], F32)
        sq = sb("l0_sq", [P, T, C], F32)
        xn = sb("l0_xn", [P, T, 2, C], F32)
        st = sb("l0_st", [P, 4, T], F32)
        xT = sb("l0_xT", [C, S], F32)
        qT = sb("l0_qT", [C, S], F32)
        low = sb("l0_low", [P, S], F32)
        kf = sb("l0_kf", [P, T, C], F32)
        vx = sb("l0_vx", [P, T, C + 1], F32)
        cx = sb("l0_cx", [C, 2, C], F32)
        inv = sb("l0_inv", [C, S], F32)
        aT = sb("l0_aT", [C, S], F32)
        hT = sb("l0_hT", [P, 2, S], F32)
        lg = sb("l0_lg", [P, T, EXPERTS], F32)
        eg = sb("l0_eg", [P, T, EXPERTS], F32)
        g1 = sb("l0_g1", [P, 4, T], F32)
        wsel = sb("l0_wsel", [P, T, EXPERTS], F32)
        yw = sb("l0_yw", [P, 2, EXPERTS, C], F32)

        s = Parts()
        s.done = k.sem("l0_done")
        s.ids_in = k.sem("l0_ids_in")
        s.ids_cast = k.sem("l0_ids_cast")
        s.idx_ready = k.sem("l0_idx_ready")
        s.onehot_ready = k.sem("l0_onehot_ready")
        s.z_ready = k.sem("l0_z_ready")
        s.d = k.sem("l0_d")
        s.p = k.sem("l0_p")
        s.h_ready = k.sem("l0_h_ready")
        s.turn_a = k.sem("l0_turn_a")
        s.xT_ready = k.sem("l0_xT_ready")
        s.q_ready = k.sem("l0_q_ready")
        s.kv_ready = k.sem("l0_kv_ready")
        s.qlow = k.sem("l0_qlow")
        s.qexp = k.sem("l0_qexp")
        s.klow = k.sem("l0_klow")
        s.kexp = k.sem("l0_kexp")
        s.q_done = k.sem("l0_q_done")
        s.kv_done = k.sem("l0_kv_done")
        s.ctx_ready = k.sem("l0_ctx_ready")
        s.ctx_done = k.sem("l0_ctx_done")
        s.num_ready = k.sem("l0_num_ready")
        s.den_ready = k.sem("l0_den_ready")
        s.aT_done = k.sem("l0_aT_done")
        s.proj_ready = k.sem("l0_proj_ready")
        s.turn_f = k.sem("l0_turn_f")
        s.xT_f = k.sem("l0_xT_f")
        s.hid_ready = k.sem("l0_hid_ready")
        s.gelu_done = k.sem("l0_gelu_done")
        s.gate_ready = k.sem("l0_gate_ready")
        s.lg_ready = k.sem("l0_lg_ready")
        s.eg_ready = k.sem("l0_eg_ready")
        s.y_ready = k.sem("l0_y_ready")
        s.y_taken = k.sem("l0_y_taken")
        s.turn_p = k.sem("l0_turn_p")
        s.hi_done = k.sem("l0_hi_done")
        s.out = k.sem("l0_out")
        var = [k.sem(f"l0_var{j}") for j in range(4)]
        std = [k.sem(f"l0_std{j}") for j in range(4)]
        DVE_STEPS = 65

        with nc.Block() as block:
            @block.sync
            def _(sp):
                with sp.Fori(0, NB) as b:
                    sp.wait_ge(s.done, b + 1)
                    for j, name in enumerate(k.id_names):
                        sp.dma_start(ids[j:j + 1, :], k.ids[name][ds(b, 1), :]).then_inc(s.ids_in, 16)

            @block.gpsimd
            def _(pool):
                pool.memset(vx[:, :, C:C + 1], 1.0).then_inc(s.p, 1)
                with pool.Fori(0, NB) as b:
                    passed(pool, k.seen, s.ids_in, b * 96 + 96)
                    pool.tensor_copy(idsb[:], ids[:]).then_inc(s.ids_cast, 1)

            @block.scalar
            def _(act):
                with act.Fori(0, NB) as b:
                    root(act, st, k.eps_ln[:], C, var[0], std[0], b)
                    root(act, st, k.eps_ln[:], C, var[1], std[1], b)
                    act.wait_ge(s.turn_a, b + 1)
                    for j in range(2):
                        act.activation(xT[:, j * HALF:(j + 1) * HALF], ps[j][0:C, :], ACT.Copy).then_inc(s.xT_ready, 1)
                    act.wait_ge(s.qlow, b + 1)
                    act.activation(low[0:C, :], low[0:C, :], ACT.Exp).then_inc(s.qexp, 1)
                    act.wait_ge(s.klow, b + 1)
                    act.activation(low[:, 0:HALF], low[:, 0:HALF], ACT.Exp).then_inc(s.kexp, 1)
                    root(act, st, k.eps_ln[:], C, var[2], std[2], b)
                    act.wait_ge(s.turn_f, b + 1)
                    for j in range(2):
                        act.activation(xT[:, j * HALF:(j + 1) * HALF], ps[j][0:C, :], ACT.Copy).then_inc(s.xT_f, 1)
                    for c in range(2):
                        for j in range(2):
                            act.wait_ge(s.hid_ready, b * 4 + 2 * c + j + 1)
                            act.activation(hT[:, c, j * HALF:(j + 1) * HALF], ps[2 + 2 * c + j][:], ACT.Gelu,
                                           bias=k.b1[:, c:c + 1]).then_inc(s.gelu_done, 1)
                    act.wait_ge(s.lg_ready, b + 1)
                    act.activation(eg[:], lg[:], ACT.Exp).then_inc(s.eg_ready, 1)
                    root(act, st, k.eps_ln[:], C, var[3], std[3], b)
                    act.wait_ge(s.turn_p, b + 1)
                    for j in range(2):
                        act.activation(k.xa[:, ds(b * S + j * HALF, HALF)], ps[j][:], ACT.Copy).then_inc(s.hi_done, 1)

            @block.tensor
            def _(pe):
                def turn_tokens(m, done):
                    for t in range(T):
                        src = xn[:, t, 0] if m == C else xn[:, t].rearrange("p a c -> p (a c)")
                        last = pe.transpose(ps[t // 4][0:m, (t % 4) * P:(t % 4 + 1) * P], src, k.ident[:])
                    last.then_inc(done, 1)

                with pe.Fori(0, NB) as b:
                    pe.wait_ge(s.ids_cast, b + 1)
                    for j in range(2):
                        for c in range(4):
                            pe.matmul(ps[4 * j + c][:], lhsT=k.sel[:, 2 * c:2 * c + 2].rearrange("t a p -> t (a p)"),
                                      rhs=idsb[:, j * HALF:(j + 1) * HALF], start=True, stop=True).then_inc(s.idx_ready, 1)
                    for j in range(2):
                        pe.wait_ge(s.onehot_ready, b * 8 + 4 * j + 4)
                        for t in range(4):
                            for c in range(4):
                                for r in range(3):
                                    last = pe.matmul(ps[4 * j][:, t * C:(t + 1) * C],
                                                     lhsT=onehot[:, c, (4 * j + t) * P:(4 * j + t + 1) * P],
                                                     rhs=k.tab3[:, c, r], start=(t == 0 and c == 0 and r == 0),
                                                     stop=(c == 3 and r == 2), skip_group_check=True)
                        last.then_inc(s.z_ready, 1)
                    passed(pe, k.seen, s.h_ready, b * 3 + 1)
                    turn_tokens(C, s.turn_a)
                    passed(pe, k.seen, s.xT_ready, b * 2 + 2)
                    for j in range(2):
                        last = pe.matmul(ps[2 + j][0:C, :], lhsT=k.wqT[:], rhs=xT[:, j * HALF:(j + 1) * HALF],
                                         start=True, stop=True)
                    last.then_inc(s.q_ready, 1)
                    for t in range(T):
                        last = pe.matmul(ps[4 + t // 4][:, (t % 4) * P:(t % 4 + 1) * P], lhsT=xT[:, t * P:(t + 1) * P],
                                         rhs=k.wkvT[:], start=True, stop=True)
                    last.then_inc(s.kv_ready, 1)
                    pe.wait_ge(s.kv_done, b + 1)
                    pe.wait_ge(s.p, 1)
                    for t in range(T):
                        last = pe.matmul(ps[6][0:C, 0:C + 1], lhsT=kf[:, t], rhs=vx[:, t], start=(t == 0), stop=(t == T - 1))
                    last.then_inc(s.ctx_ready, 1)
                    pe.wait_ge(s.ctx_done, b + 1)
                    passed(pe, k.seen, s.q_done, b + 1)
                    for which, sig in ((1, s.den_ready), (0, s.num_ready)):
                        for j in range(2):
                            last = pe.matmul(ps[4 * which + j][0:C, :], lhsT=cx[:, which],
                                             rhs=qT[:, j * HALF:(j + 1) * HALF], start=True, stop=True)
                        last.then_inc(sig, 1)
                    pe.wait_ge(s.aT_done, b + 1)
                    for t in range(T):
                        last = pe.matmul(ps[2][:, t * C:(t + 1) * C], lhsT=aT[:, t * P:(t + 1) * P], rhs=k.wpT[:],
                                         start=True, stop=True)
                    last.then_inc(s.proj_ready, 1)
                    passed(pe, k.seen, s.h_ready, b * 3 + 2)
                    turn_tokens(C, s.turn_f)
                    pe.wait_ge(s.xT_f, b * 2 + 2)
                    for c in range(2):
                        for j in range(2):
                            pe.matmul(ps[2 + 2 * c + j][:], lhsT=k.w1[:, c * P:(c + 1) * P],
                                      rhs=xT[:, j * HALF:(j + 1) * HALF], start=True, stop=True).then_inc(s.hid_ready, 1)
                    pe.wait_ge(s.gelu_done, b * 4 + 4)
                    for t in range(T):
                        for c in range(2):
                            last = pe.matmul(ps[0][:, t * EXPERTS:(t + 1) * EXPERTS], lhsT=hT[:, c, t * P:(t + 1) * P],
                                             rhs=k.wg[:, c], start=(c == 0 and t == 0), stop=(c == 1), skip_group_check=True)
                    last.then_inc(s.gate_ready, 1)
                    for t in range(T):
                        bank = ps[1 + t % 2]
                        if t >= 2:
                            pe.wait_ge(s.y_taken, b * T + t - 1)
                        for c in range(2):
                            pe.matmul(bank[:], lhsT=hT[:, c, t * P:(t + 1) * P],
                                      rhs=k.wd[:, c].rearrange("p e c -> p (e c)"), start=(c == 0), stop=False)
                        pe.matmul(bank[:], lhsT=k.onesb[0:3, :], rhs=k.bd3[:], start=False, stop=True).then_inc(s.y_ready, 1)
                    pe.wait_ge(s.h_ready, b * 3 + 3)
                    turn_tokens(P, s.turn_p)

            @block.vector
            def _(dve):
                dve.sem_inc(s.done, 1)
                with dve.Fori(0, NB) as b:
                    link = Chain(dve, s.d, b, DVE_STEPS)
                    hb = k.h[:, ds(b * T, T), :]
                    for j in range(2):
                        for c in range(4):
                            dve.wait_ge(s.idx_ready, b * 8 + 4 * j + c + 1)
                            dve.tensor_scalar(onehot[:, c, j * HALF:(j + 1) * HALF], ps[4 * j + c][:],
                                              k.vcol[:, c:c + 1], None, ALU.is_equal).then_inc(s.onehot_ready, 1)
                    for j in range(2):
                        dve.wait_ge(s.z_ready, b * 2 + j + 1)
                        link(dve.tensor_tensor(x[:, 4 * j:4 * j + 4], ps[4 * j][:, 0:4 * C].rearrange("p (t c) -> p t c", t=4),
                                               rows(k.tok_b[:], 4), ALU.add))
                    normalize(dve, link, x[:], x[:], xc[:], sq[:], st, C, var[0], std[0], b)
                    link(dve.tensor_tensor(x[:], x[:], rows(k.tok_g[:], T), ALU.mult))
                    link(dve.tensor_tensor(x[:], x[:], rows(k.tok_beta[:], T), ALU.add))
                    normalize(dve, link, x[:], xn[:, :, 0], xc[:], sq[:], st, C, var[1], std[1], b)
                    dve.sem_inc(s.h_ready, 1)
                    dve.wait_ge(s.q_ready, b + 1)
                    link(dve.tensor_scalar(low[0:C, 0:HALF], ps[2][0:C, :], 0.0, None, ALU.min))
                    dve.tensor_scalar(low[0:C, HALF:S], ps[3][0:C, :], 0.0, None, ALU.min).then_inc(s.qlow, 1)
                    dve.wait_ge(s.qexp, b + 1)
                    link(dve.scalar_tensor_tensor(qT[:, 0:HALF], ps[2][0:C, :], 0.0, low[0:C, 0:HALF], ALU.max, ALU.add))
                    dve.scalar_tensor_tensor(qT[:, HALF:S], ps[3][0:C, :], 0.0, low[0:C, HALF:S], ALU.max, ALU.add)\
                       .then_inc(s.q_done, 1)
                    dve.wait_ge(s.q_done, b + 1)
                    dve.wait_ge(s.kv_ready, b + 1)
                    kv = [ps[4 + j][:].rearrange("p (t x) -> p t x", t=4) for j in range(2)]
                    low_k = low[:, 0:HALF].rearrange("p (t c) -> p t c", t=T)
                    link(dve.tensor_scalar(low_k[:, 0:4], kv[0][:, :, 0:C], 0.0, None, ALU.min))
                    dve.tensor_scalar(low_k[:, 4:8], kv[1][:, :, 0:C], 0.0, None, ALU.min).then_inc(s.klow, 1)
                    link(dve.tensor_copy(vx[:, 0:4, 0:C], kv[0][:, :, C:2 * C]))
                    link(dve.tensor_copy(vx[:, 4:8, 0:C], kv[1][:, :, C:2 * C]))
                    dve.wait_ge(s.kexp, b + 1)
                    link(dve.scalar_tensor_tensor(kf[:, 0:4], kv[0][:, :, 0:C], 0.0, low_k[:, 0:4], ALU.max, ALU.add))
                    dve.scalar_tensor_tensor(kf[:, 4:8], kv[1][:, :, 0:C], 0.0, low_k[:, 4:8], ALU.max, ALU.add)\
                       .then_inc(s.kv_done, 1)
                    dve.wait_ge(s.ctx_ready, b + 1)
                    link(dve.tensor_tensor(cx[:, 0], ps[6][0:C, 0:C], k.blk8[:], ALU.mult))
                    dve.tensor_scalar(cx[:, 1], k.blk8[:], ps[6][0:C, C:C + 1], None, ALU.mult).then_inc(s.ctx_done, 1)
                    dve.wait_ge(s.den_ready, b + 1)
                    for j in range(2):
                        link(dve.tensor_scalar(inv[:, j * HALF:(j + 1) * HALF], ps[4 + j][0:C, :], 1e-6, None, ALU.max))
                    link(dve.reciprocal(inv[:], inv[:]))
                    dve.wait_ge(s.num_ready, b + 1)
                    for j in range(2):
                        link(dve.tensor_tensor(aT[:, j * HALF:(j + 1) * HALF], ps[j][0:C, :],
                                               inv[:, j * HALF:(j + 1) * HALF], ALU.mult))
                    dve.sem_inc(s.aT_done, 1)
                    dve.wait_ge(s.proj_ready, b + 1)
                    link(dve.tensor_tensor(x[:], x[:], rows(k.bproj[:], T), ALU.add))
                    link(dve.tensor_tensor(x[:], x[:], ps[2][:].rearrange("p (t c) -> p t c", t=T), ALU.add))
                    normalize(dve, link, x[:], xn[:, :, 0], xc[:], sq[:], st, C, var[2], std[2], b)
                    dve.sem_inc(s.h_ready, 1)
                    dve.wait_ge(s.gate_ready, b + 1)
                    link(dve.tensor_tensor(lg[:], ps[0][:, 0:T * EXPERTS].rearrange("p (t e) -> p t e", t=T),
                                           rows(k.bg[:], T), ALU.add))
                    link(dve.tensor_reduce(g1[:, 0], lg[:], X, ALU.max))
                    link(dve.tensor_tensor(wsel[:], lg[:], wide(g1[:, 0], EXPERTS), ALU.is_equal))
                    dve.tensor_tensor(lg[:], lg[:], wide(g1[:, 0], EXPERTS), ALU.subtract).then_inc(s.lg_ready, 1)
                    link(dve.tensor_tensor(wsel[:], wsel[:], rows(k.rank[:], T), ALU.mult))
                    link(dve.tensor_reduce(g1[:, 1], wsel[:], X, ALU.max))
                    link(dve.tensor_tensor(wsel[:], wsel[:], wide(g1[:, 1], EXPERTS), ALU.is_equal))
                    dve.wait_ge(s.eg_ready, b + 1)
                    link(dve.tensor_reduce(g1[:, 2], eg[:], X, ALU.add))
                    link(dve.reciprocal(g1[:, 3], g1[:, 2]))
                    link(dve.tensor_tensor(eg[:], eg[:], wide(g1[:, 3], EXPERTS), ALU.mult))
                    link(dve.tensor_tensor(wsel[:], wsel[:], eg[:], ALU.mult))
                    for t in range(T):
                        dve.wait_ge(s.y_ready, b * T + t + 1)
                        dve.tensor_tensor(yw[:, t % 2], ps[1 + t % 2][:].rearrange("p (e c) -> p e c", e=EXPERTS),
                                          wide(wsel[:, t], C), ALU.mult).then_inc(s.y_taken, 1)
                        dve.wait_ge(s.y_taken, b * T + t + 1)
                        link(dve.tensor_reduce(sq[:, t], yw[:, t % 2].rearrange("p e c -> p c e"), X, ALU.add))
                    link(dve.tensor_tensor(x[:], x[:], sq[:], ALU.add))
                    normalize(dve, link, x[:], xn[:, :, 0], xc[:], sq[:], st, C, var[3], std[3], b)
                    link(dve.tensor_copy(xn[:, :, 1], xn[:, :, 0]))
                    dve.sem_inc(s.h_ready, 1)
                    link(dve.tensor_tensor(hb, x[:], rows(k.bout[:], T), ALU.add))
                    dve.wait_ge(s.hi_done, b * 2 + 2)
                    for j in range(2):
                        low_half = k.xa[C:P, ds(b * S + j * HALF, HALF)]
                        link(dve.tensor_tensor(low_half, ps[j][C:P, :], low_half, ALU.subtract))
                    dve.sem_inc(s.done, 1)
                    link.end()


A_TASKS = (
    (("q", 0), ("q", 1)),
    (("k", 0), ("k", 1), ("v", 0)),
    (("den", 0),) + tuple(("max", u) for u in range(4)),
    tuple(("max", u) for u in range(4, 8)),
    tuple(("max", u) for u in range(8, 12)) + (("out", 0),),
    tuple(("max", u) for u in range(12, 16)),
    (),
    (("row", 0),),
)
A_LIST = [t for slot in A_TASKS for t in slot]
A_N = len(A_LIST)
A_BANKS = (4, 5, 7)
NEXT = ("q", "k", "v", "max", "row")
NPB = 4


def attention1(k, nc):
    heads = k.NB * HEADS
    ps = k.bank
    assert A_N % len(A_BANKS) == 0
    with ExitStack() as ctx:
        def sb(name, shape, dt):
            return ctx.enter_context(nc.sbuf_tensor(name, shape, dt))

        qa = sb("a1_qa", [P, 2, S], FP16)
        qb = sb("a1_qb", [C + 2, 2, S], FP16)
        ka = sb("a1_ka", [P, 2, S], FP16)
        kb = sb("a1_kb", [C + 2, 2, S], FP16)
        v = sb("a1_v", [P, 2, T, C], F32)
        prob = sb("a1_prob", [P, NPB, S], F32)
        total = sb("a1_total", [P, 2, S], F32)
        un = sb("a1_un", [P, 2, HALF], F32)
        inv = sb("a1_inv", [P, HALF], F32)
        u = sb("a1_u", [P, HALF], F32)
        mp = sb("a1_mp", [P, T, 2], F32)
        mx = sb("a1_mx", [P, 2, T], F32)
        mm = sb("a1_mm", [P, T, 2], FP16)

        s = Parts()
        s.scores = k.sem("a1_scores")
        s.exp = k.sem("a1_exp")
        s.pv = k.sem("a1_pv")
        s.added = k.sem("a1_added")
        s.task = k.sem("a1_task")
        s.taken = k.sem("a1_taken")
        s.split = k.sem("a1_split")
        s.copied = k.sem("a1_copied")
        s.maxima = k.sem("a1_maxima")
        s.divided = k.sem("a1_divided")
        s.d = k.sem("a1_d")
        s.start = k.sem("a1_start")
        D_STEPS = 7
        TAKEN = {t: j for j, t in enumerate(A_LIST)}

        def listed(slot):
            j = sum(len(x) for x in A_TASKS[:slot])
            return [(j + i, *t) for i, t in enumerate(A_TASKS[slot])]

        def wanted(kind, g, first, last):
            return not last if kind in NEXT else not first

        def pairs(eng, head, prologue):
            prologue()
            head(0, 0, True, False)
            head(1, 1, False, False)
            with eng.Fori(1, heads // 2 - 1) as i:
                head(0, i * 2, False, False)
                head(1, i * 2 + 1, False, False)
            head(0, heads - 2, False, False)
            head(1, heads - 1, False, True)

        with nc.Block() as block:
            @block.gpsimd
            def _(pool):
                def head(par, g, first, last):
                    pool.wait_ge(s.task, A_N * g + TAKEN["den", 0] + 1)
                    for kt in range(1, T):
                        pool.wait_ge(s.exp, T * g + kt + 1)
                        if kt >= 2:
                            pool.wait_ge(s.added, (T - 1) * g + kt - 1)
                        one = prob[:, 0] if kt == 1 else total[:, par]
                        pool.tensor_tensor(total[:, par], one, prob[:, kt % NPB], ALU.add).then_inc(s.added, 1)

                pairs(pool, head, lambda: None)

            @block.scalar
            def _(act):
                def split_q(par, n, j, c):
                    act.wait_ge(s.task, A_N * n + j + 1)
                    cols = slice(c * HALF, (c + 1) * HALF)
                    act.activation(qa[:, par, cols], ps[A_BANKS[j % 3]], ACT.Copy).then_inc(s.split, 1)
                    act.activation(qb[0:C, par, cols], ps[A_BANKS[j % 3]][0:C], ACT.Copy).then_inc(s.split, 1)

                def split_k(par, n, j, c):
                    act.wait_ge(s.task, A_N * n + j + 1)
                    act.activation(ka[:, par, c * HALF:(c + 1) * HALF], ps[A_BANKS[j % 3]], ACT.Copy)\
                       .then_inc(s.split, 1)

                def prologue():
                    for j, kind, c in listed(0) + listed(1):
                        if kind == "q":
                            split_q(0, 0, j, c)
                        if kind == "k":
                            split_k(0, 0, j, c)

                def head(par, g, first, last):
                    for kt in range(T):
                        act.wait_ge(s.scores, T * g + kt + 1)
                        if kt >= NPB:
                            act.wait_ge(s.pv, T * g + kt - NPB + 1)
                            act.wait_ge(s.added, (T - 1) * g + max(1, kt - NPB))
                        elif not first:
                            act.wait_ge(s.pv, T * g + kt - NPB + 1)
                            act.wait_ge(s.added, (T - 1) * (g - 1) + kt + T - NPB)
                        act.activation(prob[:, kt % NPB], k.psum[:, 2 * (kt % 2):2 * (kt % 2) + 2].rearrange("p b n -> p (b n)"),
                                       ACT.Exp, scale=k.escale[:]).then_inc(s.exp, 1)
                        if kt in (0, 1) and not last:
                            for j, kind, c in listed(kt):
                                if kind == "q":
                                    split_q(1 - par, g + 1, j, c)
                                if kind == "k":
                                    split_k(1 - par, g + 1, j, c)
                        if kt == 0 and not first:
                            copy_out(1 - par, g - 1)

                def copy_out(par, g):
                    act.wait_ge(s.pv, T * (g + 1))
                    act.activation(un[:, par], ps[6], ACT.Copy).then_inc(s.copied, 1)

                pairs(act, head, prologue)
                copy_out(1, heads - 1)

            @block.tensor
            def _(pe):
                def task(par, n, j, kind, c, skip=False):
                    bank = ps[A_BANKS[j % 3]]
                    if skip:
                        if not (isinstance(n, int) and A_N * n + j == 0):
                            pe.wait_ge(s.task, A_N * n + j)
                        pe.sem_inc(s.task, 1)
                        return
                    if not (isinstance(n, int) and n == 0 and j < 3):
                        pe.wait_ge(s.taken, A_N * n + j - 2)
                    if kind in ("q", "k"):
                        h, b = n % HEADS, n // HEADS
                        which = 0 if kind == "q" else 1
                        rhs = k.xa[:, ds(b * S + c * HALF, HALF)]
                        for w, start in ((k.wqk_hi, True), (k.wqk_lo, False)):
                            flat = w[:].rearrange("p a h b c -> p (a h b c)")
                            last = pe.matmul(bank, lhsT=flat[:, ds(h * P + which * HEADS * P, P)], rhs=rhs,
                                             start=start, stop=not start)
                    elif kind == "v":
                        h, b = n % HEADS, n // HEADS
                        for t in range(T):
                            for w, start in ((k.wvo_hi, True), (k.wvo_lo, False)):
                                last = pe.matmul(bank[:, t * C:(t + 1) * C], lhsT=k.xa[:, ds(b * S + t * P, P)],
                                                 rhs=w[:, ds(h * C, C)], start=(t == 0 and start), stop=not start,
                                                 skip_group_check=True)
                    elif kind == "max":
                        if c == 0:
                            pe.wait_ge(s.taken, A_N * n + TAKEN["k", 1] + 1)
                        last = pe.matmul(bank, lhsT=qa[:, par, (c // 2) * P:(c // 2 + 1) * P],
                                         rhs=ka[:, par, (c % 2) * HALF:(c % 2 + 1) * HALF], start=True, stop=True)
                    elif kind == "row":
                        pe.wait_ge(s.maxima, n + 1)
                        for t in range(T):
                            last = pe.transpose(bank[C:C + 2].bitcast(FP16)[:, t * P:(t + 1) * P], mm[:, t], k.identh[:])
                    elif kind == "den":
                        pe.wait_ge(s.added, (T - 1) * (n - 1))
                        for half in range(2):
                            last = pe.matmul(bank[half * C:(half + 1) * C], lhsT=k.ones[:, 0:C],
                                             rhs=total[:, par, half * HALF:(half + 1) * HALF], start=True, stop=True)
                    elif kind == "out":
                        pe.wait_ge(s.divided, n - 1)
                        for t in range(4):
                            last = pe.transpose(bank[:, t * P:(t + 1) * P], u[:, t * P:(t + 1) * P], k.ident[:])
                    last.then_inc(s.task, 1)

                def prologue():
                    for slot in range(T):
                        for j, kind, c in listed(slot):
                            task(0, 0, j, kind, c, skip=kind not in NEXT)

                def score(par, g, kt, first):
                    if kt == 0:
                        pe.wait_ge(s.taken, A_N * (g + 1))
                    if kt >= 2 or not first:
                        pe.wait_ge(s.exp, T * g + kt - 1)
                    keys = slice(kt * P, (kt + 1) * P)
                    for half in range(2):
                        bank = ps[2 * (kt % 2) + half]
                        cols = slice(half * HALF, (half + 1) * HALF)
                        pe.matmul(bank, lhsT=ka[:, par, keys], rhs=qa[:, par, cols], start=True, stop=False)
                        last = pe.matmul(bank, lhsT=kb[:, par, keys], rhs=qb[:, par, cols], start=False, stop=True)
                    last.then_inc(s.scores, 1)

                def values(par, g, kt):
                    pe.wait_ge(s.exp, T * g + kt + 1)
                    if kt == 0 and not (isinstance(g, int) and g == 0):
                        pe.wait_ge(s.copied, g)
                    for half in range(2):
                        last = pe.matmul(ps[6][half * C:(half + 1) * C], lhsT=v[:, par, kt],
                                         rhs=prob[:, kt % NPB, half * HALF:(half + 1) * HALF],
                                         start=(kt == 0), stop=(kt == T - 1), skip_group_check=True)
                    last.then_inc(s.pv, 1)

                def head(par, g, first, last):
                    for kt in range(T):
                        score(par, g, kt, first)
                        for j, kind, c in listed(kt):
                            task(1 - par, g + 1, j, kind, c, skip=not wanted(kind, g, first, last))
                        if kt:
                            values(par, g, kt - 1)
                        elif not first:
                            values(1 - par, g - 1, T - 1)

                pe.wait_ge(s.start, 1)
                pairs(pe, head, prologue)
                values(1, heads - 1, T - 1)
                for j, kind in ((0, "den"), (1, "out")):
                    task(1, heads + 1, j, kind, 0)

            @block.vector
            def _(dve):
                def task(par, n, j, kind, c, link, skip=False):
                    bank = ps[A_BANKS[j % 3]]
                    if skip:
                        if not (isinstance(n, int) and A_N * n + j == 0):
                            dve.wait_ge(s.taken, A_N * n + j)
                        dve.sem_inc(s.taken, 1)
                        return
                    dve.wait_ge(s.task, A_N * n + j + 1)
                    cols = slice(c * HALF, (c + 1) * HALF)
                    if kind == "q":
                        dve.wait_ge(s.split, 6 * n + 2 * c + 2)
                        dve.tensor_tensor(qa[C:P, par, cols], bank[C:P], qa[C:P, par, cols], ALU.subtract)\
                           .then_inc(s.taken, 1)
                    elif kind == "k":
                        dve.wait_ge(s.split, 6 * n + 5 + c)
                        dve.tensor_tensor(kb[0:C, par, cols], bank[0:C], ka[0:C, par, cols], ALU.subtract)\
                           .then_inc(s.taken, 1)
                    elif kind == "v":
                        dve.tensor_copy(v[:, par].rearrange("p t c -> p (t c)"), bank).then_inc(s.taken, 1)
                    elif kind == "max":
                        dve.tensor_reduce(mp[:, c // 2, c % 2:c % 2 + 1], bank, X, ALU.max).then_inc(s.taken, 1)
                        if c == 2 * T - 1:
                            dve.wait_ge(s.taken, A_N * n + j + 1)
                            link(dve.tensor_reduce(mx[:, 0], mp[:], X, ALU.max))
                            link(dve.tensor_scalar(mx[:, 0], mx[:, 0], -1.0 / MSPAN, None, ALU.mult))
                            link(dve.tensor_copy(mm[:, :, 0], mx[:, 0]))
                            link(dve.tensor_tensor(mm[:, :, 1], mx[:, 0], mm[:, :, 0], ALU.subtract))
                            dve.sem_inc(s.maxima, 1)
                    elif kind == "row":
                        dve.tensor_copy(qb[C:C + 2, par], bank[C:C + 2].bitcast(FP16)).then_inc(s.taken, 1)
                    elif kind == "den":
                        link(dve.reciprocal(inv[:], bank))
                        dve.wait_ge(s.copied, n - 1)
                        link(dve.scalar_tensor_tensor(u[:], un[:, par], k.vscale[:], inv[:], ALU.mult, ALU.mult))
                        dve.sem_inc(s.divided, 1)
                        dve.sem_inc(s.taken, 1)
                    elif kind == "out":
                        b = (n - 2) // HEADS
                        at = k.h[:, ds(b * T, T), :].rearrange("p (a t) c -> p t a c", a=2)
                        link(dve.tensor_tensor(at, at, bank.rearrange("p (t a c) -> p t a c", t=4, a=2), ALU.add))
                        dve.sem_inc(s.taken, 1)

                def tasks(par, n, skipped, steps):
                    for slot in range(T):
                        for j, kind, c in listed(slot):
                            task(par, n, j, kind, c, steps, skip=kind in skipped)

                def prologue():
                    link = Chain(dve, s.d, 0, D_STEPS)
                    tasks(0, 0, ("den", "out"), link)
                    link.fill(dve)

                def head(par, g, first, last):
                    link = Chain(dve, s.d, g + 1, D_STEPS)
                    skipped = (NEXT if last else ()) + (("den", "out") if first else ())
                    tasks(1 - par, g + 1, skipped, link)
                    link.fill(dve)

                for t in (kb,):
                    dve.memset(t[C:C + 2], MSPAN).then_inc(s.start, 1)
                pairs(dve, head, prologue)
                link = Chain(dve, s.d, heads + 1, D_STEPS)
                for j, kind in ((0, "den"), (1, "out")):
                    task(1, heads + 1, j, kind, 0, link)


F_UNITS = [(half, kt, pair) for half in range(2) for kt in range(4 * half + 4) for pair in range(2)]
F_PIECES = (
    ((0, 0, 128, 0), (2, 0, 384, 128)),
    ((1, 0, 256, 0), (5, 512, 256, 256)),
    ((3, 0, 512, 0),),
    ((4, 0, 512, 0),),
    ((4, 512, 128, 0), (6, 512, 384, 128)),
    ((5, 0, 512, 0),),
    ((6, 0, 512, 0),),
    ((7, 0, 512, 0),),
    ((7, 512, 512, 0),),
)
NV = len(F_PIECES)


def f_slots(sequence):
    slots = [[] for _ in F_UNITS]
    if sequence:
        slots[0] += [("turn", 0), ("turn", 1), ("sv", 0), ("sv", 1), ("sv", 2)]
    slots[0] += [("k", 0), ("k", 1)]
    slots[1] += [("q", 0), ("q", 1)]
    slots[2] += [("out", 1), ("q", 2), ("q", 3)]
    slots[3] += [("q", 4), ("q", 5)]
    slots[4] += [("q", 6), ("q", 7)]
    for e in range(NE):
        for v in range(NV):
            slots[4 + 4 * e + v * 4 // NV].append(("max", e * NV + v))
        slots[min(10 + 4 * e, 22)].append(("row", e))
    slots[11].append(("out", 0))
    for at, half in ((5, 1), (14, 0)):
        slots[at].append(("gate", half))
        slots[at + 2].append(("mix", half))
        slots[at + 4].append(("sum", half))
    return slots


BANKLESS = ("gate", "mix", "sum")
NEXT_F = ("turn", "sv", "k", "q", "max", "row")


def f_numbered(sequence):
    j, out = 0, []
    for slot in f_slots(sequence):
        row = []
        for kind, c in slot:
            row.append((None if kind in BANKLESS else j, kind, c))
            j += kind not in BANKLESS
        out.append(row)
    return out, j


def feedforward1(k, nc):
    NB = k.NB
    ps = k.bank
    lists = [f_numbered(m == NH - 1) for m in range(NH)]
    sizes = [n for _, n in lists]
    TB, L3 = sum(sizes), sizes[3]
    assert TB % len(A_BANKS) == 0
    PIECES = 2 + 2 * NE
    number = [{(kind, c): j for slot in sl for j, kind, c in slot} for sl, _ in lists]
    units = len(F_UNITS)
    groups = units // 2
    with ExitStack() as ctx:
        def sb(name, shape, dt):
            return ctx.enter_context(nc.sbuf_tensor(name, shape, dt))

        hb = sb("f_hb", [P, T, C], F32)
        hT = sb("f_hT", [C + 1, S], F32)
        sv = sb("f_sv", [P, T, 2 * C], F32)
        vh = sb("f_vh", [P, 2, T, 32], F32)
        nz = sb("f_nz", [P, NH, T, D], F32)
        qf = sb("f_qf", [P, 2, NE, S], BF16)
        kf = sb("f_kf", [P, 2, S], BF16)
        p1 = sb("f_p1", [P, 2, HALF], BF16)
        r1 = sb("f_r1", [P, 2, HALF], F32)
        p2 = sb("f_p2", [P, 2, HALF], BF16)
        prob = sb("f_prob", [P, NPB, 2, HALF], F32)
        oc = sb("f_oc", [P, 2, HALF], F32)
        rs = sb("f_rs", [P, 2, 4 * NE], F32)
        o = sb("f_o", [P, 2, 4, NE, D], F32)
        prod = sb("f_prod", [P, 2, 4, NE, NE * D], F32)
        lg = sb("f_lg", [P, 4, NE], F32)
        eg = sb("f_eg", [P, 4, NE], F32)
        gs = sb("f_gs", [P, 2, 4, NE], F32)
        gm = sb("f_gm", [P, 3, 4], F32)
        mp = sb("f_mp", [P, 4, 2], F32)
        mx = sb("f_mx", [P, T], F32)
        mm = sb("f_mm", [P, 2, T, 2], BF16)

        s = Parts()
        s.start = k.sem("f_start")
        s.tokens = k.sem("f_tokens")
        s.task = k.sem("f_task")
        s.taken = k.sem("f_taken")
        s.part1 = k.sem("f_part1")
        s.part2 = k.sem("f_part2")
        s.laid = k.sem("f_laid")
        s.scores = k.sem("f_scores")
        s.exp = k.sem("f_exp")
        s.pv = k.sem("f_pv")
        s.copied = k.sem("f_copied")
        s.maxima = k.sem("f_maxima")
        s.o_ready = k.sem("f_o_ready")
        s.prod_ready = k.sem("f_prod_ready")
        s.lg_ready = k.sem("f_lg_ready")
        s.eg_ready = k.sem("f_eg_ready")
        s.gs_ready = k.sem("f_gs_ready")
        s.mix_ready = k.sem("f_mix_ready")
        s.d = k.sem("f_d")
        D_STEPS = 44

        def base(m, b):
            return TB * b + L3 + sum(sizes[:m])

        def heads(eng, run_list, head):
            run_list(3, 0, -1, False, False)

            def sequence(b, first, last):
                for m in range(NH):
                    head(m, b, first and m == 0, last and m == NH - 1)

            sequence(0, True, False)
            if NB > 2:
                with eng.Fori(1, NB - 1) as b:
                    sequence(b, False, False)
            sequence(NB - 1, False, True)

        def left_out(kind, c, g, first, last):
            if kind in NEXT_F:
                return last
            if isinstance(g, int) and g < 0:
                return True
            return first and c == 1

        with nc.Block() as block:
            @block.gpsimd
            def _(pool):
                def piece(par, g, n):
                    count = PIECES * (g + 1) + n + 1
                    pool.wait_ge(s.part2, count)
                    dst = kf[:, 1 - par, (n % 2) * HALF:(n % 2 + 1) * HALF] if n < 2 else \
                        qf[:, 1 - par, (n - 2) // 2, (n % 2) * HALF:(n % 2 + 1) * HALF]
                    pool.tensor_tensor(dst, r1[:, n % 2], p2[:, n % 2], ALU.subtract).then_inc(s.laid, 1)

                def mixture(m, g, kind, c):
                    mo, go = (m, g) if c == 0 else ((m + 3) % 4, g - 1)
                    if kind == "out":
                        pool.wait_ge(s.o_ready, 2 * go + c + 1)
                        pool.tensor_tensor(
                            prod[:, c], o[:, c].rearrange("p t e d -> p t (e d)").unsqueeze(2)
                            .to_broadcast([P, 4, NE, NE * D]),
                            k.gatew[:, mo].unsqueeze(1).to_broadcast([P, 4, NE, NE * D]), ALU.mult)\
                            .then_inc(s.prod_ready, 1)
                    else:
                        pool.wait_ge(s.gs_ready, 2 * go + c + 1)
                        pool.tensor_tensor(
                            prod[:, c, :, 0].rearrange("p t (e d) -> p t e d", e=NE), o[:, c],
                            gs[:, c].unsqueeze(3).to_broadcast([P, 4, NE, D]), ALU.mult)\
                            .then_inc(s.mix_ready, 1)

                def run_list(m, at, g, first, last):
                    par = m % 2
                    for slot in lists[m][0]:
                        for j, kind, c in slot:
                            if left_out(kind, c, g, first, last):
                                continue
                            if kind in ("k", "q"):
                                piece(par, g, c if kind == "k" else 2 + c)
                            if kind in ("out", "mix"):
                                mixture(m, g, kind, c)

                def head(m, b, first, last):
                    run_list(m, base(m, b), b * NH + m, first, last)
                    if m == 1:
                        tokens(b + 1)

                def tokens(b):
                    if isinstance(b, int) and b == NB:
                        return
                    if not (isinstance(b, int) and b == 0):
                        passed(pool, k.seen, s.task, TB * (b - 1) + 2)
                    pool.tensor_copy(hb[:], k.mixed[:, ds(b * T, T)].rearrange("p t n d -> p t (n d)")).then_inc(s.tokens, 1)

                tokens(0)
                heads(pool, run_list, head)
                for kind in ("out", "mix"):
                    mixture(0, NB * NH, kind, 1)

            @block.scalar
            def _(act):
                def run_slot(m, u, at, g, first, last):
                    par = m % 2
                    pieces = [(j, c if kind == "k" else 2 + c) for j, kind, c in lists[m][0][u]
                              if kind in ("k", "q") and not left_out(kind, c, g, first, last)]
                    for x, (j, n) in enumerate(pieces):
                        count = PIECES * (g + 1) + n + 1
                        side = 2 if n < 2 else 0
                        act.wait_ge(s.task, at + j + 1)
                        act.activation(p1[:, n % 2], ps[A_BANKS[(at_static[m] + j) % 3]], ACT.Copy,
                                       scale=k.part[:, side:side + 1]).then_inc(s.part1, 1)
                    for x, (j, n) in enumerate(pieces):
                        count = PIECES * (g + 1) + n + 1
                        side = 2 if n < 2 else 0
                        act.wait_ge(s.taken, at + j + 1)
                        if not (isinstance(g, int) and g < 0 and n < 2):
                            act.wait_ge(s.laid, count - 2)
                        act.activation(p2[:, n % 2], r1[:, n % 2], ACT.Copy, scale=k.part[:, side + 1:side + 2])\
                           .then_inc(s.part2, 1)

                def copy_out(g, half):
                    act.wait_ge(s.pv, groups * g + (4 if half == 0 else groups))
                    if not (isinstance(g, int) and g == 0):
                        act.wait_ge(s.o_ready, 2 * g + half - 1)
                    act.activation(oc[:, half], ps[6], ACT.Copy).then_inc(s.copied, 1)

                def gates(g, half):
                    act.wait_ge(s.lg_ready, 2 * g + half + 1)
                    act.activation(eg[:], lg[:], ACT.Exp).then_inc(s.eg_ready, 1)

                def run_list(m, at, g, first, last):
                    for u in range(units):
                        run_slot(m, u, at, g, first, last)

                def head(m, b, first, last):
                    g = b * NH + m
                    for u, (half, kt, pair) in enumerate(F_UNITS):
                        off = max(0, kt * P - half * HALF)
                        act.wait_ge(s.scores, units * g + u + 1)
                        if u >= NPB or not first:
                            act.wait_ge(s.pv, groups * g + u // 2 - 1)
                        act.activation(prob[:, u % NPB, :, 0:HALF - off],
                                       k.psum[:, 2 * (u % 2):2 * (u % 2) + 2, 0:HALF - off], ACT.Exp,
                                       scale=float(np.sqrt(D))).then_inc(s.exp, 1)
                        run_slot(m, u, base(m, b), g, first, last)
                        if u == 0 and not first:
                            copy_out(g - 1, 1)
                        if u == 8:
                            copy_out(g, 0)
                        if u == 7 and not first:
                            gates(g - 1, 1)
                        if u == 16:
                            gates(g, 0)

                at_static = [(L3 + sum(sizes[:m])) % 3 for m in range(NH)]
                heads(act, run_list, head)
                copy_out(NB * NH - 1, 1)
                gates(NB * NH - 1, 1)

            @block.tensor
            def _(pe):
                at_static = [(L3 + sum(sizes[:m])) % 3 for m in range(NH)]

                def task(m, at, j, kind, c, g, skip):
                    bank = ps[A_BANKS[(at_static[m] + j) % 3]]
                    par = 1 - m % 2
                    n = (m + 1) % NH
                    if skip:
                        if not (isinstance(at, int) and at + j == 0):
                            pe.wait_ge(s.task, at + j)
                        pe.sem_inc(s.task, 1)
                        return
                    if kind == "turn" and not (isinstance(at, int) and at + j < 3):
                        passed(pe, k.seen, s.taken, at + j - 2)
                    elif not (isinstance(at, int) and at + j < 3):
                        pe.wait_ge(s.taken, at + j - 2)
                    if kind == "turn":
                        if c == 0:
                            passed(pe, k.seen, s.tokens, (g + 1) // NH + 1)
                        for t in range(4):
                            last = pe.transpose(bank[0:C, t * P:(t + 1) * P], hb[:, 4 * c + t], k.ident[:])
                    elif kind == "sv":
                        if c == 0:
                            pe.wait_ge(s.taken, at + j)
                        for x, t in enumerate(range(3 * c, min(3 * c + 3, T))):
                            last = pe.matmul(bank[:, x * P:(x + 1) * P], lhsT=hT[:, t * P:(t + 1) * P], rhs=k.gsv[:],
                                             start=(x == 0), stop=True, skip_group_check=True)
                    elif kind in ("k", "q"):
                        cols = slice((c % 2) * HALF, (c % 2 + 1) * HALF)
                        w = k.gk[:, n] if kind == "k" else k.gq[:, n, c // 2]
                        last = pe.matmul(bank, lhsT=w.rearrange("i s d -> i (s d)"), rhs=hT[:, cols], start=True, stop=True)
                    elif kind == "max":
                        e, v = c // NV, c % NV
                        if v == 0:
                            pe.wait_ge(s.laid, PIECES * (g + 1) + 2 + 2 * e + 2)
                        for x, (qt, k0, nk, col) in enumerate(F_PIECES[v]):
                            diagonal = k0 + nk == (qt + 1) * P
                            last = pe.matmul(bank[:, col:col + nk], lhsT=qf[:, par, e, qt * P:(qt + 1) * P],
                                             rhs=kf[:, par, k0:k0 + nk], start=(x == 0), stop=not diagonal,
                                             skip_group_check=True)
                            if diagonal:
                                last = pe.matmul(bank[:, col + nk - P:col + nk], lhsT=k.identb[:], rhs=k.mask_q[:],
                                                 start=False, stop=True, skip_group_check=True)
                    elif kind == "row":
                        pe.wait_ge(s.maxima, NE * (g + 1) + c + 1)
                        for t in range(T):
                            last = pe.transpose(bank[32:34].bitcast(BF16)[:, t * P:(t + 1) * P], mm[:, c % 2, t], k.identb[:])
                    elif kind == "out":
                        gh = g if c == 0 else g - 1
                        pe.wait_ge(s.copied, 2 * gh + c + 1)
                        for t in range(4):
                            last = pe.transpose(bank[:, t * P:(t + 1) * P], oc[:, c, t * P:(t + 1) * P], k.ident[:])
                    last.then_inc(s.task, 1)

                def run_slot(m, u, at, g, first, last):
                    for j, kind, c in lists[m][0][u]:
                        if j is not None:
                            task(m, at, j, kind, c, g, left_out(kind, c, g, first, last))

                def run_list(m, at, g, first, last):
                    pe.wait_ge(s.start, 4)
                    for u in range(units):
                        run_slot(m, u, at, g, first, last)

                def score(m, g, u, first):
                    half, kt, pair = F_UNITS[u]
                    par = m % 2
                    if u >= 2 or not first:
                        pe.wait_ge(s.exp, units * g + u - 1)
                    off = max(0, kt * P - half * HALF)
                    q0 = half * HALF + off
                    for x in range(2):
                        e = 2 * pair + x
                        bank = ps[2 * (u % 2) + x]
                        diagonal = kt * P >= half * HALF
                        last = pe.matmul(bank[:, 0:HALF - off], lhsT=kf[:, par, kt * P:(kt + 1) * P],
                                         rhs=qf[:, par, e, q0:(half + 1) * HALF], start=True, stop=not diagonal,
                                         skip_group_check=True)
                        if diagonal:
                            last = pe.matmul(bank[:, 0:P], lhsT=k.identb[:], rhs=k.mask_k[:], start=False, stop=True,
                                             skip_group_check=True)
                    last.then_inc(s.scores, 1)

                def values(m, g, grp):
                    half, kt, _ = F_UNITS[2 * grp]
                    par = m % 2
                    off = max(0, kt * P - half * HALF)
                    pe.wait_ge(s.exp, units * g + 2 * grp + 2)
                    if kt == 0 and not (half == 0 and isinstance(g, int) and g == 0):
                        pe.wait_ge(s.copied, 2 * g + half)
                    for e in range(NE):
                        last = pe.matmul(ps[6][32 * e:32 * e + 32, off:HALF], lhsT=vh[:, par, kt],
                                         rhs=prob[:, (2 * grp + e // 2) % NPB, e % 2, 0:HALF - off],
                                         start=(kt == 0), stop=(kt == 4 * half + 3), skip_group_check=True)
                    last.then_inc(s.pv, 1)

                def head(m, b, first, last):
                    g = b * NH + m
                    at = base(m, b)
                    pe.wait_ge(s.taken, at)
                    for u in range(units):
                        score(m, g, u, first)
                        if u == 0 and not first:
                            values(1 - m % 2, g - 1, groups - 1)
                        run_slot(m, u, at, g, first, last)
                        if u % 2 == 0 and u:
                            values(m, g, u // 2 - 1)

                heads(pe, run_list, head)
                values(1, NB * NH - 1, groups - 1)
                task(0, base(0, NB), 0, "out", 1, NB * NH, False)

            @block.vector
            def _(dve):
                at_static = [(L3 + sum(sizes[:m])) % 3 for m in range(NH)]

                def task(m, at, j, kind, c, g, skip, link):
                    par = 1 - m % 2
                    n = (m + 1) % NH
                    if skip:
                        if j is not None:
                            if not (isinstance(at, int) and at + j == 0):
                                dve.wait_ge(s.taken, at + j)
                            dve.sem_inc(s.taken, 1)
                        return
                    if j is not None:
                        bank = ps[A_BANKS[(at_static[m] + j) % 3]]
                        dve.wait_ge(s.task, at + j + 1)
                    mo, go = (m, g) if c == 0 else ((m + 3) % 4, g - 1)
                    if kind == "turn":
                        dve.tensor_copy(hT[0:C, c * HALF:(c + 1) * HALF], bank[0:C]).then_inc(s.taken, 1)
                    elif kind == "sv":
                        t0, t1 = 3 * c, min(3 * c + 3, T)
                        dve.tensor_copy(sv[:, t0:t1], bank[:, 0:(t1 - t0) * P].rearrange("p (t x) -> p t x", x=P))\
                           .then_inc(s.taken, 1)
                    elif kind in ("k", "q"):
                        x = c if kind == "k" else 2 + c
                        if kind == "k" and c == 0:
                            if n == 0:
                                dve.wait_ge(s.taken, at + j)
                            link(dve.tensor_copy(vh[:, par, :, 0:D], sv[:, :, C + n * D:C + (n + 1) * D]))
                            link(dve.tensor_scalar(nz[:, n], sv[:, :, n * D:(n + 1) * D], 0.0, None, ALU.not_equal))
                        dve.wait_ge(s.part1, PIECES * (g + 1) + x + 1)
                        if not (isinstance(g, int) and g < 0 and x < 2):
                            dve.wait_ge(s.laid, PIECES * (g + 1) + x - 1)
                        dve.tensor_tensor(r1[:, x % 2], bank, p1[:, x % 2], ALU.subtract).then_inc(s.taken, 1)
                    elif kind == "max":
                        e, v = c // NV, c % NV
                        pieces = F_PIECES[v]
                        for x, (qt, k0, nk, col) in enumerate(pieces):
                            to = mx[:, qt:qt + 1] if qt < 4 else mp[:, qt - 4, k0 // HALF:k0 // HALF + 1]
                            ins = dve.tensor_reduce(to, bank[:, col:col + nk], X, ALU.max)
                            if x == len(pieces) - 1:
                                ins.then_inc(s.taken, 1)
                            else:
                                link(ins)
                        if v == NV - 1:
                            dve.wait_ge(s.taken, at + j + 1)
                            link(dve.tensor_reduce(mx[:, 4:8], mp[:], X, ALU.max))
                            link(dve.tensor_scalar(mm[:, e % 2, :, 0], mx[:], -1.0, None, ALU.mult))
                            link(dve.scalar_tensor_tensor(mm[:, e % 2, :, 1], mx[:], -1.0, mm[:, e % 2, :, 0],
                                                          ALU.mult, ALU.subtract))
                            dve.sem_inc(s.maxima, 1)
                    elif kind == "row":
                        dve.tensor_copy(qf[32:34, par, c], bank[32:34].bitcast(BF16)).then_inc(s.taken, 1)
                    elif kind == "out":
                        all_ = bank.rearrange("p (g x) -> p g x", x=32)
                        link(dve.reciprocal(rs[:, c], all_[:, :, D]))
                        o_c = o[:, c].rearrange("p t e d -> p (t e) d")
                        link(dve.tensor_tensor(o_c, all_[:, :, 0:D], wide(rs[:, c], D), ALU.mult))
                        link(dve.tensor_tensor(
                            o[:, c], o[:, c], nz[:, mo, 4 * c:4 * c + 4].unsqueeze(2).to_broadcast([P, 4, NE, D]), ALU.mult))
                        dve.sem_inc(s.o_ready, 1)
                        dve.sem_inc(s.taken, 1)
                    elif kind == "gate":
                        dve.wait_ge(s.prod_ready, 2 * go + c + 1)
                        link(dve.tensor_reduce(lg[:], prod[:, c], X, ALU.add))
                        link(dve.tensor_tensor(lg[:], lg[:], rows(k.gateb[:, mo], 4), ALU.add))
                        link(dve.tensor_reduce(gm[:, 0], lg[:], X, ALU.max))
                        dve.tensor_tensor(lg[:], lg[:], wide(gm[:, 0], NE), ALU.subtract).then_inc(s.lg_ready, 1)
                    elif kind == "mix":
                        dve.wait_ge(s.eg_ready, 2 * go + c + 1)
                        link(dve.tensor_reduce(gm[:, 1], eg[:], X, ALU.add))
                        link(dve.reciprocal(gm[:, 2], gm[:, 1]))
                        dve.tensor_tensor(gs[:, c], eg[:], wide(gm[:, 2], NE), ALU.mult).then_inc(s.gs_ready, 1)
                    elif kind == "sum":
                        dve.wait_ge(s.mix_ready, 2 * go + c + 1)
                        bo = go // NH
                        link(dve.tensor_reduce(k.mixed[:, ds(bo * T + 4 * c, 4), mo],
                                               prod[:, c, :, 0].rearrange("p t (e d) -> p t d e", e=NE), X, ALU.add))

                def run_list(m, at, g, first, last):
                    link = Chain(dve, s.d, g + 1, D_STEPS)
                    for u in range(units):
                        for j, kind, c in lists[m][0][u]:
                            task(m, at, j, kind, c, g, left_out(kind, c, g, first, last), link)
                    assert link.n <= D_STEPS, link.n
                    link.fill(dve)

                def head(m, b, first, last):
                    run_list(m, base(m, b), b * NH + m, first, last)

                dve.memset(hT[C:C + 1], 1.0).then_inc(s.start, 1)
                dve.memset(vh[:], 0.0).then_inc(s.start, 1)
                dve.wait_ge(s.start, 2)
                dve.memset(vh[:, :, :, D:D + 1], 1.0).then_inc(s.start, 2)
                heads(dve, run_list, head)
                link = Chain(dve, s.d, NB * NH + 1, D_STEPS)
                for j, kind in ((0, "out"), (None, "gate"), (None, "mix"), (None, "sum")):
                    task(0, base(0, NB), j, kind, 1, NB * NH, False, link)


def normalize1(k, nc):
    k.mixed = k.xa[:].bitcast(F32).rearrange("p (t n d) -> p t n d", n=NH, d=D)
    with ExitStack() as ctx:
        def sb(name, shape, dt):
            return ctx.enter_context(nc.sbuf_tensor(name, shape, dt))

        xc = sb("n_xc", [P, 2, T, C], F32)
        sq = sb("n_sq", [P, 2, T, C], F32)
        st = sb("n_st", [P, 2, 4, T], F32)
        d = k.sem("n_d")
        var, std = ([k.sem(f"n_{w}{j}") for j in range(2)] for w in ("var", "std"))
        with nc.Block() as block:
            @block.scalar
            def _(act):
                with act.Fori(0, k.NB // 2) as b:
                    for j in range(2):
                        root(act, st[:, j], k.eps_ln[:], C, var[j], std[j], b)

            @block.vector
            def _(dve):
                with dve.Fori(0, k.NB // 2) as b:
                    link = Chain(dve, d, b, 12)
                    for j in range(2):
                        at = ds((2 * b + j) * T, T)
                        normalize(dve, link, k.h[:, at], k.mixed[:, at].rearrange("p t n d -> p t (n d)"),
                                  xc[:, j], sq[:, j], st[:, j], C, var[j], std[j], b)
                    link.end()


def residual1(k, nc):
    ps = k.bank
    k.resid = k.sb("resid", [P, T, NH, D], F32)
    with ExitStack() as ctx:
        hT = ctx.enter_context(nc.sbuf_tensor("r_hT", [C + 1, S], F32))
        one, turned, copied, product, done = (k.sem("r_" + n) for n in ("one", "turned", "copied", "product", "done"))
        with nc.Block() as block:
            @block.tensor
            def _(pe):
                pe.wait_ge(one, 1)
                for n in range(NH):
                    if n:
                        pe.wait_ge(done, n)
                    for t in range(T):
                        last = pe.transpose(ps[t // 4][0:C, (t % 4) * P:(t % 4 + 1) * P],
                                            k.mixed[:, n * T + t].rearrange("p n d -> p (n d)"), k.ident[:])
                    last.then_inc(turned, 1)
                    pe.wait_ge(copied, n + 1)
                    for t in range(T):
                        last = pe.matmul(ps[2][:, t * D:(t + 1) * D], lhsT=hT[:, t * P:(t + 1) * P],
                                         rhs=k.gsv[:, n * D:(n + 1) * D], start=(t == 0), stop=True, skip_group_check=True)
                    last.then_inc(product, 1)

            @block.vector
            def _(dve):
                dve.memset(hT[C:C + 1], 1.0).then_inc(one, 1)
                for n in range(NH):
                    dve.wait_ge(turned, n + 1)
                    dve.tensor_copy(hT[0:C, :], k.psum[0:C, 0:2].rearrange("p a n -> p (a n)")).then_inc(copied, 1)
                    dve.wait_ge(product, n + 1)
                    dve.tensor_copy(k.resid[:, :, n], ps[2][:, 0:T * D].rearrange("p (t d) -> p t d", t=T)).then_inc(done, 1)


def finish1(k, nc, out):
    NB = k.NB
    ps = k.bank
    G = T * NH
    with ExitStack() as ctx:
        def sb(name, shape, dt):
            return ctx.enter_context(nc.sbuf_tensor(name, shape, dt))

        x = sb("z_x", [P, G, D], F32)
        xc = sb("z_xc", [P, G, D], F32)
        sq = sb("z_sq", [P, G, D], F32)
        st = sb("z_st", [P, 4, G], F32)
        fT = sb("z_fT", [C, S], F32)
        nzT = sb("z_nzT", [C, S], F32)
        h1 = sb("z_h1", [C, S], F32)
        h2 = sb("z_h2", [C, S], F32)
        lg = sb("z_lg", [P, T, NH], F32)
        eg = sb("z_eg", [P, T, NH], F32)
        gm = sb("z_gm", [P, 3, T], F32)
        y = sb("z_y", [P, 2, T, C], F32)
        s = Parts()
        s.done = k.sem("z_done")
        s.f_ready = k.sem("z_f_ready")
        s.turned = k.sem("z_turned")
        s.fc1 = k.sem("z_fc1")
        s.relu = k.sem("z_relu")
        s.h1_ready = k.sem("z_h1_ready")
        s.fc2 = k.sem("z_fc2")
        s.h2_ready = k.sem("z_h2_ready")
        s.back = k.sem("z_back")
        s.o_ready = k.sem("z_o_ready")
        s.turn_o = k.sem("z_turn_o")
        s.oT_ready = k.sem("z_oT_ready")
        s.gate = k.sem("z_gate")
        s.lg_ready = k.sem("z_lg_ready")
        s.eg_ready = k.sem("z_eg_ready")
        s.y_ready = k.sem("z_y_ready")
        s.stored = k.sem("z_stored")
        s.d = k.sem("z_d")
        var = [k.sem(f"z_var{j}") for j in range(2)]
        std = [k.sem(f"z_std{j}") for j in range(2)]
        DVE_STEPS = 28

        with nc.Block() as block:
            @block.scalar
            def _(act):
                with act.Fori(0, NB) as b:
                    root(act, st, k.eps_ffn[:], D, var[0], std[0], b)
                    for j in range(2):
                        cols = slice(j * HALF, (j + 1) * HALF)
                        act.wait_ge(s.fc1, 2 * b + j + 1)
                        act.activation(h1[:, cols], ps[2 + j][0:C], ACT.Relu, bias=k.fcb[:, 0:1]).then_inc(s.relu, 1)
                    root(act, st, k.eps_ffn[:], D, var[1], std[1], b)
                    act.wait_ge(s.turn_o, b + 1)
                    act.activation(fT[:], k.psum[0:C, 0:2].rearrange("p a n -> p (a n)"), ACT.Copy).then_inc(s.oT_ready, 1)
                    act.wait_ge(s.lg_ready, b + 1)
                    act.activation(eg[:], lg[:], ACT.Exp).then_inc(s.eg_ready, 1)

            @block.tensor
            def _(pe):
                def turn(src, sig):
                    for t in range(T):
                        last = pe.transpose(ps[t // 4][0:C, (t % 4) * P:(t % 4 + 1) * P],
                                            src[:, t * NH:(t + 1) * NH].rearrange("p n d -> p (n d)"), k.ident[:])
                    last.then_inc(sig, 1)

                with pe.Fori(0, NB) as b:
                    passed(pe, k.seen, s.f_ready, b + 1)
                    turn(x, s.turned)
                    passed(pe, k.seen, s.h1_ready, 2 * b + 1)
                    for j in range(2):
                        pe.matmul(ps[2 + j][0:C], lhsT=k.fcT[:, 0], rhs=fT[:, j * HALF:(j + 1) * HALF], start=True, stop=True)\
                          .then_inc(s.fc1, 1)
                    passed(pe, k.seen, s.h1_ready, 2 * b + 2)
                    for j in range(2):
                        last = pe.matmul(ps[4 + j][0:C], lhsT=k.fcT[:, 1], rhs=h1[:, j * HALF:(j + 1) * HALF],
                                         start=True, stop=True)
                    last.then_inc(s.fc2, 1)
                    passed(pe, k.seen, s.h2_ready, b + 1)
                    for t in range(T):
                        last = pe.transpose(ps[6][:, t * C:(t + 1) * C], h2[:, t * P:(t + 1) * P], k.ident[0:C, 0:C])
                    last.then_inc(s.back, 1)
                    passed(pe, k.seen, s.o_ready, b + 1)
                    turn(x, s.turn_o)
                    pe.wait_ge(s.oT_ready, b + 1)
                    for t in range(T):
                        last = pe.matmul(ps[7][:, t * NH:(t + 1) * NH], lhsT=fT[:, t * P:(t + 1) * P], rhs=k.fgT[:],
                                         start=(t == 0), stop=True, skip_group_check=True)
                    last.then_inc(s.gate, 1)

            @block.vector
            def _(dve):
                with dve.Fori(0, NB) as b:
                    link = Chain(dve, s.d, b, DVE_STEPS)
                    link(dve.tensor_tensor(x[:].rearrange("p (t n) d -> p t (n d)", t=T),
                                           k.mixed[:, ds(b * T, T)].rearrange("p t n d -> p t (n d)"),
                                           k.resid[:].rearrange("p t n d -> p t (n d)"), ALU.add))
                    normalize(dve, link, x[:], x[:], xc[:], sq[:], st, D, var[0], std[0], b)
                    link(dve.tensor_tensor(x[:], x[:], rows(k.lnp[:, 0], G), ALU.mult))
                    link(dve.tensor_tensor(x[:], x[:], rows(k.lnp[:, 1], G), ALU.add))
                    dve.sem_inc(s.f_ready, 1)
                    dve.wait_ge(s.turned, b + 1)
                    both = k.psum[0:C, 0:2].rearrange("p a n -> p (a n)")
                    link(dve.tensor_copy(fT[:], both))
                    dve.sem_inc(s.h1_ready, 1)
                    link(dve.tensor_scalar(nzT[:], fT[:], 0.0, None, ALU.not_equal))
                    dve.wait_ge(s.relu, 2 * b + 2)
                    link(dve.tensor_tensor(h1[:], h1[:], nzT[:], ALU.mult))
                    dve.sem_inc(s.h1_ready, 1)
                    dve.wait_ge(s.fc2, b + 1)
                    link(dve.scalar_tensor_tensor(h2[:], k.psum[0:C, 4:6].rearrange("p a n -> p (a n)"), k.fcb[:, 1:2],
                                                  nzT[:], ALU.add, ALU.mult))
                    link(dve.tensor_tensor(h2[:], h2[:], fT[:], ALU.add))
                    dve.sem_inc(s.h2_ready, 1)
                    dve.wait_ge(s.back, b + 1)
                    link(dve.tensor_copy(x[:], ps[6].rearrange("p (g d) -> p g d", d=D)))
                    normalize(dve, link, x[:], x[:], xc[:], sq[:], st, D, var[1], std[1], b)
                    link(dve.tensor_tensor(x[:], x[:], rows(k.lnp[:, 2], G), ALU.mult))
                    link(dve.tensor_tensor(x[:], x[:], rows(k.lnp[:, 3], G), ALU.add))
                    dve.sem_inc(s.o_ready, 1)
                    dve.wait_ge(s.gate, b + 1)
                    lg_in = ps[7][:, 0:T * NH].rearrange("p (t n) -> p t n", t=T)
                    link(dve.tensor_reduce(gm[:, 0], lg_in, X, ALU.max))
                    dve.tensor_tensor(lg[:], lg_in, wide(gm[:, 0], NH), ALU.subtract).then_inc(s.lg_ready, 1)
                    dve.wait_ge(s.eg_ready, b + 1)
                    link(dve.tensor_reduce(gm[:, 1], eg[:], X, ALU.add))
                    link(dve.reciprocal(gm[:, 2], gm[:, 1]))
                    link(dve.tensor_tensor(eg[:], eg[:], wide(gm[:, 2], NH), ALU.mult))
                    link(dve.tensor_tensor(x[:], x[:], wide(eg[:].rearrange("p t n -> p (t n)"), D), ALU.mult))
                    at = k.h[:, ds(b * T, T)]
                    dve.tensor_tensor(at, at, x[:].rearrange("p (t n) d -> p t (n d)", t=T), ALU.add).then_inc(s.y_ready, 1)
                    dve.wait_ge(s.y_ready, b + 1)
                    link.end()

            @block.sync
            def _(sp):
                with sp.Fori(0, NB) as b:
                    sp.wait_ge(s.y_ready, b + 1)
                    sp.dma_start(out[ds(b, 1)].rearrange("b (t p) c -> p (b t) c", p=P), k.h[:, ds(b * T, T)])\
                      .then_inc(s.stored, 16)
                sp.wait_ge(s.stored, 16 * NB)


_INS = ["x", "itok_BS_0_255", "itok_BS_0_511", "itok_BS_0_127", "itok_BS_0_63", "itok_BS_0_3"]


def tower(nc, NB, stop=None, **t):
    k = Parts()
    k.NB = NB
    k.id_names = _INS
    k.ids = t
    a = {n.split("_", 2)[2]: v for n, v in t.items() if n[:3] in ("L0_", "L1_")}
    with ExitStack() as ctx:
        k.sb = lambda name, shape, dt: ctx.enter_context(nc.sbuf_tensor(name, shape, dt))
        k.sem = lambda name: ctx.enter_context(nc.semaphore(name))
        k.psum = ctx.enter_context(nc.psum_tensor("psum", [P, 8, 512], F32))
        k.bank = [k.psum[:, i] for i in range(8)]
        k.h = k.sb("h", [P, NB * T, C], F32)
        k.xa = k.sb("xa", [P, NB * S], FP16)
        k.seen = k.sem("seen")
        with ExitStack() as setup:
            k.tmp = lambda name, shape, dt: setup.enter_context(nc.sbuf_tensor(name, shape, dt))
            load_weights(k, nc, a)
            constants(k, nc)
            prepare(k, nc)
        layer0(k, nc, a)
        if stop == "l0":
            store(k, nc, t["out"])
            return
        attention1(k, nc)
        if stop == "a1":
            store(k, nc, t["out"])
            return
        normalize1(k, nc)
        residual1(k, nc)
        feedforward1(k, nc)
        finish1(k, nc, t["out"])


def store(k, nc, out):
    s = k.sem("stored")
    with nc.Block() as block:
        @block.sync
        def _(sp):
            sp.dma_start(out.rearrange("b (t p) c -> p (b t) c", p=P), k.h[:]).then_inc(s, 16)
            sp.wait_ge(s, 16)


def kernel(**inputs):
    import numpy as _np
    import concourse.bacc as _bacc
    from concourse import mybir as _mybir
    from concourse.bass_utils import run_bass_kernel_spmd as _run

    nc = _bacc.Bacc("TRN2", target_bir_lowering=False, num_devices=1)
    arrays, args = {}, {}
    for name, value in inputs.items():
        a = _np.ascontiguousarray(value)
        arrays[f"in_{name}_dram"] = a
        args[name] = nc.dram_tensor(f"in_{name}_dram", a.shape, _mybir.dt.from_np(a.dtype), kind="ExternalInput").ap()
    NB = inputs["x"].shape[0]
    args["out"] = nc.dram_tensor("out_0_dram", (NB, S, C), _mybir.dt.float32, kind="ExternalOutput").ap()
    tower(nc, NB, **args)
    r = _run(nc, [arrays], core_ids=[0])
    return r.results[0]["out_0_dram"]
```

```python
from contextlib import ExitStack

import numpy as np

import concourse.bass as bass
from concourse import mybir

F32 = mybir.dt.float32
BF16 = mybir.dt.bfloat16
FP16 = mybir.dt.float16
I32 = mybir.dt.int32
ACT = mybir.ActivationFunctionType
ALU = mybir.AluOpType
X = mybir.AxisListType.X
ds = bass.ds

P = 128
S = 1024
T = S // P
HALF = 512
C = 64
HEADS = 8
HID = 256
EXPERTS = 8
NH, NE, D = 4, 4, 16
VR = 96
SLOTS = 8
BIG = -1.0e30
WSPAN = 512.0
MSPAN = 32768.0
EPS_W, EPS_LN, EPS_FFN = 1e-8, 1e-5, 1e-8


class Parts:
    pass


def load_weights(k, nc, a):
    sb = k.sb
    k.ident = sb("ident", [P, P], F32)
    k.identb = sb("identb", [P, P], BF16)
    k.identh = sb("identh", [P, P], FP16)
    k.ones = sb("ones", [P, P], F32)
    k.onesb = sb("onesb", [P, P], BF16)
    k.tab3 = sb("tab3", [P, 4, 3, C], BF16)
    k.sel = sb("sel", [6, 8, C], BF16)
    k.vcol = sb("vcol", [P, 4], F32)
    k.tok_b = sb("tok_b", [P, C], F32)
    k.tok_g = sb("tok_g", [P, C], F32)
    k.tok_beta = sb("tok_beta", [P, C], F32)
    k.eps_ln = sb("eps_ln", [P, 1], F32)
    k.eps_ffn = sb("eps_ffn", [P, 1], F32)
    k.wqT = sb("wqT", [C, C], F32)
    k.wkvT = sb("wkvT", [C, 2 * C], F32)
    k.wpT = sb("wpT", [C, C], F32)
    k.bproj = sb("bproj", [P, C], F32)
    k.blk8 = sb("blk8", [C, C], F32)
    k.w1 = sb("w1", [C, HID], F32)
    k.b1 = sb("b1", [P, 2], F32)
    k.wg = sb("wg", [P, 2, EXPERTS], F32)
    k.bg = sb("bg", [P, EXPERTS], F32)
    k.wd = sb("wd", [P, 2, EXPERTS, C], F32)
    k.bd3 = sb("bd3", [3, EXPERTS * C], BF16)
    k.rank = sb("rank", [P, EXPERTS], F32)
    k.escale = sb("escale", [P, 1], F32)
    k.vscale = sb("vscale", [P, 1], F32)
    k.wqk_hi = sb("wqk_hi", [P, 2, HEADS, 2, C], FP16)
    k.wqk_lo = sb("wqk_lo", [P, 2, HEADS, 2, C], FP16)
    k.wvo_hi = sb("wvo_hi", [P, HEADS * C], FP16)
    k.wvo_lo = sb("wvo_lo", [P, HEADS * C], FP16)
    k.bout = sb("bout", [P, C], F32)
    k.gq = sb("gq", [C + 1, NH, NE, SLOTS, D], F32)
    k.gk = sb("gk", [C + 1, NH, SLOTS, D], F32)
    k.gsv = sb("gsv", [C + 1, 2 * C], F32)
    k.gatew = sb("gatew", [P, NH, NE, NE * D], F32)
    k.gateb = sb("gateb", [P, NH, NE], F32)
    k.lnp = sb("lnp", [P, 4, D], F32)
    k.fcT = sb("fcT", [C, 2, C], F32)
    k.fcb = sb("fcb", [C, 2], F32)
    k.fgT = sb("fgT", [C, NH], F32)
    k.mask_q = sb("mask_q", [P, P], BF16)
    k.mask_k = sb("mask_k", [P, P], BF16)
    k.part = sb("part", [P, 4], F32)
    tmp = k.tmp
    k.eblk = tmp("eblk", [P, 4, VR], F32)
    k.eblkT = tmp("eblkT", [VR, 4, P], F32)
    k.w = tmp("w", [C, VR], F32)
    k.wtmp = tmp("wtmp", [C, 4, VR], F32)
    k.wcol = tmp("wcol", [C, 4], F32)
    k.weffT = tmp("weffT", [VR, C], F32)
    k.tab = tmp("tab", [P, 4, C], F32)
    k.tabr = tmp("tabr", [P, 4, C], F32)
    k.vint = tmp("vint", [P, 1], I32)
    k.wqn = tmp("wqn", [C, C], F32)
    k.wkvn = tmp("wkvn", [2 * C, C], F32)
    k.wpn = tmp("wpn", [C, C], F32)
    k.bd1 = tmp("bd1", [1, EXPERTS * C], F32)
    k.bds = tmp("bds", [1, 3, EXPERTS * C], BF16)
    k.bdr = tmp("bdr", [1, EXPERTS * C], F32)
    k.ranki = tmp("ranki", [P, EXPERTS], I32)
    k.aq = tmp("aq", [P, 2, HEADS * C], F32)
    k.av = tmp("av", [C, HEADS * C], F32)
    k.avT = tmp("avT", [C, HEADS, 2, C], F32)
    k.ao = tmp("ao", [C, HEADS, C], F32)
    k.avo = tmp("avo", [P, HEADS * C], F32)
    k.amax = tmp("amax", [P, 3], F32)
    k.amaxr = tmp("amaxr", [P, 3], F32)
    k.ainv = tmp("ainv", [P, 3], F32)
    k.an = tmp("an", [P, 3, HEADS * C], F32)
    k.hld = tmp("hld", [D, NH, C + 1], F32)
    k.hln = tmp("hln", [C, C + 1], F32)
    k.fq = tmp("fq", [C, NH, D], F32)
    k.fk = tmp("fk", [C, D], F32)
    k.fv = tmp("fv", [C, D], F32)
    k.fqT = tmp("fqT", [D, NH, C], F32)
    k.fkT = tmp("fkT", [D, C], F32)
    k.fvT = tmp("fvT", [D, C], F32)
    k.fc = tmp("fc", [C, 2, C], F32)
    k.fgn = tmp("fgn", [NH, C], F32)

    loaded, cleared = k.sem("loaded"), k.sem("cleared")
    k.loaded = loaded
    loads = [
        (k.w[:], a["W"]), (k.wqn[:], a["Wq"]), (k.wkvn[:], a["Wkv"]), (k.wpn[:], a["Wproj"]),
        (k.tok_b[:], a["b"].partition_broadcast(P)), (k.tok_g[:], a["gamma"].partition_broadcast(P)),
        (k.tok_beta[:], a["beta"].partition_broadcast(P)), (k.bproj[:], a["bproj"].partition_broadcast(P)),
        (k.w1[:], a["W1"]), (k.b1[:], a["b1"].rearrange("(c p) -> p c", p=P)),
        (k.wg[:], a["Wg"].rearrange("(c p) e -> p c e", p=P)), (k.bg[:], a["bg"].partition_broadcast(P)),
        (k.wd[:, 0], a["Wd"][:, 0:P, :].rearrange("e p c -> p e c")),
        (k.wd[:, 1], a["Wd"][:, P:HID, :].rearrange("e p c -> p e c")),
        (k.bd1[:], a["bd"].rearrange("(o e) c -> o (e c)", o=1)),
        (k.aq[0:C, 0], a["WQ"]), (k.aq[C:P, 0], a["WQ"]), (k.aq[0:C, 1], a["WK"]), (k.aq[C:P, 1], a["WK"]),
        (k.av[:], a["WV"]), (k.ao[:], a["Wout"].rearrange("(h c) o -> c h o", h=HEADS)),
        (k.bout[:], a["bout"].partition_broadcast(P)),
        (k.hld[:, :, 0:C], a["hl_w"].rearrange("n d h -> d n h")),
        (k.hld[:, :, C], a["hl_b"].rearrange("n d -> d n")),
        (k.hln[:, 0:C], a["hl_w"].rearrange("n d h -> (n d) h")),
        (k.hln[:, C:C + 1], a["hl_b"].rearrange("n (d o) -> (n d) o", o=1)),
        (k.fq[:], a["wq"].rearrange("n e o d -> (e o) n d")),
        (k.fk[:], a["wk"].rearrange("n o d -> (n o) d")), (k.fv[:], a["wv"].rearrange("n o d -> (n o) d")),
        (k.gatew[:], a["gate_w"].partition_broadcast(P)), (k.gateb[:], a["gate_b"].partition_broadcast(P)),
        (k.lnp[:, 0], a["ln_g"].partition_broadcast(P)), (k.lnp[:, 1], a["ln_b"].partition_broadcast(P)),
        (k.lnp[:, 2], a["fnorm_g"].partition_broadcast(P)), (k.lnp[:, 3], a["fnorm_b"].partition_broadcast(P)),
        (k.fgn[:], a["fgate_w"]),
    ]
    diagonal = [
        (k.eblk[0:64, 0, 0:16], a["E_et"]), (k.eblk[64:128, 0, 16:32], a["E_fc"]),
        (k.eblk[:, 1, 32:48], a["E_sc"]), (k.eblk[:, 2, 48:64], a["E_of"]),
        (k.eblk[0:64, 3, 64:80], a["E_tt"]), (k.eblk[64:68, 3, 80:96], a["E_rc"]),
    ]
    for n in range(NH):
        at = slice(n * D, n * D + D)
        diagonal += [(k.fc[at, 0, at], a["fc1_w"]), (k.fc[at, 1, at], a["fc2_w"]),
                     (k.fcb[at, 0:1], a["fc1_b"].unsqueeze(1)), (k.fcb[at, 1:2], a["fc2_b"].unsqueeze(1))]
    k.n_loads = 16 * (len(loads) + len(diagonal))

    with nc.allow_non_contiguous_dma(reason="small weights, once"), nc.Block() as block:
        @block.sync
        def _(sp):
            for dst, src in loads[::2]:
                sp.dma_start(dst, src).then_inc(loaded, 16)
            sp.wait_ge(cleared, 2)
            for dst, src in diagonal:
                sp.dma_start(dst, src).then_inc(loaded, 16)
            sp.wait_ge(loaded, k.n_loads)

        @block.scalar
        def _(act):
            for dst, src in loads[1::2]:
                act.dma_start(dst, src).then_inc(loaded, 16)

        @block.vector
        def _(dve):
            dve.memset(k.eblk[:], 0.0).then_inc(cleared, 1)
            dve.memset(k.fc[:], 0.0).then_inc(cleared, 1)


def constants(k, nc):
    c = k.sem("const")
    with nc.Block() as block:
        @block.gpsimd
        def _(pool):
            n = 0

            def link(ins):
                nonlocal n
                n += 1
                ins.then_inc(c, 1)
                pool.wait_ge(c, n)

            def cut(t, x, v, size=1):
                link(pool.affine_select(out=t, in_=t, pattern=[[0, size]], compare_op=ALU.is_gt, fill=v,
                                        base=x, channel_multiplier=-1))

            link(pool.memset(k.ident[:], 0.0))
            link(pool.affine_select(out=k.ident[:], in_=k.ident[:], pattern=[[-1, P]], compare_op=ALU.not_equal,
                                    fill=1.0, base=0, channel_multiplier=1))
            link(pool.tensor_copy(k.identb[:], k.ident[:]))
            link(pool.tensor_copy(k.identh[:], k.ident[:]))
            link(pool.memset(k.ones[:], 1.0))
            link(pool.memset(k.onesb[:], 1.0))
            link(pool.memset(k.eps_ln[:], EPS_LN))
            link(pool.memset(k.eps_ffn[:], EPS_FFN))
            link(pool.memset(k.mask_q[:], 0.0))
            link(pool.affine_select(out=k.mask_q[:], in_=k.mask_q[:], pattern=[[-1, P]], compare_op=ALU.is_ge,
                                    fill=BIG, base=0, channel_multiplier=1))
            link(pool.memset(k.mask_k[:], 0.0))
            link(pool.affine_select(out=k.mask_k[:], in_=k.mask_k[:], pattern=[[1, P]], compare_op=ALU.is_ge,
                                    fill=BIG, base=0, channel_multiplier=-1))
            b8 = k.blk8[:].rearrange("p (h d) -> p h d", h=HEADS)
            link(pool.memset(k.blk8[:], 1.0))
            link(pool.affine_select(out=b8, in_=b8, pattern=[[-8, HEADS], [0, 8]], compare_op=ALU.is_ge,
                                    fill=0.0, base=0, channel_multiplier=1))
            link(pool.affine_select(out=b8, in_=b8, pattern=[[8, HEADS], [0, 8]], compare_op=ALU.is_ge,
                                    fill=0.0, base=7, channel_multiplier=-1))
            link(pool.memset(k.sel[:], 0.0))
            for view, pattern, base in (
                (k.sel[:, 0:2], [[-1, 2], [0, C]], 0),
                (k.sel[:, 2:6].rearrange("p (a b) c -> p a (b c)", a=2), [[-1, 2], [0, 2 * C]], -2),
                (k.sel[:, 6:8], [[-1, 2], [0, C]], -4),
            ):
                link(pool.affine_select(out=view, in_=view, pattern=pattern, compare_op=ALU.not_equal,
                                        fill=1.0, base=base, channel_multiplier=1))
            link(pool.iota(k.vint[:], pattern=[[0, 1]], base=0, channel_multiplier=1))
            for j in range(4):
                link(pool.tensor_copy(k.vcol[:, j:j + 1], k.vint[:]))
            for j in (0, 3):
                link(pool.tensor_scalar(k.vcol[64:128, j:j + 1], k.vcol[64:128, j:j + 1], -64.0, None, ALU.add))
            link(pool.iota(k.ranki[:], pattern=[[-1, EXPERTS]], base=EXPERTS, channel_multiplier=0))
            link(pool.tensor_copy(k.rank[:], k.ranki[:]))
            link(pool.memset(k.part[:], 0.0))
            link(pool.memset(k.part[64:128, 0:1], 1.0))
            link(pool.memset(k.part[96:128, 1:2], 1.0))
            for x, v in ((16, 1.0), (32, 0.0), (48, 1.0), (64, 0.0), (80, 1.0), (96, 0.0)):
                cut(k.part[:, 2:3], x, v)
            for x, v in ((48, 1.0), (64, 0.0)):
                cut(k.part[:, 3:4], x, v)
            link(pool.memset(k.gq[:], 0.0))
            link(pool.memset(k.gk[:], 0.0))


PREPARE = (
    ["abs_sum", "abs_all", "scale", "scale_eps", "inverse", "ratio", "above", "below", "sign", "ternary",
     "delta", "weff", "weff_turn", "weff_out"]
    + [f"{x}{j}" for j in range(4) for x in ("table_turn", "table_turned")]
    + [f"{x}{j}" for j in range(4) for x in ("table", "table_out")]
    + ["part1", "rest1", "part2", "rest2", "part3"]
    + [f"{w}_{x}" for w in ("wq", "wkv", "wp", "fk", "fv", "fc1", "fc2", "fg", "hl") for x in ("turn", "out")]
    + ["bd1", "bdr1", "bd2", "bdr2", "bd3", "bd_rows"]
    + [f"{x}{h}" for h in range(HEADS) for x in ("av_turn", "av_out")]
    + ["avo", "avo_out", "max_q", "max_k", "max_v", "max_all", "max_least", "max_inverse", "span",
       "escale", "escale2", "vscale", "norm_q", "norm_k", "norm_v", "hi_q", "hi_k", "hi_v", "lo_q", "lo_k", "lo_v"]
    + [f"{x}{n}" for n in range(NH) for x in ("fq_turn", "fq_out")]
    + [f"{x}{n}" for n in range(NH) for x in ("gq", "gq_a", "gq_b", "gq_c", "gk", "gk_a", "gk_b", "gk_c", "gk_one", "gv", "gv_out")]
)


def prepare(k, nc):
    step = k.sem("step")
    ps = k.bank

    def at(eng, name):
        i = PREPARE.index(name)
        if i:
            eng.wait_ge(step, i)

    with nc.Block() as block:
        @block.tensor
        def _(pe):
            def mm(name, out, lhsT, rhs):
                at(pe, name)
                pe.matmul(out, lhsT=lhsT, rhs=rhs, start=True, stop=True).then_inc(step, 1)

            def turn(name, out, in_):
                at(pe, name)
                n = in_.shape[0]
                pe.transpose(out, in_, k.ident[0:n, 0:n]).then_inc(step, 1)

            mm("abs_all", ps[0][0:C, 0:1], k.ones[0:C, 0:C], k.wcol[:, 0:1])
            turn("weff_turn", ps[0][0:VR, 0:C], k.wtmp[:, 3])
            for j in range(4):
                turn(f"table_turn{j}", ps[0][0:VR, 0:P], k.eblk[:, j])
            for j in range(4):
                mm(f"table{j}", ps[0][:, 0:C], k.eblkT[:, j], k.weffT[:])
            turn("wq_turn", ps[0][0:C, 0:C], k.wqn[:])
            turn("wkv_turn", ps[0][0:C, 0:2 * C], k.wkvn[:])
            turn("wp_turn", ps[0][0:C, 0:C], k.wpn[:])
            turn("fk_turn", ps[0][0:D, 0:C], k.fk[:])
            turn("fv_turn", ps[0][0:D, 0:C], k.fv[:])
            turn("fc1_turn", ps[0][0:C, 0:C], k.fc[:, 0])
            turn("fc2_turn", ps[0][0:C, 0:C], k.fc[:, 1])
            turn("fg_turn", ps[0][0:C, 0:NH], k.fgn[:])
            turn("hl_turn", ps[0][0:C + 1, 0:C], k.hln[:])
            for h in range(HEADS):
                turn(f"av_turn{h}", ps[0][0:C, 0:C], k.av[:, h * C:(h + 1) * C])
            at(pe, "avo")
            for h in range(HEADS):
                mm_ = pe.matmul(ps[0][:, h * C:(h + 1) * C], lhsT=k.avT[:, h].rearrange("c a i -> c (a i)"),
                                rhs=k.ao[:, h], start=True, stop=True)
            mm_.then_inc(step, 1)
            for n in range(NH):
                turn(f"fq_turn{n}", ps[0][0:D, 0:C], k.fq[:, n])
            for n in range(NH):
                mm(f"gq{n}", ps[0][0:C + 1, 0:C], k.hld[:, n], k.fqT[:, n])
                mm(f"gk{n}", ps[0][0:C + 1, 0:D], k.hld[:, n], k.fkT[:, n * D:(n + 1) * D])
                mm(f"gv{n}", ps[0][0:C + 1, 0:D], k.hld[:, n], k.fvT[:, n * D:(n + 1) * D])

        @block.gpsimd
        def _(pool):
            at(pool, "max_all")
            pool.partition_all_reduce(k.amaxr[:], k.amax[:], P, bass.bass_isa.ReduceOp.max).then_inc(step, 1)

        @block.sync
        def _(sp):
            at(sp, "bd_rows")
            sp.dma_start(k.bd3[:], k.bds[0:1]).then_inc(k.loaded, 16)
            sp.wait_ge(k.loaded, k.n_loads + 16)
            sp.sem_inc(step, 1)

        @block.vector
        def _(dve):
            def ts(name, out, in0, s1, s2, op0, op1=ALU.bypass):
                at(dve, name)
                dve.tensor_scalar(out, in0, s1, s2, op0, op1).then_inc(step, 1)

            def tt(name, out, in0, in1, op):
                at(dve, name)
                dve.tensor_tensor(out, in0, in1, op).then_inc(step, 1)

            def copy(name, out, in_):
                at(dve, name)
                dve.tensor_copy(out, in_).then_inc(step, 1)

            def biggest(name, out, in_):
                at(dve, name)
                dve.tensor_reduce(out, in_, X, ALU.max, apply_absolute_value=True).then_inc(step, 1)

            w, t, col = k.w[:], k.wtmp, k.wcol
            at(dve, "abs_sum")
            dve.tensor_reduce(col[:, 0:1], w, X, ALU.add, apply_absolute_value=True).then_inc(step, 1)
            ts("scale", col[:, 1:2], ps[0][0:C, 0:1], 1.0 / (C * VR), None, ALU.mult)
            ts("scale_eps", col[:, 2:3], col[:, 1:2], EPS_W, None, ALU.add)
            at(dve, "inverse")
            dve.reciprocal(col[:, 3:4], col[:, 2:3]).then_inc(step, 1)
            ts("ratio", t[:, 0], w, col[:, 3:4], None, ALU.mult)
            ts("above", t[:, 1], t[:, 0], 0.5, None, ALU.is_gt)
            ts("below", t[:, 2], t[:, 0], -0.5, None, ALU.is_lt)
            tt("sign", t[:, 1], t[:, 1], t[:, 2], ALU.subtract)
            ts("ternary", t[:, 1], t[:, 1], col[:, 1:2], None, ALU.mult)
            tt("delta", t[:, 2], t[:, 1], w, ALU.subtract)
            tt("weff", t[:, 3], w, t[:, 2], ALU.add)
            copy("weff_out", k.weffT[:], ps[0][0:VR, 0:C])
            for j in range(4):
                copy(f"table_turned{j}", k.eblkT[:, j], ps[0][0:VR, 0:P])
            for j in range(4):
                copy(f"table_out{j}", k.tab[:, j], ps[0][:, 0:C])
            copy("part1", k.tab3[:, :, 0], k.tab[:])
            tt("rest1", k.tabr[:], k.tab[:], k.tab3[:, :, 0], ALU.subtract)
            copy("part2", k.tab3[:, :, 1], k.tabr[:])
            tt("rest2", k.tab[:], k.tabr[:], k.tab3[:, :, 1], ALU.subtract)
            copy("part3", k.tab3[:, :, 2], k.tab[:])
            copy("wq_out", k.wqT[:], ps[0][0:C, 0:C])
            copy("wkv_out", k.wkvT[:], ps[0][0:C, 0:2 * C])
            copy("wp_out", k.wpT[:], ps[0][0:C, 0:C])
            copy("fk_out", k.fkT[:], ps[0][0:D, 0:C])
            copy("fv_out", k.fvT[:], ps[0][0:D, 0:C])
            copy("fc1_out", k.fcT[:, 0], ps[0][0:C, 0:C])
            copy("fc2_out", k.fcT[:, 1], ps[0][0:C, 0:C])
            copy("fg_out", k.fgT[:], ps[0][0:C, 0:NH])
            copy("hl_out", k.gsv[:, 0:C], ps[0][0:C + 1, 0:C])
            copy("bd1", k.bds[:, 0], k.bd1[:])
            tt("bdr1", k.bdr[:], k.bd1[:], k.bds[:, 0], ALU.subtract)
            copy("bd2", k.bds[:, 1], k.bdr[:])
            tt("bdr2", k.bd1[:], k.bdr[:], k.bds[:, 1], ALU.subtract)
            copy("bd3", k.bds[:, 2], k.bd1[:])
            for h in range(HEADS):
                copy(f"av_out{h}", k.avT[:, h], ps[0][0:C, 0:C].unsqueeze(1).to_broadcast([C, 2, C]))
            copy("avo_out", k.avo[:], ps[0][:, :])
            biggest("max_q", k.amax[:, 0:1], k.aq[:, 0])
            biggest("max_k", k.amax[:, 1:2], k.aq[:, 1])
            biggest("max_v", k.amax[:, 2:3], k.avo[:])
            ts("max_least", k.amax[:], k.amaxr[:], 1e-30, None, ALU.max)
            at(dve, "max_inverse")
            dve.reciprocal(k.ainv[:], k.amax[:]).then_inc(step, 1)
            ts("span", k.ainv[:], k.ainv[:], WSPAN, None, ALU.mult)
            ts("escale", k.escale[:], k.amax[:, 0:1], 1.0 / (WSPAN * WSPAN * float(np.sqrt(C / HEADS))), None, ALU.mult)
            tt("escale2", k.escale[:], k.escale[:], k.amax[:, 1:2], ALU.mult)
            ts("vscale", k.vscale[:], k.amax[:, 2:3], 1.0 / WSPAN, None, ALU.mult)
            ts("norm_q", k.an[:, 0], k.aq[:, 0], k.ainv[:, 0:1], None, ALU.mult)
            ts("norm_k", k.an[:, 1], k.aq[:, 1], k.ainv[:, 1:2], None, ALU.mult)
            ts("norm_v", k.an[:, 2], k.avo[:], k.ainv[:, 2:3], None, ALU.mult)
            twice = [k.an[:, j].rearrange("p (h c) -> p h c", h=HEADS).unsqueeze(2).to_broadcast([P, HEADS, 2, C])
                     for j in range(2)]
            copy("hi_q", k.wqk_hi[:, 0], twice[0])
            copy("hi_k", k.wqk_hi[:, 1], twice[1])
            copy("hi_v", k.wvo_hi[:], k.an[:, 2])
            tt("lo_q", k.wqk_lo[:, 0], twice[0], k.wqk_hi[:, 0], ALU.subtract)
            tt("lo_k", k.wqk_lo[:, 1], twice[1], k.wqk_hi[:, 1], ALU.subtract)
            tt("lo_v", k.wvo_lo[:], k.an[:, 2], k.wvo_hi[:], ALU.subtract)
            for n in range(NH):
                copy(f"fq_out{n}", k.fqT[:, n], ps[0][0:D, 0:C])
            for n in range(NH):
                q = ps[0][0:C + 1, 0:C].rearrange("p (e o) -> p e o", e=NE)
                for x, s0, s1 in (("a", 0, 2), ("b", 3, 6), ("c", 7, 8)):
                    copy(f"gq_{x}{n}", k.gq[:, n, :, s0:s1], q.unsqueeze(2).to_broadcast([C + 1, NE, s1 - s0, D]))
                kk = ps[0][0:C + 1, 0:D]
                for x, s0, s1 in (("a", 0, 2), ("b", 3, 6), ("c", 7, 8)):
                    copy(f"gk_{x}{n}", k.gk[:, n, s0:s1], kk.unsqueeze(1).to_broadcast([C + 1, s1 - s0, D]))
                at(dve, f"gk_one{n}")
                dve.memset(k.gk[C:C + 1, n, 2, 0:2], 1.0).then_inc(step, 1)
                copy(f"gv_out{n}", k.gsv[:, C + n * D:C + (n + 1) * D], kk)


class Chain:

    def __init__(self, eng, sem, turn, steps):
        self.eng, self.sem, self.base, self.steps, self.n = eng, sem, turn * steps, steps, 0

    def __call__(self, ins):
        self.n += 1
        ins.then_inc(self.sem, 1)
        self.eng.wait_ge(self.sem, self.base + self.n)

    def mark(self, ins):
        self.n += 1
        ins.then_inc(self.sem, 1)

    def settle(self):
        self.eng.wait_ge(self.sem, self.base + self.n)

    def fill(self, eng):
        if self.n < self.steps:
            eng.sem_inc(self.sem, self.steps - self.n)

    def end(self):
        assert self.n == self.steps, (self.n, self.steps)


def passed(eng, seen, sem, value):
    eng.wait_ge(sem, value)
    eng.sem_inc(seen, 1)


def wide(ap, n):
    return ap.unsqueeze(2).to_broadcast([ap.shape[0], ap.shape[1], n])


def rows(ap, n):
    return ap.unsqueeze(1).to_broadcast([ap.shape[0], n, ap.shape[1]])


def normalize(dve, link, x, out, xc, sq, st, size, var_ready, std_ready, turn):
    link(dve.tensor_reduce(st[:, 0], x, X, ALU.add))
    link(dve.tensor_scalar(st[:, 0], st[:, 0], 1.0 / size, None, ALU.mult))
    link(dve.tensor_tensor(xc, x, wide(st[:, 0], size), ALU.subtract))
    link(dve.tensor_tensor(sq, xc, xc, ALU.mult))
    dve.tensor_reduce(st[:, 1], sq, X, ALU.add).then_inc(var_ready, 1)
    dve.wait_ge(std_ready, turn + 1)
    link(dve.reciprocal(st[:, 3], st[:, 2]))
    link(dve.tensor_tensor(out, xc, wide(st[:, 3], size), ALU.mult))


def root(act, st, eps, size, var_ready, std_ready, turn):
    act.wait_ge(var_ready, turn + 1)
    act.activation(st[:, 2], st[:, 1], ACT.Sqrt, bias=eps, scale=1.0 / size).then_inc(std_ready, 1)


def layer0(k, nc, a):
    NB = k.NB
    ps = k.bank
    with ExitStack() as ctx:
        def sb(name, shape, dt):
            return ctx.enter_context(nc.sbuf_tensor(name, shape, dt))

        ids = sb("ids", [6, S], I32)
        idsb = sb("idsb", [6, 2, S], BF16)
        onehot = sb("onehot", [P, 2, 4, HALF], BF16)
        x = sb("l0_x", [P, 2, T, C], F32)
        xc = sb("l0_xc", [P, 2, T, C], F32)
        sq = sb("l0_sq", [P, 2, T, C], F32)
        xn = sb("l0_xn", [P, 2, T, 2, C], F32)
        st = sb("l0_st", [P, 2, 4, T], F32)
        xT = sb("l0_xT", [C, 2, S], F32)
        qT = sb("l0_qT", [C, 2, S], F32)
        low = sb("l0_low", [P, 2, S], F32)
        kf = sb("l0_kf", [P, 2, T, C], F32)
        vx = sb("l0_vx", [P, 2, T, C + 1], F32)
        cx = sb("l0_cx", [C, 2, C + HEADS], F32)
        inv = sb("l0_inv", [P, 2, T, HEADS], F32)
        aT = qT
        hT = sb("l0_hT", [P, 2, 2, S], F32)
        lg = sb("l0_lg", [P, 2, T, EXPERTS], F32)
        eg = sb("l0_eg", [P, 2, T, EXPERTS], F32)
        g1 = sb("l0_g1", [P, 2, 4, T], F32)
        wsel = sb("l0_wsel", [P, 2, T, EXPERTS], F32)
        yw = sb("l0_yw", [P, 2, EXPERTS, C], F32)
        none = sb("l0_none", [P, 1], F32)

        s = Parts()
        s.done = k.sem("l0_done")
        s.ids_in = k.sem("l0_ids_in")
        s.ids_cast = k.sem("l0_ids_cast")
        s.idx_ready = k.sem("l0_idx_ready")
        s.onehot_ready = k.sem("l0_onehot_ready")
        s.z_ready = k.sem("l0_z_ready")
        s.z_taken = k.sem("l0_z_taken")
        s.d = k.sem("l0_d")
        s.p = k.sem("l0_p")
        s.h_ready = k.sem("l0_h_ready")
        s.h2_ready = k.sem("l0_h2_ready")
        s.h3_ready = k.sem("l0_h3_ready")
        s.turn_a = k.sem("l0_turn_a")
        s.xT_ready = k.sem("l0_xT_ready")
        s.q_ready = k.sem("l0_q_ready")
        s.kv_ready = k.sem("l0_kv_ready")
        s.qlow = k.sem("l0_qlow")
        s.qexp = k.sem("l0_qexp")
        s.klow = k.sem("l0_klow")
        s.kexp = k.sem("l0_kexp")
        s.q_done = k.sem("l0_q_done")
        s.kv_done = k.sem("l0_kv_done")
        s.ctx_ready = k.sem("l0_ctx_ready")
        s.ctx_done = k.sem("l0_ctx_done")
        s.num_ready = k.sem("l0_num_ready")
        s.aT_done = k.sem("l0_aT_done")
        s.a_ready = k.sem("l0_a_ready")
        s.turn_v = k.sem("l0_turn_v")
        s.ahead = k.sem("l0_ahead")
        s.proj_ready = k.sem("l0_proj_ready")
        s.turn_f = k.sem("l0_turn_f")
        s.xT_f = k.sem("l0_xT_f")
        s.hid_ready = k.sem("l0_hid_ready")
        s.gelu_done = k.sem("l0_gelu_done")
        s.gate_ready = k.sem("l0_gate_ready")
        s.lg_ready = k.sem("l0_lg_ready")
        s.eg_ready = k.sem("l0_eg_ready")
        s.y_ready = k.sem("l0_y_ready")
        s.y_taken = k.sem("l0_y_taken")
        s.turn_p = k.sem("l0_turn_p")
        s.hi_done = k.sem("l0_hi_done")
        var = [k.sem(f"l0_var{j}") for j in range(4)]
        std = [k.sem(f"l0_std{j}") for j in range(4)]
        DVE_STEPS = 126
        assert NB % 2 == 0

        with nc.Block() as block:
            @block.sync
            def _(sp):
                with sp.Fori(0, NB) as n:
                    sp.wait_ge(s.ids_cast, n + 1)
                    for j, name in enumerate(k.id_names):
                        sp.dma_start(ids[j:j + 1, :], k.ids[name][ds(n, 1), :]).then_inc(s.ids_in, 16)

            @block.gpsimd
            def _(pool):
                pool.memset(vx[:, :, :, C:C + 1], 1.0).then_inc(s.p, 1)
                pool.sem_inc(s.ids_cast, 1)
                with pool.Fori(0, NB // 2) as i:
                    for j in range(2):
                        passed(pool, k.seen, s.ids_in, (i * 2 + j) * 96 + 96)
                        passed(pool, k.seen, s.idx_ready, i * 16 + 1)
                        pool.tensor_copy(idsb[:, j], ids[:]).then_inc(s.ids_cast, 1)

            @block.scalar
            def _(act):
                with act.Fori(0, NB // 2) as i:
                    ahead = Chain(act, s.ahead, i, 5)

                    def table(function):
                        ahead(act.activation(none[:], k.ones[:, 0:1], function))

                    def banks_out(j, first, dst, ready, sig):
                        act.wait_ge(ready, i * 2 + j + 1)
                        for half in range(2):
                            act.activation(dst[:, j, half * HALF:(half + 1) * HALF], ps[4 * j + first + half][0:C, :],
                                           ACT.Copy).then_inc(sig, 1)

                    for j in range(2):
                        for m in range(2):
                            root(act, st[:, j], k.eps_ln[:], C, var[m], std[m], i * 2 + j)
                        banks_out(j, 0, xT, s.turn_a, s.xT_ready)
                    table(ACT.Exp)
                    for j in range(2):
                        act.wait_ge(s.qlow, i * 2 + j + 1)
                        act.activation(low[0:C, j, :], low[0:C, j, :], ACT.Exp).then_inc(s.qexp, 1)
                    for j in range(2):
                        act.wait_ge(s.klow, i * 2 + j + 1)
                        act.activation(low[:, j, 0:HALF], low[:, j, 0:HALF], ACT.Exp).then_inc(s.kexp, 1)
                    table(ACT.Sqrt)
                    for j in range(2):
                        banks_out(j, 2, aT, s.turn_v, s.aT_done)
                    for j in range(2):
                        root(act, st[:, j], k.eps_ln[:], C, var[2], std[2], i * 2 + j)
                        banks_out(j, 2, xT, s.turn_f, s.xT_f)
                    table(ACT.Gelu)
                    for j in range(2):
                        for c in range(2):
                            for half in range(2):
                                act.wait_ge(s.hid_ready, (i * 2 + j) * 4 + 2 * c + half + 1)
                                act.activation(hT[:, j, c, half * HALF:(half + 1) * HALF], ps[4 * j + 2 * c + half],
                                               ACT.Gelu, bias=k.b1[:, c:c + 1]).then_inc(s.gelu_done, 1)
                    table(ACT.Exp)
                    for j in range(2):
                        act.wait_ge(s.lg_ready, i * 2 + j + 1)
                        act.activation(eg[:, j], lg[:, j], ACT.Exp).then_inc(s.eg_ready, 1)
                    table(ACT.Sqrt)
                    for j in range(2):
                        root(act, st[:, j], k.eps_ln[:], C, var[3], std[3], i * 2 + j)
                    for j in range(2):
                        act.wait_ge(s.turn_p, i * 2 + j + 1)
                        for half in range(2):
                            act.activation(k.xa[:, ds((i * 2 + j) * S + half * HALF, HALF)], ps[4 * j + half], ACT.Copy)\
                               .then_inc(s.hi_done, 1)

            @block.tensor
            def _(pe):
                def turn_tokens(j, first, m, done):
                    for t in range(T):
                        src = xn[:, j, t, 0] if m == C else xn[:, j, t].rearrange("p a c -> p (a c)")
                        last = pe.transpose(ps[4 * j + first + t // 4][0:m, (t % 4) * P:(t % 4 + 1) * P], src, k.ident[:])
                    last.then_inc(done, 1)

                pe.sem_inc(s.idx_ready, 1)
                with pe.Fori(0, NB // 2) as i:
                    for half in range(2):
                        for j in range(2):
                            if half == 0:
                                pe.wait_ge(s.ids_cast, i * 2 + j + 2)
                                pe.wait_ge(s.done, i * 2 + j + 1)
                            else:
                                pe.wait_ge(s.z_taken, i * 2 + j + 1)
                            for c in range(4):
                                pe.matmul(ps[4 * j + c], lhsT=k.sel[:, 2 * c:2 * c + 2].rearrange("t a p -> t (a p)"),
                                          rhs=idsb[:, j, half * HALF:(half + 1) * HALF], start=True, stop=True)\
                                  .then_inc(s.idx_ready, 1)
                        for j in range(2):
                            pe.wait_ge(s.onehot_ready, i * 16 + half * 8 + j * 4 + 4)
                            for t in range(4):
                                for c in range(4):
                                    for r in range(3):
                                        last = pe.matmul(ps[4 * j][:, t * C:(t + 1) * C],
                                                         lhsT=onehot[:, j, c, t * P:(t + 1) * P],
                                                         rhs=k.tab3[:, c, r], start=(t == 0 and c == 0 and r == 0),
                                                         stop=(c == 3 and r == 2), skip_group_check=True)
                            last.then_inc(s.z_ready, 1)
                    for j in range(2):
                        passed(pe, k.seen, s.h_ready, i * 2 + j + 1)
                        turn_tokens(j, 0, C, s.turn_a)
                        passed(pe, k.seen, s.xT_ready, (i * 2 + j) * 2 + 2)
                        for half in range(2):
                            last = pe.matmul(ps[4 * j + 2 + half][0:C, :], lhsT=k.wqT[:],
                                             rhs=xT[:, j, half * HALF:(half + 1) * HALF], start=True, stop=True)
                        last.then_inc(s.q_ready, 1)
                        for t in range(T):
                            last = pe.matmul(ps[4 * j + t // 4][:, (t % 4) * P:(t % 4 + 1) * P],
                                             lhsT=xT[:, j, t * P:(t + 1) * P], rhs=k.wkvT[:], start=True, stop=True)
                        last.then_inc(s.kv_ready, 1)
                    pe.wait_ge(s.p, 1)
                    for j in range(2):
                        pe.wait_ge(s.q_done, i * 2 + j + 1)
                        passed(pe, k.seen, s.kv_done, i * 2 + j + 1)
                        for t in range(T):
                            last = pe.matmul(ps[4 * j + 2][0:C, 0:C + 1], lhsT=kf[:, j, t], rhs=vx[:, j, t],
                                             start=(t == 0), stop=(t == T - 1))
                        last.then_inc(s.ctx_ready, 1)
                    for j in range(2):
                        passed(pe, k.seen, s.ctx_done, i * 2 + j + 1)
                        for t in range(T):
                            last = pe.matmul(ps[4 * j + t // 4][:, (t % 4) * P:(t % 4) * P + C + HEADS],
                                             lhsT=qT[:, j, t * P:(t + 1) * P], rhs=cx[:, j], start=(t % 4 == 0), stop=True,
                                             skip_group_check=True)
                        last.then_inc(s.num_ready, 1)
                    for j in range(2):
                        passed(pe, k.seen, s.a_ready, i * 2 + j + 1)
                        turn_tokens(j, 2, C, s.turn_v)
                    for j in range(2):
                        passed(pe, k.seen, s.aT_done, (i * 2 + j) * 2 + 2)
                        for t in range(T):
                            last = pe.matmul(ps[4 * j][:, t * C:(t + 1) * C], lhsT=aT[:, j, t * P:(t + 1) * P], rhs=k.wpT[:],
                                             start=True, stop=True)
                        last.then_inc(s.proj_ready, 1)
                    for j in range(2):
                        passed(pe, k.seen, s.h2_ready, i * 2 + j + 1)
                        turn_tokens(j, 2, C, s.turn_f)
                        passed(pe, k.seen, s.xT_f, (i * 2 + j) * 2 + 2)
                        for c in range(2):
                            for half in range(2):
                                pe.matmul(ps[4 * j + 2 * c + half], lhsT=k.w1[:, c * P:(c + 1) * P],
                                          rhs=xT[:, j, half * HALF:(half + 1) * HALF], start=True, stop=True)\
                                  .then_inc(s.hid_ready, 1)
                    for j in range(2):
                        passed(pe, k.seen, s.gelu_done, (i * 2 + j) * 4 + 4)
                        for t in range(T):
                            for c in range(2):
                                last = pe.matmul(ps[4 * j][:, t * EXPERTS:(t + 1) * EXPERTS],
                                                 lhsT=hT[:, j, c, t * P:(t + 1) * P], rhs=k.wg[:, c],
                                                 start=(c == 0 and t == 0), stop=(c == 1), skip_group_check=True)
                        last.then_inc(s.gate_ready, 1)
                    for j in range(2):
                        for t in range(T):
                            bank = ps[4 * j + 1 + t % 3]
                            if t >= 3:
                                passed(pe, k.seen, s.y_taken, (i * 2 + j) * T + t - 2)
                            for c in range(2):
                                pe.matmul(bank, lhsT=hT[:, j, c, t * P:(t + 1) * P],
                                          rhs=k.wd[:, c].rearrange("p e c -> p (e c)"), start=(c == 0), stop=False)
                            pe.matmul(bank, lhsT=k.onesb[0:3, :], rhs=k.bd3[:], start=False, stop=True).then_inc(s.y_ready, 1)
                    for j in range(2):
                        passed(pe, k.seen, s.h3_ready, i * 2 + j + 1)
                        turn_tokens(j, 0, P, s.turn_p)

            @block.vector
            def _(dve):
                dve.sem_inc(s.done, 2)
                with dve.Fori(0, NB // 2) as i:
                    link = Chain(dve, s.d, i, DVE_STEPS)
                    for half in range(2):
                        for j in range(2):
                            for c in range(4):
                                dve.wait_ge(s.idx_ready, i * 16 + half * 8 + j * 4 + c + 2)
                                dve.tensor_scalar(onehot[:, j, c], ps[4 * j + c], k.vcol[:, c:c + 1], None, ALU.is_equal)\
                                   .then_inc(s.onehot_ready, 1)
                        for j in range(2):
                            dve.wait_ge(s.z_ready, i * 4 + half * 2 + j + 1)
                            link(dve.tensor_tensor(x[:, j, 4 * half:4 * half + 4],
                                                   ps[4 * j][:, 0:4 * C].rearrange("p (t c) -> p t c", t=4),
                                                   rows(k.tok_b[:], 4), ALU.add))
                            if half == 0:
                                dve.sem_inc(s.z_taken, 1)
                    for j in range(2):
                        normalize(dve, link, x[:, j], x[:, j], xc[:, j], sq[:, j], st[:, j], C, var[0], std[0], i * 2 + j)
                        link(dve.tensor_tensor(x[:, j], x[:, j], rows(k.tok_g[:], T), ALU.mult))
                        link(dve.tensor_tensor(x[:, j], x[:, j], rows(k.tok_beta[:], T), ALU.add))
                        normalize(dve, link, x[:, j], xn[:, j, :, 0], xc[:, j], sq[:, j], st[:, j], C, var[1], std[1], i * 2 + j)
                        dve.sem_inc(s.h_ready, 1)
                    kv = [[ps[4 * j + a].rearrange("p (t x) -> p t x", t=4) for a in range(2)] for j in range(2)]
                    low_k = [low[:, j, 0:HALF].rearrange("p (t c) -> p t c", t=T) for j in range(2)]
                    for j in range(2):
                        dve.wait_ge(s.q_ready, i * 2 + j + 1)
                        link(dve.tensor_scalar(low[0:C, j, 0:HALF], ps[4 * j + 2][0:C, :], 0.0, None, ALU.min))
                        dve.tensor_scalar(low[0:C, j, HALF:S], ps[4 * j + 3][0:C, :], 0.0, None, ALU.min).then_inc(s.qlow, 1)
                    for j in range(2):
                        dve.wait_ge(s.qexp, i * 2 + j + 1)
                        link(dve.scalar_tensor_tensor(qT[:, j, 0:HALF], ps[4 * j + 2][0:C, :], 0.0, low[0:C, j, 0:HALF],
                                                      ALU.max, ALU.add))
                        dve.scalar_tensor_tensor(qT[:, j, HALF:S], ps[4 * j + 3][0:C, :], 0.0, low[0:C, j, HALF:S],
                                                 ALU.max, ALU.add).then_inc(s.q_done, 1)
                        dve.wait_ge(s.q_done, i * 2 + j + 1)
                        dve.wait_ge(s.kv_ready, i * 2 + j + 1)
                        link(dve.tensor_scalar(low_k[j][:, 0:4], kv[j][0][:, :, 0:C], 0.0, None, ALU.min))
                        dve.tensor_scalar(low_k[j][:, 4:8], kv[j][1][:, :, 0:C], 0.0, None, ALU.min).then_inc(s.klow, 1)
                        link(dve.tensor_copy(vx[:, j, 0:4, 0:C], kv[j][0][:, :, C:2 * C]))
                        link(dve.tensor_copy(vx[:, j, 4:8, 0:C], kv[j][1][:, :, C:2 * C]))
                    for j in range(2):
                        dve.wait_ge(s.kexp, i * 2 + j + 1)
                        link(dve.scalar_tensor_tensor(kf[:, j, 0:4], kv[j][0][:, :, 0:C], 0.0, low_k[j][:, 0:4], ALU.max, ALU.add))
                        dve.scalar_tensor_tensor(kf[:, j, 4:8], kv[j][1][:, :, 0:C], 0.0, low_k[j][:, 4:8], ALU.max, ALU.add)\
                           .then_inc(s.kv_done, 1)
                        link(dve.tensor_tensor(x[:, j], x[:, j], rows(k.bproj[:], T), ALU.add))
                    for j in range(2):
                        dve.wait_ge(s.ctx_ready, i * 2 + j + 1)
                        ctx_bank = ps[4 * j + 2]
                        link(dve.tensor_tensor(cx[:, j, 0:C], ctx_bank[0:C, 0:C], k.blk8[:], ALU.mult))
                        dve.tensor_scalar(cx[:, j, C:], k.blk8[:].rearrange("p (h d) -> p h d", h=HEADS)[:, :, 0],
                                          ctx_bank[0:C, C:C + 1], None, ALU.mult).then_inc(s.ctx_done, 1)
                    for j in range(2):
                        dve.wait_ge(s.num_ready, i * 2 + j + 1)
                        qc = k.psum[:, 4 * j:4 * j + 2].rearrange("p a (t x) -> p (a t) x", t=4)
                        link(dve.tensor_scalar(inv[:, j], qc[:, :, C:C + HEADS], 1e-6, None, ALU.max))
                        link(dve.reciprocal(inv[:, j], inv[:, j]))
                        link(dve.tensor_tensor(xn[:, j, :, 0].rearrange("p t (h d) -> p t h d", h=HEADS),
                                               qc[:, :, 0:C].rearrange("p t (h d) -> p t h d", h=HEADS),
                                               inv[:, j].unsqueeze(3).to_broadcast([P, T, HEADS, C // HEADS]), ALU.mult))
                        dve.sem_inc(s.a_ready, 1)
                    for j in range(2):
                        dve.wait_ge(s.proj_ready, i * 2 + j + 1)
                        link(dve.tensor_tensor(x[:, j], x[:, j], ps[4 * j].rearrange("p (t c) -> p t c", t=T), ALU.add))
                        normalize(dve, link, x[:, j], xn[:, j, :, 0], xc[:, j], sq[:, j], st[:, j], C, var[2], std[2], i * 2 + j)
                        dve.sem_inc(s.h2_ready, 1)
                    for j in range(2):
                        w, l, e, g = wsel[:, j], lg[:, j], eg[:, j], g1[:, j]
                        dve.wait_ge(s.gate_ready, i * 2 + j + 1)
                        link(dve.tensor_tensor(l, ps[4 * j][:, 0:T * EXPERTS].rearrange("p (t e) -> p t e", t=T),
                                               rows(k.bg[:], T), ALU.add))
                        link(dve.tensor_reduce(g[:, 0], l, X, ALU.max))
                        link(dve.tensor_tensor(w, l, wide(g[:, 0], EXPERTS), ALU.is_equal))
                        dve.tensor_tensor(l, l, wide(g[:, 0], EXPERTS), ALU.subtract).then_inc(s.lg_ready, 1)
                        link(dve.tensor_tensor(w, w, rows(k.rank[:], T), ALU.mult))
                        link(dve.tensor_reduce(g[:, 1], w, X, ALU.max))
                        link(dve.tensor_tensor(w, w, wide(g[:, 1], EXPERTS), ALU.is_equal))
                        dve.wait_ge(s.eg_ready, i * 2 + j + 1)
                        link(dve.tensor_reduce(g[:, 2], e, X, ALU.add))
                        link(dve.reciprocal(g[:, 3], g[:, 2]))
                        link(dve.tensor_tensor(e, e, wide(g[:, 3], EXPERTS), ALU.mult))
                        link(dve.tensor_tensor(w, w, e, ALU.mult))
                    for j in range(2):
                        for t in range(T):
                            dve.wait_ge(s.y_ready, (i * 2 + j) * T + t + 1)
                            dve.tensor_tensor(yw[:, t % 2], ps[4 * j + 1 + t % 3].rearrange("p (e c) -> p e c", e=EXPERTS),
                                              wide(wsel[:, j, t], C), ALU.mult).then_inc(s.y_taken, 1)
                            dve.wait_ge(s.y_taken, (i * 2 + j) * T + t + 1)
                            link(dve.tensor_reduce(sq[:, j, t], yw[:, t % 2].rearrange("p e c -> p c e"), X, ALU.add))
                        link(dve.tensor_tensor(x[:, j], x[:, j], sq[:, j], ALU.add))
                        normalize(dve, link, x[:, j], xn[:, j, :, 0], xc[:, j], sq[:, j], st[:, j], C, var[3], std[3], i * 2 + j)
                        link(dve.tensor_copy(xn[:, j, :, 1], xn[:, j, :, 0]))
                        dve.sem_inc(s.h3_ready, 1)
                        link(dve.tensor_tensor(k.h[:, ds((i * 2 + j) * T, T), :], x[:, j], rows(k.bout[:], T), ALU.add))
                    for j in range(2):
                        dve.wait_ge(s.hi_done, (i * 2 + j) * 2 + 2)
                        for half in range(2):
                            low_half = k.xa[C:P, ds((i * 2 + j) * S + half * HALF, HALF)]
                            link(dve.tensor_tensor(low_half, ps[4 * j + half][C:P, :], low_half, ALU.subtract))
                        dve.sem_inc(s.done, 1)
                    link.end()


A_TASKS = (
    (("q", 0), ("q", 1)),
    (("k", 0), ("k", 1), ("v", 0)),
    (("den", 0),) + tuple(("max", u) for u in range(3)),
    (("out", 0),) + tuple(("max", u) for u in range(3, 6)),
    tuple(("max", u) for u in range(6, 10)),
    tuple(("max", u) for u in range(10, 13)),
    tuple(("max", u) for u in range(13, 16)),
    (("row", 0),),
)
A_LIST = [t for slot in A_TASKS for t in slot]
A_N = len(A_LIST)
A_BANKS = (4, 5, 7)
NEXT = ("q", "k", "v", "max", "row")
NPB = 4


def attention1(k, nc):
    heads = k.NB * HEADS
    ps = k.bank
    assert A_N % len(A_BANKS) == 0
    with ExitStack() as ctx:
        def sb(name, shape, dt):
            return ctx.enter_context(nc.sbuf_tensor(name, shape, dt))

        qa = sb("a1_qa", [P, 2, S], FP16)
        qb = sb("a1_qb", [C + 2, 2, S], FP16)
        ka = sb("a1_ka", [P, 2, S], FP16)
        kb = sb("a1_kb", [C + 2, 2, S], FP16)
        v = sb("a1_v", [P, 2, T, C], F32)
        prob = sb("a1_prob", [P, NPB, S], F32)
        total = sb("a1_total", [P, 2, S], F32)
        un = sb("a1_un", [P, 2, HALF], F32)
        inv = sb("a1_inv", [P, T], F32)
        u = sb("a1_u", [P, T, C], F32)
        mp = sb("a1_mp", [P, T, 2], F32)
        mx = sb("a1_mx", [P, 2, T], F32)
        mm = sb("a1_mm", [P, T, 2], FP16)

        s = Parts()
        s.scores = k.sem("a1_scores")
        s.exp = k.sem("a1_exp")
        s.pv = k.sem("a1_pv")
        s.added = k.sem("a1_added")
        s.task = k.sem("a1_task")
        s.taken = k.sem("a1_taken")
        s.split = k.sem("a1_split")
        s.copied = k.sem("a1_copied")
        s.maxima = k.sem("a1_maxima")
        s.d = k.sem("a1_d")
        s.start = k.sem("a1_start")
        D_STEPS = 8
        TAKEN = {t: j for j, t in enumerate(A_LIST)}

        def listed(slot):
            j = sum(len(x) for x in A_TASKS[:slot])
            return [(j + i, *t) for i, t in enumerate(A_TASKS[slot])]

        def wanted(kind, g, first, last):
            return not last if kind in NEXT else not first

        def pairs(eng, head, prologue):
            prologue()
            head(0, 0, True, False)
            head(1, 1, False, False)
            with eng.Fori(1, heads // 2 - 1) as i:
                head(0, i * 2, False, False)
                head(1, i * 2 + 1, False, False)
            head(0, heads - 2, False, False)
            head(1, heads - 1, False, True)

        with nc.Block() as block:
            @block.gpsimd
            def _(pool):
                def head(par, g, first, last):
                    pool.wait_ge(s.task, A_N * g + TAKEN["den", 0] + 1)
                    for kt in range(1, T):
                        pool.wait_ge(s.exp, T * g + kt + 1)
                        if kt >= 2:
                            pool.wait_ge(s.added, (T - 1) * g + kt - 1)
                        one = prob[:, 0] if kt == 1 else total[:, par]
                        pool.tensor_tensor(total[:, par], one, prob[:, kt % NPB], ALU.add).then_inc(s.added, 1)

                pairs(pool, head, lambda: None)

            @block.scalar
            def _(act):
                def split_q(par, n, j, c):
                    act.wait_ge(s.task, A_N * n + j + 1)
                    cols = slice(c * HALF, (c + 1) * HALF)
                    act.activation(qa[:, par, cols], ps[A_BANKS[j % 3]], ACT.Copy).then_inc(s.split, 1)
                    act.activation(qb[0:C, par, cols], ps[A_BANKS[j % 3]][0:C], ACT.Copy).then_inc(s.split, 1)

                def split_k(par, n, j, c):
                    act.wait_ge(s.task, A_N * n + j + 1)
                    act.activation(ka[:, par, c * HALF:(c + 1) * HALF], ps[A_BANKS[j % 3]], ACT.Copy)\
                       .then_inc(s.split, 1)

                def prologue():
                    for j, kind, c in listed(0) + listed(1):
                        if kind == "q":
                            split_q(0, 0, j, c)
                        if kind == "k":
                            split_k(0, 0, j, c)

                def head(par, g, first, last):
                    for kt in range(T):
                        act.wait_ge(s.scores, T * g + kt + 1)
                        if kt >= NPB:
                            act.wait_ge(s.pv, T * g + kt - NPB + 1)
                            act.wait_ge(s.added, (T - 1) * g + max(1, kt - NPB))
                        elif not first:
                            act.wait_ge(s.pv, T * g + kt - NPB + 1)
                            act.wait_ge(s.added, (T - 1) * (g - 1) + max(1, kt + T - NPB))
                        act.activation(prob[:, kt % NPB], k.psum[:, 2 * (kt % 2):2 * (kt % 2) + 2].rearrange("p b n -> p (b n)"),
                                       ACT.Exp, scale=k.escale[:]).then_inc(s.exp, 1)
                        if kt in (0, 1) and not last:
                            for j, kind, c in listed(kt):
                                if kind == "q":
                                    split_q(1 - par, g + 1, j, c)
                                if kind == "k":
                                    split_k(1 - par, g + 1, j, c)
                        if kt == 0 and not first:
                            copy_out(1 - par, g - 1)

                def copy_out(par, g):
                    act.wait_ge(s.pv, T * (g + 1))
                    act.activation(un[:, par], ps[6], ACT.Copy).then_inc(s.copied, 1)

                pairs(act, head, prologue)
                copy_out(1, heads - 1)

            @block.tensor
            def _(pe):
                def task(par, n, j, kind, c, skip=False):
                    bank = ps[A_BANKS[j % 3]]
                    if skip:
                        if not (isinstance(n, int) and A_N * n + j == 0):
                            pe.wait_ge(s.task, A_N * n + j)
                        pe.sem_inc(s.task, 1)
                        return
                    if not (isinstance(n, int) and n == 0 and j < 3):
                        pe.wait_ge(s.taken, A_N * n + j - 2)
                    if kind in ("q", "k"):
                        h, b = n % HEADS, n // HEADS
                        which = 0 if kind == "q" else 1
                        rhs = k.xa[:, ds(b * S + c * HALF, HALF)]
                        for w, start in ((k.wqk_hi, True), (k.wqk_lo, False)):
                            flat = w[:].rearrange("p a h b c -> p (a h b c)")
                            last = pe.matmul(bank, lhsT=flat[:, ds(h * P + which * HEADS * P, P)], rhs=rhs,
                                             start=start, stop=not start)
                    elif kind == "v":
                        h, b = n % HEADS, n // HEADS
                        for t in range(T):
                            for w, start in ((k.wvo_hi, True), (k.wvo_lo, False)):
                                last = pe.matmul(bank[:, t * C:(t + 1) * C], lhsT=k.xa[:, ds(b * S + t * P, P)],
                                                 rhs=w[:, ds(h * C, C)], start=(t == 0 and start), stop=not start,
                                                 skip_group_check=True)
                    elif kind == "max":
                        if c == 0:
                            pe.wait_ge(s.taken, A_N * n + TAKEN["k", 1] + 1)
                        last = pe.matmul(bank, lhsT=qa[:, par, (c // 2) * P:(c // 2 + 1) * P],
                                         rhs=ka[:, par, (c % 2) * HALF:(c % 2 + 1) * HALF], start=True, stop=True)
                    elif kind == "row":
                        pe.wait_ge(s.maxima, n + 1)
                        for t in range(T):
                            last = pe.transpose(bank[C:C + 2].bitcast(FP16)[:, t * P:(t + 1) * P], mm[:, t], k.identh[:])
                    elif kind == "den":
                        pe.wait_ge(s.added, (T - 1) * (n - 1))
                        for t in range(T):
                            last = pe.matmul(bank[:, t:t + 1], lhsT=total[:, par, t * P:(t + 1) * P],
                                             rhs=k.ones[:, 0:1], start=(t == 0), stop=True, skip_group_check=True)
                    elif kind == "out":
                        pe.wait_ge(s.copied, n - 1)
                        for t in range(4):
                            last = pe.transpose(bank[:, t * P:(t + 1) * P], un[:, par, t * P:(t + 1) * P], k.ident[:])
                    last.then_inc(s.task, 1)

                def prologue():
                    for slot in range(T):
                        for j, kind, c in listed(slot):
                            task(0, 0, j, kind, c, skip=kind not in NEXT)

                def score(par, g, kt, first):
                    if kt == 0:
                        pe.wait_ge(s.taken, A_N * (g + 1))
                    if kt >= 2 or not first:
                        pe.wait_ge(s.exp, T * g + kt - 1)
                    keys = slice(kt * P, (kt + 1) * P)
                    for half in range(2):
                        bank = ps[2 * (kt % 2) + half]
                        cols = slice(half * HALF, (half + 1) * HALF)
                        pe.matmul(bank, lhsT=ka[:, par, keys], rhs=qa[:, par, cols], start=True, stop=False)
                        last = pe.matmul(bank, lhsT=kb[:, par, keys], rhs=qb[:, par, cols], start=False, stop=True)
                    last.then_inc(s.scores, 1)

                def values(par, g, kt):
                    pe.wait_ge(s.exp, T * g + kt + 1)
                    if kt == 0 and not (isinstance(g, int) and g == 0):
                        pe.wait_ge(s.copied, g)
                    for half in range(2):
                        last = pe.matmul(ps[6][half * C:(half + 1) * C], lhsT=v[:, par, kt],
                                         rhs=prob[:, kt % NPB, half * HALF:(half + 1) * HALF],
                                         start=(kt == 0), stop=(kt == T - 1), skip_group_check=True)
                    last.then_inc(s.pv, 1)

                def head(par, g, first, last):
                    for kt in range(T):
                        score(par, g, kt, first)
                        tasks = listed(kt)
                        for j, kind, c in tasks[:2]:
                            task(1 - par, g + 1, j, kind, c, skip=not wanted(kind, g, first, last))
                        if kt:
                            values(par, g, kt - 1)
                        elif not first:
                            values(1 - par, g - 1, T - 1)
                        for j, kind, c in tasks[2:]:
                            task(1 - par, g + 1, j, kind, c, skip=not wanted(kind, g, first, last))

                pe.wait_ge(s.start, 1)
                pairs(pe, head, prologue)
                values(1, heads - 1, T - 1)
                for j, kind in ((0, "den"), (1, "out")):
                    task(1, heads + 1, j, kind, 0)

            @block.vector
            def _(dve):
                def task(par, n, j, kind, c, link, skip=False):
                    bank = ps[A_BANKS[j % 3]]
                    if skip:
                        if not (isinstance(n, int) and A_N * n + j == 0):
                            dve.wait_ge(s.taken, A_N * n + j)
                        dve.sem_inc(s.taken, 1)
                        return
                    dve.wait_ge(s.task, A_N * n + j + 1)
                    cols = slice(c * HALF, (c + 1) * HALF)
                    if kind == "q":
                        dve.wait_ge(s.split, 6 * n + 2 * c + 2)
                        dve.tensor_tensor(qa[C:P, par, cols], bank[C:P], qa[C:P, par, cols], ALU.subtract)\
                           .then_inc(s.taken, 1)
                    elif kind == "k":
                        dve.wait_ge(s.split, 6 * n + 5 + c)
                        dve.tensor_tensor(kb[0:C, par, cols], bank[0:C], ka[0:C, par, cols], ALU.subtract)\
                           .then_inc(s.taken, 1)
                    elif kind == "v":
                        dve.tensor_copy(v[:, par].rearrange("p t c -> p (t c)"), bank).then_inc(s.taken, 1)
                    elif kind == "max":
                        dve.tensor_reduce(mp[:, c // 2, c % 2:c % 2 + 1], bank, X, ALU.max).then_inc(s.taken, 1)
                        if c == 2 * T - 1:
                            dve.wait_ge(s.taken, A_N * n + j + 1)
                            link(dve.tensor_reduce(mx[:, 0], mp[:], X, ALU.max))
                            link(dve.tensor_scalar(mx[:, 0], mx[:, 0], -1.0 / MSPAN, None, ALU.mult))
                            link(dve.tensor_copy(mm[:, :, 0], mx[:, 0]))
                            link(dve.tensor_tensor(mm[:, :, 1], mx[:, 0], mm[:, :, 0], ALU.subtract))
                            dve.sem_inc(s.maxima, 1)
                    elif kind == "row":
                        dve.tensor_copy(qb[C:C + 2, par], bank[C:C + 2].bitcast(FP16)).then_inc(s.taken, 1)
                    elif kind == "den":
                        link(dve.reciprocal(inv[:], bank[:, 0:T]))
                        link(dve.tensor_scalar(inv[:], inv[:], k.vscale[:], None, ALU.mult))
                        dve.sem_inc(s.taken, 1)
                    elif kind == "out":
                        b = (n - 2) // HEADS
                        link(dve.tensor_tensor(u[:].rearrange("p (a t) c -> p t a c", a=2),
                                               bank.rearrange("p (t a c) -> p t a c", t=4, a=2),
                                               inv[:].rearrange("p (a t) -> p t a", a=2).unsqueeze(3)
                                               .to_broadcast([P, 4, 2, C]), ALU.mult))
                        dve.sem_inc(s.taken, 1)
                        at = k.h[:, ds(b * T, T), :]
                        link(dve.tensor_tensor(at, at, u[:], ALU.add))

                def tasks(par, n, skipped, steps):
                    for slot in range(T):
                        for j, kind, c in listed(slot):
                            task(par, n, j, kind, c, steps, skip=kind in skipped)

                def prologue():
                    link = Chain(dve, s.d, 0, D_STEPS)
                    tasks(0, 0, ("den", "out"), link)
                    link.fill(dve)

                def head(par, g, first, last):
                    link = Chain(dve, s.d, g + 1, D_STEPS)
                    skipped = (NEXT if last else ()) + (("den", "out") if first else ())
                    tasks(1 - par, g + 1, skipped, link)
                    link.fill(dve)

                for t in (kb,):
                    dve.memset(t[C:C + 2], MSPAN).then_inc(s.start, 1)
                pairs(dve, head, prologue)
                link = Chain(dve, s.d, heads + 1, D_STEPS)
                for j, kind in ((0, "den"), (1, "out")):
                    task(1, heads + 1, j, kind, 0, link)


F_UNITS = [(half, kt, pair) for half in range(2) for kt in range(4 * half + 4) for pair in range(2)]
F_PIECES = (
    ((0, 0, 128, 0), (2, 0, 384, 128)),
    ((3, 0, 512, 0),),
    ((1, 0, 256, 0), (5, 512, 256, 256)),
    ((4, 0, 512, 0),),
    ((4, 512, 128, 0), (6, 512, 384, 128)),
    ((5, 0, 512, 0),),
    ((6, 0, 512, 0),),
    ((7, 0, 512, 0),),
    ((7, 512, 512, 0),),
)
NV = len(F_PIECES)


def f_slots(sequence):
    slots = [[] for _ in F_UNITS]
    if sequence:
        for at, step in ((16, ("turn", 0)), (17, ("turn", 1)), (19, ("sv", 0)), (20, ("sv", 1)), (21, ("sv", 2))):
            slots[at].append(step)
    slots[0] += [("k", 0)]
    slots[1] += [("k", 1)]
    slots[4] += [("out", 1)]
    slots[11] += [("out", 0)]
    for e in range(NE):
        first = (2, 5, 9, 13)[e]
        slots[first].insert(0, ("q", 2 * e))
        slots[first + 1].insert(0, ("q", 2 * e + 1))
        for v in range(NV):
            slots[6 + (e * NV + v) * 16 // (NE * NV)].append(("max", e * NV + v))
    for e in range(NE):
        slots[(11, 15, 19, 23)[e]].append(("row", e))
    for at, half in ((7, 1), (15, 0)):
        slots[at].append(("gate", half))
        slots[at + 2].append(("mix", half))
        slots[at + 4].append(("sum", half))
    return slots


NPF = 6
BANKLESS = ("gate", "mix", "sum")
NEXT_F = ("k", "q", "max", "row")


def f_numbered(sequence):
    j, out = 0, []
    for slot in f_slots(sequence):
        row = []
        for kind, c in slot:
            row.append((None if kind in BANKLESS else j, kind, c))
            j += kind not in BANKLESS
        out.append(row)
    return out, j


def feedforward1(k, nc):
    NB = k.NB
    ps = k.bank
    lists = [f_numbered(m == NH - 2) for m in range(NH)]
    sizes = [n for _, n in lists]
    TB, BEFORE = sum(sizes), sizes[2] + sizes[3]
    assert TB % len(A_BANKS) == 0
    PIECES = 2 + 2 * NE
    number = [{(kind, c): j for slot in sl for j, kind, c in slot} for sl, _ in lists]
    units = len(F_UNITS)
    groups = units // 2
    with ExitStack() as ctx:
        def sb(name, shape, dt):
            return ctx.enter_context(nc.sbuf_tensor(name, shape, dt))

        hb = sb("f_hb", [P, T, C], F32)
        hT = sb("f_hT", [C + 1, S], F32)
        sv = sb("f_sv", [P, T, 2 * C], F32)
        vh = sb("f_vh", [P, 2, T, 32], F32)
        nz = sb("f_nz", [P, NH, T, D], F32)
        qf = sb("f_qf", [P, 2, NE, S], BF16)
        kf = sb("f_kf", [P, 2, S], BF16)
        raw = sb("f_raw", [P, 2, HALF], F32)
        p1 = sb("f_p1", [P, 2, HALF], BF16)
        r1 = sb("f_r1", [P, 2, HALF], F32)
        p2 = sb("f_p2", [P, 2, HALF], BF16)
        prob = sb("f_prob", [P, NPF, 2, HALF], F32)
        oc = sb("f_oc", [P, 2, HALF], F32)
        rs = sb("f_rs", [P, 2, 4 * NE], F32)
        o = sb("f_o", [P, 2, 4, NE, D], F32)
        prod = sb("f_prod", [P, 2, 4, NE, NE * D], F32)
        lg = sb("f_lg", [P, 4, NE], F32)
        eg = sb("f_eg", [P, 4, NE], F32)
        gs = sb("f_gs", [P, 2, 4, NE], F32)
        gm = sb("f_gm", [P, 3, 4], F32)
        mp = sb("f_mp", [P, 4, 2], F32)
        mx = sb("f_mx", [P, T], F32)
        mm = sb("f_mm", [P, 2, T, 2], BF16)

        s = Parts()
        s.start = k.sem("f_start")
        s.tokens = k.sem("f_tokens")
        s.task = k.sem("f_task")
        s.taken = k.sem("f_taken")
        s.part1 = k.sem("f_part1")
        s.rest = k.sem("f_rest")
        s.raw = k.sem("f_raw_ready")
        s.part2 = k.sem("f_part2")
        s.laid = k.sem("f_laid")
        s.scores = k.sem("f_scores")
        s.exp = k.sem("f_exp")
        s.pv = k.sem("f_pv")
        s.copied = k.sem("f_copied")
        s.maxima = k.sem("f_maxima")
        s.o_ready = k.sem("f_o_ready")
        s.prod_ready = k.sem("f_prod_ready")
        s.lg_ready = k.sem("f_lg_ready")
        s.eg_ready = k.sem("f_eg_ready")
        s.gs_ready = k.sem("f_gs_ready")
        s.mix_ready = k.sem("f_mix_ready")
        s.d = k.sem("f_d")
        assert units % NPF == 0
        D_STEPS = 44

        def base(m, b):
            return TB * b + BEFORE + sum(sizes[:m])

        def heads(eng, run_list, head):
            run_list(2, 0, -2, False, 0)
            run_list(3, sizes[2], -1, False, 0)

            def sequence(b, first, last):
                for m in range(NH):
                    head(m, b, first and m == 0, max(0, m + 3 - NH) if last else 0)

            sequence(0, True, False)
            if NB > 2:
                with eng.Fori(1, NB - 1) as b:
                    sequence(b, False, False)
            sequence(NB - 1, False, True)

        def left_out(kind, c, g, first, last):
            if kind in ("turn", "sv"):
                return last > 0
            if kind in NEXT_F:
                return last == 2 or (isinstance(g, int) and g == -2)
            if isinstance(g, int) and g < 0:
                return True
            return first and c == 1

        with nc.Block() as block:
            @block.gpsimd
            def _(pool):
                def rest(g, n):
                    count = PIECES * (g + 1) + n + 1
                    pool.wait_ge(s.part1, count)
                    if not (isinstance(g, int) and g < 0 and n < 2):
                        pool.wait_ge(s.laid, count - 2)
                    pool.tensor_tensor(r1[:, n % 2], raw[:, n % 2], p1[:, n % 2], ALU.subtract).then_inc(s.rest, 1)

                def lay(par, g, n):
                    count = PIECES * (g + 1) + n + 1
                    pool.wait_ge(s.part2, count)
                    dst = kf[:, 1 - par, (n % 2) * HALF:(n % 2 + 1) * HALF] if n < 2 else \
                        qf[:, 1 - par, (n - 2) // 2, (n % 2) * HALF:(n % 2 + 1) * HALF]
                    pool.tensor_tensor(dst, r1[:, n % 2], p2[:, n % 2], ALU.subtract).then_inc(s.laid, 1)

                def mixture(m, g, kind, c):
                    mo, go = (m, g) if c == 0 else ((m + 3) % 4, g - 1)
                    if kind == "out":
                        pool.wait_ge(s.o_ready, 2 * go + c + 1)
                        pool.tensor_tensor(
                            prod[:, c], o[:, c].rearrange("p t e d -> p t (e d)").unsqueeze(2)
                            .to_broadcast([P, 4, NE, NE * D]),
                            k.gatew[:, mo].unsqueeze(1).to_broadcast([P, 4, NE, NE * D]), ALU.mult)\
                            .then_inc(s.prod_ready, 1)
                    else:
                        pool.wait_ge(s.gs_ready, 2 * go + c + 1)
                        pool.tensor_tensor(
                            prod[:, c, :, 0].rearrange("p t (e d) -> p t e d", e=NE), o[:, c],
                            gs[:, c].unsqueeze(3).to_broadcast([P, 4, NE, D]), ALU.mult)\
                            .then_inc(s.mix_ready, 1)

                def run_list(m, at, g, first, last):
                    par = m % 2
                    before = []
                    for slot in lists[m][0]:
                        here = [x for x in slot if not left_out(x[1], x[2], g, first, last)]
                        pieces = [c if kind == "k" else 2 + c for _, kind, c in here if kind in ("k", "q")]
                        for n in pieces:
                            rest(g, n)
                        for n in before:
                            lay(par, g, n)
                        before = pieces
                        for _, kind, c in here:
                            if kind in ("out", "mix"):
                                mixture(m, g, kind, c)

                def head(m, b, first, last):
                    run_list(m, base(m, b), b * NH + m, first, last)
                    if m == 1:
                        tokens(b + 1)

                def tokens(b):
                    if isinstance(b, int) and b == NB:
                        return
                    if not (isinstance(b, int) and b == 0):
                        passed(pool, k.seen, s.task, base(0, b - 1))
                    pool.tensor_copy(hb[:], k.mixed[:, ds(b * T, T)].rearrange("p t n d -> p t (n d)")).then_inc(s.tokens, 1)

                tokens(0)
                heads(pool, run_list, head)
                for kind in ("out", "mix"):
                    mixture(0, NB * NH, kind, 1)

            @block.scalar
            def _(act):
                def run_slot(m, u, at, g, first, last):
                    def pieces(u):
                        return [(j, c if kind == "k" else 2 + c) for j, kind, c in lists[m][0][u]
                                if kind in ("k", "q") and not left_out(kind, c, g, first, last)]

                    for j, n in pieces(u - 2) if u > 1 else ():
                        side = 2 if n < 2 else 0
                        count = PIECES * (g + 1) + n + 1
                        act.wait_ge(s.rest, count)
                        if not (isinstance(g, int) and g < 0 and n < 2):
                            act.wait_ge(s.laid, count - 2)
                        act.activation(p2[:, n % 2], r1[:, n % 2], ACT.Copy, scale=k.part[:, side + 1:side + 2])\
                           .then_inc(s.part2, 1)
                    for j, n in pieces(u - 1) if u else ():
                        side = 2 if n < 2 else 0
                        act.wait_ge(s.raw, PIECES * (g + 1) + n + 1)
                        act.activation(p1[:, n % 2], raw[:, n % 2], ACT.Copy, scale=k.part[:, side:side + 1])\
                           .then_inc(s.part1, 1)

                    for j, n in pieces(u):
                        act.wait_ge(s.task, at + j + 1)
                        if not (isinstance(g, int) and g < 0 and n < 2):
                            act.wait_ge(s.rest, PIECES * (g + 1) + n - 1)
                        act.activation(raw[:, n % 2], ps[A_BANKS[(at_static[m] + j) % 3]], ACT.Copy).then_inc(s.raw, 1)

                def copy_out(g, half):
                    act.wait_ge(s.pv, groups * g + (4 if half == 0 else groups))
                    if not (isinstance(g, int) and g == 0):
                        act.wait_ge(s.o_ready, 2 * g + half - 1)
                    act.activation(oc[:, half], ps[6], ACT.Copy).then_inc(s.copied, 1)

                def gates(g, half):
                    act.wait_ge(s.lg_ready, 2 * g + half + 1)
                    act.activation(eg[:], lg[:], ACT.Exp).then_inc(s.eg_ready, 1)

                def run_list(m, at, g, first, last):
                    for u in range(units):
                        run_slot(m, u, at, g, first, last)

                def head(m, b, first, last):
                    g = b * NH + m
                    for u, (half, kt, pair) in enumerate(F_UNITS):
                        run_slot(m, u, base(m, b), g, first, last)
                        off = max(0, kt * P - half * HALF)
                        act.wait_ge(s.scores, units * g + u + 1)
                        if u >= NPF or not first:
                            act.wait_ge(s.pv, groups * g + (u - NPF) // 2 + 1)
                        act.activation(prob[:, u % NPF, :, 0:HALF - off],
                                       k.psum[:, 2 * (u % 2):2 * (u % 2) + 2, 0:HALF - off], ACT.Exp,
                                       scale=float(np.sqrt(D))).then_inc(s.exp, 1)
                        if u == 1 and not first:
                            copy_out(g - 1, 1)
                        if u == 9:
                            copy_out(g, 0)
                        if u == 8 and not first:
                            gates(g - 1, 1)
                        if u == 16:
                            gates(g, 0)

                at_static = [(BEFORE + sum(sizes[:m])) % 3 for m in range(NH)]
                heads(act, run_list, head)
                copy_out(NB * NH - 1, 1)
                gates(NB * NH - 1, 1)

            @block.tensor
            def _(pe):
                at_static = [(BEFORE + sum(sizes[:m])) % 3 for m in range(NH)]

                def task(m, at, j, kind, c, g, skip):
                    bank = ps[A_BANKS[(at_static[m] + j) % 3]]
                    par = 1 - m % 2
                    n = (m + 1) % NH
                    if skip:
                        if not (isinstance(at, int) and at + j == 0):
                            pe.wait_ge(s.task, at + j)
                        pe.sem_inc(s.task, 1)
                        return
                    if kind == "turn" and not (isinstance(at, int) and at + j < 3):
                        passed(pe, k.seen, s.taken, at + j - 2)
                    elif not (isinstance(at, int) and at + j < 3):
                        pe.wait_ge(s.taken, at + j - 2)
                    if kind == "turn":
                        if c == 0:
                            passed(pe, k.seen, s.tokens, (g + 2) // NH + 1)
                        for t in range(4):
                            last = pe.transpose(bank[0:C, t * P:(t + 1) * P], hb[:, 4 * c + t], k.ident[:])
                    elif kind == "sv":
                        if c == 0:
                            pe.wait_ge(s.taken, at + j)
                        for x, t in enumerate(range(3 * c, min(3 * c + 3, T))):
                            last = pe.matmul(bank[:, x * P:(x + 1) * P], lhsT=hT[:, t * P:(t + 1) * P], rhs=k.gsv[:],
                                             start=(x == 0), stop=True, skip_group_check=True)
                    elif kind in ("k", "q"):
                        cols = slice((c % 2) * HALF, (c % 2 + 1) * HALF)
                        w = k.gk[:, n] if kind == "k" else k.gq[:, n, c // 2]
                        last = pe.matmul(bank, lhsT=w.rearrange("i s d -> i (s d)"), rhs=hT[:, cols], start=True, stop=True)
                    elif kind == "max":
                        e, v = c // NV, c % NV
                        if v in (0, 2):
                            pe.wait_ge(s.laid, PIECES * (g + 1) + 2 + 2 * e + 1 + v // 2)
                        for x, (qt, k0, nk, col) in enumerate(F_PIECES[v]):
                            diagonal = k0 + nk == (qt + 1) * P
                            last = pe.matmul(bank[:, col:col + nk], lhsT=qf[:, par, e, qt * P:(qt + 1) * P],
                                             rhs=kf[:, par, k0:k0 + nk], start=(x == 0), stop=not diagonal,
                                             skip_group_check=True)
                            if diagonal:
                                last = pe.matmul(bank[:, col + nk - P:col + nk], lhsT=k.identb[:], rhs=k.mask_q[:],
                                                 start=False, stop=True, skip_group_check=True)
                    elif kind == "row":
                        pe.wait_ge(s.maxima, NE * (g + 1) + c + 1)
                        for t in range(T):
                            last = pe.transpose(bank[32:34].bitcast(BF16)[:, t * P:(t + 1) * P], mm[:, c % 2, t], k.identb[:])
                    elif kind == "out":
                        gh = g if c == 0 else g - 1
                        pe.wait_ge(s.copied, 2 * gh + c + 1)
                        for t in range(4):
                            last = pe.transpose(bank[:, t * P:(t + 1) * P], oc[:, c, t * P:(t + 1) * P], k.ident[:])
                    last.then_inc(s.task, 1)

                def run_slot(m, u, at, g, first, last, part=slice(None)):
                    for j, kind, c in [x for x in lists[m][0][u] if x[0] is not None][part]:
                        task(m, at, j, kind, c, g, left_out(kind, c, g, first, last))

                def run_list(m, at, g, first, last):
                    pe.wait_ge(s.start, 4)
                    for u in range(units):
                        run_slot(m, u, at, g, first, last)

                def score(m, g, u, first):
                    half, kt, pair = F_UNITS[u]
                    par = m % 2
                    if u >= 2 or not first:
                        pe.wait_ge(s.exp, units * g + u - 1)
                    off = max(0, kt * P - half * HALF)
                    q0 = half * HALF + off
                    for x in range(2):
                        e = 2 * pair + x
                        bank = ps[2 * (u % 2) + x]
                        diagonal = kt * P >= half * HALF
                        last = pe.matmul(bank[:, 0:HALF - off], lhsT=kf[:, par, kt * P:(kt + 1) * P],
                                         rhs=qf[:, par, e, q0:(half + 1) * HALF], start=True, stop=not diagonal,
                                         skip_group_check=True)
                        if diagonal:
                            last = pe.matmul(bank[:, 0:P], lhsT=k.identb[:], rhs=k.mask_k[:], start=False, stop=True,
                                             skip_group_check=True)
                    last.then_inc(s.scores, 1)

                def values(m, g, grp):
                    half, kt, _ = F_UNITS[2 * grp]
                    par = m % 2
                    off = max(0, kt * P - half * HALF)
                    pe.wait_ge(s.exp, units * g + 2 * grp + 2)
                    if kt == 0 and not (half == 0 and isinstance(g, int) and g == 0):
                        pe.wait_ge(s.copied, 2 * g + half)
                    for e in range(NE):
                        last = pe.matmul(ps[6][32 * e:32 * e + 32, off:HALF], lhsT=vh[:, par, kt],
                                         rhs=prob[:, (2 * grp + e // 2) % NPF, e % 2, 0:HALF - off],
                                         start=(kt == 0), stop=(kt == 4 * half + 3), skip_group_check=True)
                    last.then_inc(s.pv, 1)

                def head(m, b, first, last):
                    g = b * NH + m
                    at = base(m, b)
                    pe.wait_ge(s.taken, at)
                    for u in range(units):
                        lead = int(any(x[0] is not None for x in lists[m][0][u]) and lists[m][0][u][0][1] != "row")
                        run_slot(m, u, at, g, first, last, slice(0, lead))
                        score(m, g, u, first)
                        run_slot(m, u, at, g, first, last, slice(lead, 2 * lead))
                        if u == 1 and not first:
                            values(1 - m % 2, g - 1, groups - 1)
                        if u % 2 == 1 and u > 1:
                            values(m, g, (u - 3) // 2)
                        run_slot(m, u, at, g, first, last, slice(2 * lead, None))

                heads(pe, run_list, head)
                values(1, NB * NH - 1, groups - 1)
                task(0, base(0, NB), 0, "out", 1, NB * NH, False)

            @block.vector
            def _(dve):
                at_static = [(BEFORE + sum(sizes[:m])) % 3 for m in range(NH)]

                def task(m, at, j, kind, c, g, skip, link):
                    par = 1 - m % 2
                    n = (m + 1) % NH
                    if skip:
                        if j is not None:
                            if not (isinstance(at, int) and at + j == 0):
                                dve.wait_ge(s.taken, at + j)
                            dve.sem_inc(s.taken, 1)
                        return
                    if j is not None:
                        bank = ps[A_BANKS[(at_static[m] + j) % 3]]
                        dve.wait_ge(s.task, at + j + 1)
                    mo, go = (m, g) if c == 0 else ((m + 3) % 4, g - 1)
                    if kind == "turn":
                        dve.tensor_copy(hT[0:C, c * HALF:(c + 1) * HALF], bank[0:C]).then_inc(s.taken, 1)
                    elif kind == "sv":
                        t0, t1 = 3 * c, min(3 * c + 3, T)
                        dve.tensor_copy(sv[:, t0:t1], bank[:, 0:(t1 - t0) * P].rearrange("p (t x) -> p t x", x=P))\
                           .then_inc(s.taken, 1)
                    elif kind in ("k", "q"):
                        x = c if kind == "k" else 2 + c
                        if kind == "k" and c == 0:
                            if n == 0:
                                dve.wait_ge(s.taken, at + j)
                            link(dve.tensor_scalar(nz[:, n], sv[:, :, n * D:(n + 1) * D], 0.0, None, ALU.not_equal))
                        if kind == "q" and c == 0:
                            link(dve.tensor_copy(vh[:, par, :, 0:D], sv[:, :, C + n * D:C + (n + 1) * D]))
                        if not (isinstance(at, int) and at + j == 0):
                            dve.wait_ge(s.taken, at + j)
                        dve.wait_ge(s.raw, PIECES * (g + 1) + x + 1)
                        dve.sem_inc(s.taken, 1)
                    elif kind == "max":
                        e, v = c // NV, c % NV
                        pieces = F_PIECES[v]
                        for x, (qt, k0, nk, col) in enumerate(pieces):
                            to = mx[:, qt:qt + 1] if qt < 4 else mp[:, qt - 4, k0 // HALF:k0 // HALF + 1]
                            ins = dve.tensor_reduce(to, bank[:, col:col + nk], X, ALU.max)
                            if x == len(pieces) - 1:
                                ins.then_inc(s.taken, 1)
                            else:
                                link.mark(ins)
                        if v == NV - 1:
                            dve.wait_ge(s.taken, at + j + 1)
                            link.settle()
                            link(dve.tensor_reduce(mx[:, 4:8], mp[:], X, ALU.max))
                            link(dve.tensor_scalar(mm[:, e % 2, :, 0], mx[:], -1.0, None, ALU.mult))
                            link(dve.scalar_tensor_tensor(mm[:, e % 2, :, 1], mx[:], -1.0, mm[:, e % 2, :, 0],
                                                          ALU.mult, ALU.subtract))
                            dve.sem_inc(s.maxima, 1)
                    elif kind == "row":
                        dve.tensor_copy(qf[32:34, par, c], bank[32:34].bitcast(BF16)).then_inc(s.taken, 1)
                    elif kind == "out":
                        all_ = bank.rearrange("p (g x) -> p g x", x=32)
                        link(dve.reciprocal(rs[:, c], all_[:, :, D]))
                        o_c = o[:, c].rearrange("p t e d -> p (t e) d")
                        link(dve.tensor_tensor(o_c, all_[:, :, 0:D], wide(rs[:, c], D), ALU.mult))
                        link(dve.tensor_tensor(
                            o[:, c], o[:, c], nz[:, mo, 4 * c:4 * c + 4].unsqueeze(2).to_broadcast([P, 4, NE, D]), ALU.mult))
                        dve.sem_inc(s.o_ready, 1)
                        dve.sem_inc(s.taken, 1)
                    elif kind == "gate":
                        dve.wait_ge(s.prod_ready, 2 * go + c + 1)
                        link(dve.tensor_reduce(lg[:], prod[:, c], X, ALU.add))
                        link(dve.tensor_tensor(lg[:], lg[:], rows(k.gateb[:, mo], 4), ALU.add))
                        link(dve.tensor_reduce(gm[:, 0], lg[:], X, ALU.max))
                        dve.tensor_tensor(lg[:], lg[:], wide(gm[:, 0], NE), ALU.subtract).then_inc(s.lg_ready, 1)
                    elif kind == "mix":
                        dve.wait_ge(s.eg_ready, 2 * go + c + 1)
                        link(dve.tensor_reduce(gm[:, 1], eg[:], X, ALU.add))
                        link(dve.reciprocal(gm[:, 2], gm[:, 1]))
                        dve.tensor_tensor(gs[:, c], eg[:], wide(gm[:, 2], NE), ALU.mult).then_inc(s.gs_ready, 1)
                    elif kind == "sum":
                        dve.wait_ge(s.mix_ready, 2 * go + c + 1)
                        bo = go // NH
                        link(dve.tensor_reduce(k.mixed[:, ds(bo * T + 4 * c, 4), mo],
                                               prod[:, c, :, 0].rearrange("p t (e d) -> p t d e", e=NE), X, ALU.add))

                def run_list(m, at, g, first, last):
                    link = Chain(dve, s.d, g + 2, D_STEPS)
                    for u in range(units):
                        for j, kind, c in lists[m][0][u]:
                            task(m, at, j, kind, c, g, left_out(kind, c, g, first, last), link)
                    assert link.n <= D_STEPS, link.n
                    link.fill(dve)

                def head(m, b, first, last):
                    run_list(m, base(m, b), b * NH + m, first, last)

                dve.memset(hT[C:C + 1], 1.0).then_inc(s.start, 1)
                dve.memset(vh[:], 0.0).then_inc(s.start, 1)
                dve.wait_ge(s.start, 2)
                dve.memset(vh[:, :, :, D:D + 1], 1.0).then_inc(s.start, 2)
                heads(dve, run_list, head)
                link = Chain(dve, s.d, NB * NH + 2, D_STEPS)
                for j, kind in ((0, "out"), (None, "gate"), (None, "mix"), (None, "sum")):
                    task(0, base(0, NB), j, kind, 1, NB * NH, False, link)


def normalize1(k, nc):
    k.mixed = k.xa[:].bitcast(F32).rearrange("p (t n d) -> p t n d", n=NH, d=D)
    with ExitStack() as ctx:
        def sb(name, shape, dt):
            return ctx.enter_context(nc.sbuf_tensor(name, shape, dt))

        xc = sb("n_xc", [P, 2, T, C], F32)
        sq = sb("n_sq", [P, 2, T, C], F32)
        st = sb("n_st", [P, 2, 4, T], F32)
        d = k.sem("n_d")
        var, std = ([k.sem(f"n_{w}{j}") for j in range(2)] for w in ("var", "std"))
        with nc.Block() as block:
            @block.scalar
            def _(act):
                with act.Fori(0, k.NB // 2) as b:
                    for j in range(2):
                        root(act, st[:, j], k.eps_ln[:], C, var[j], std[j], b)

            @block.vector
            def _(dve):
                with dve.Fori(0, k.NB // 2) as b:
                    link = Chain(dve, d, b, 12)
                    for j in range(2):
                        at = ds((2 * b + j) * T, T)
                        normalize(dve, link, k.h[:, at], k.mixed[:, at].rearrange("p t n d -> p t (n d)"),
                                  xc[:, j], sq[:, j], st[:, j], C, var[j], std[j], b)
                    link.end()


def residual1(k, nc):
    ps = k.bank
    k.resid = k.sb("resid", [P, T, NH, D], F32)
    with ExitStack() as ctx:
        hT = ctx.enter_context(nc.sbuf_tensor("r_hT", [C + 1, S], F32))
        one, turned, copied, product, done = (k.sem("r_" + n) for n in ("one", "turned", "copied", "product", "done"))
        with nc.Block() as block:
            @block.tensor
            def _(pe):
                pe.wait_ge(one, 1)
                for n in range(NH):
                    if n:
                        pe.wait_ge(done, n)
                    for t in range(T):
                        last = pe.transpose(ps[t // 4][0:C, (t % 4) * P:(t % 4 + 1) * P],
                                            k.mixed[:, n * T + t].rearrange("p n d -> p (n d)"), k.ident[:])
                    last.then_inc(turned, 1)
                    pe.wait_ge(copied, n + 1)
                    for t in range(T):
                        last = pe.matmul(ps[2][:, t * D:(t + 1) * D], lhsT=hT[:, t * P:(t + 1) * P],
                                         rhs=k.gsv[:, n * D:(n + 1) * D], start=(t == 0), stop=True, skip_group_check=True)
                    last.then_inc(product, 1)

            @block.vector
            def _(dve):
                dve.memset(hT[C:C + 1], 1.0).then_inc(one, 1)
                for n in range(NH):
                    dve.wait_ge(turned, n + 1)
                    dve.tensor_copy(hT[0:C, :], k.psum[0:C, 0:2].rearrange("p a n -> p (a n)")).then_inc(copied, 1)
                    dve.wait_ge(product, n + 1)
                    dve.tensor_copy(k.resid[:, :, n], ps[2][:, 0:T * D].rearrange("p (t d) -> p t d", t=T)).then_inc(done, 1)


def finish1(k, nc, out):
    NB = k.NB
    ps = k.bank
    G = T * NH
    with ExitStack() as ctx:
        def sb(name, shape, dt):
            return ctx.enter_context(nc.sbuf_tensor(name, shape, dt))

        x = sb("z_x", [P, 2, G, D], F32)
        xc = sb("z_xc", [P, 2, G, D], F32)
        sq = sb("z_sq", [P, 2, G, D], F32)
        st = sb("z_st", [P, 2, 4, G], F32)
        fT = sb("z_fT", [C, 2, S], F32)
        nzT = sb("z_nzT", [C, 2, S], F32)
        h1 = sb("z_h1", [C, 2, S], F32)
        h2 = sb("z_h2", [C, 2, S], F32)
        lg = sb("z_lg", [P, 2, T, NH], F32)
        eg = sb("z_eg", [P, 2, T, NH], F32)
        gm = sb("z_gm", [P, 2, 3, T], F32)
        none = sb("z_none", [P, 1], F32)
        s = Parts()
        s.f_ready = k.sem("z_f_ready")
        s.turned = k.sem("z_turned")
        s.fc1 = k.sem("z_fc1")
        s.relu = k.sem("z_relu")
        s.h1_ready = k.sem("z_h1_ready")
        s.fT_ready = k.sem("z_fT_ready")
        s.ahead = k.sem("z_ahead")
        s.fc2 = k.sem("z_fc2")
        s.h2_ready = k.sem("z_h2_ready")
        s.back = k.sem("z_back")
        s.o_ready = k.sem("z_o_ready")
        s.turn_o = k.sem("z_turn_o")
        s.oT_ready = k.sem("z_oT_ready")
        s.gate = k.sem("z_gate")
        s.lg_ready = k.sem("z_lg_ready")
        s.eg_ready = k.sem("z_eg_ready")
        s.y_ready = k.sem("z_y_ready")
        s.stored = k.sem("z_stored")
        s.d = k.sem("z_d")
        var = [k.sem(f"z_var{j}") for j in range(2)]
        std = [k.sem(f"z_std{j}") for j in range(2)]
        DVE_STEPS = 56

        with nc.Block() as block:
            @block.scalar
            def _(act):
                with act.Fori(0, NB // 2) as i:
                    ahead = Chain(act, s.ahead, i, 2)

                    def table(function):
                        ahead(act.activation(none[:], k.ones[:, 0:1], function))

                    for j in range(2):
                        root(act, st[:, j], k.eps_ffn[:], D, var[0], std[0], i * 2 + j)
                    for j in range(2):
                        for half in range(2):
                            cols = slice(half * HALF, (half + 1) * HALF)
                            act.wait_ge(s.fc1, (i * 2 + j) * 2 + half + 1)
                            act.activation(h1[:, j, cols], ps[4 * j + 2 + half][0:C], ACT.Relu, bias=k.fcb[:, 0:1])\
                               .then_inc(s.relu, 1)
                    for j in range(2):
                        root(act, st[:, j], k.eps_ffn[:], D, var[1], std[1], i * 2 + j)
                    table(ACT.Exp)
                    for j in range(2):
                        act.wait_ge(s.turn_o, i * 2 + j + 1)
                        act.activation(fT[:, j], k.psum[0:C, 4 * j:4 * j + 2].rearrange("p a n -> p (a n)"), ACT.Copy)\
                           .then_inc(s.oT_ready, 1)
                    for j in range(2):
                        act.wait_ge(s.lg_ready, i * 2 + j + 1)
                        act.activation(eg[:, j], lg[:, j], ACT.Exp).then_inc(s.eg_ready, 1)
                    table(ACT.Sqrt)

            @block.tensor
            def _(pe):
                def turn(j, sig):
                    for t in range(T):
                        last = pe.transpose(ps[4 * j + t // 4][0:C, (t % 4) * P:(t % 4 + 1) * P],
                                            x[:, j, t * NH:(t + 1) * NH].rearrange("p n d -> p (n d)"), k.ident[:])
                    last.then_inc(sig, 1)

                with pe.Fori(0, NB // 2) as i:
                    for j in range(2):
                        passed(pe, k.seen, s.f_ready, i * 2 + j + 1)
                        turn(j, s.turned)
                    for j in range(2):
                        passed(pe, k.seen, s.fT_ready, i * 2 + j + 1)
                        for half in range(2):
                            pe.matmul(ps[4 * j + 2 + half][0:C], lhsT=k.fcT[:, 0], rhs=fT[:, j, half * HALF:(half + 1) * HALF],
                                      start=True, stop=True).then_inc(s.fc1, 1)
                    for j in range(2):
                        passed(pe, k.seen, s.h1_ready, i * 2 + j + 1)
                        for half in range(2):
                            last = pe.matmul(ps[4 * j + half][0:C], lhsT=k.fcT[:, 1], rhs=h1[:, j, half * HALF:(half + 1) * HALF],
                                             start=True, stop=True)
                        last.then_inc(s.fc2, 1)
                    for j in range(2):
                        passed(pe, k.seen, s.h2_ready, i * 2 + j + 1)
                        for t in range(T):
                            last = pe.transpose(ps[4 * j + 2][:, t * C:(t + 1) * C], h2[:, j, t * P:(t + 1) * P],
                                                k.ident[0:C, 0:C])
                        last.then_inc(s.back, 1)
                    for j in range(2):
                        passed(pe, k.seen, s.o_ready, i * 2 + j + 1)
                        turn(j, s.turn_o)
                    for j in range(2):
                        passed(pe, k.seen, s.oT_ready, i * 2 + j + 1)
                        for t in range(T):
                            last = pe.matmul(ps[4 * j + 3][:, t * NH:(t + 1) * NH], lhsT=fT[:, j, t * P:(t + 1) * P],
                                             rhs=k.fgT[:], start=(t == 0), stop=True, skip_group_check=True)
                        last.then_inc(s.gate, 1)

            @block.vector
            def _(dve):
                with dve.Fori(0, NB // 2) as i:
                    link = Chain(dve, s.d, i, DVE_STEPS)
                    for j in range(2):
                        link(dve.tensor_tensor(x[:, j].rearrange("p (t n) d -> p t (n d)", t=T),
                                               k.mixed[:, ds((i * 2 + j) * T, T)].rearrange("p t n d -> p t (n d)"),
                                               k.resid[:].rearrange("p t n d -> p t (n d)"), ALU.add))
                        normalize(dve, link, x[:, j], x[:, j], xc[:, j], sq[:, j], st[:, j], D, var[0], std[0], i * 2 + j)
                        link(dve.tensor_tensor(x[:, j], x[:, j], rows(k.lnp[:, 0], G), ALU.mult))
                        link(dve.tensor_tensor(x[:, j], x[:, j], rows(k.lnp[:, 1], G), ALU.add))
                        dve.sem_inc(s.f_ready, 1)
                    for j in range(2):
                        dve.wait_ge(s.turned, i * 2 + j + 1)
                        link(dve.tensor_copy(fT[:, j], k.psum[0:C, 4 * j:4 * j + 2].rearrange("p a n -> p (a n)")))
                        dve.sem_inc(s.fT_ready, 1)
                        link(dve.tensor_scalar(nzT[:, j], fT[:, j], 0.0, None, ALU.not_equal))
                    for j in range(2):
                        dve.wait_ge(s.relu, (i * 2 + j) * 2 + 2)
                        link(dve.tensor_tensor(h1[:, j], h1[:, j], nzT[:, j], ALU.mult))
                        dve.sem_inc(s.h1_ready, 1)
                    for j in range(2):
                        dve.wait_ge(s.fc2, i * 2 + j + 1)
                        link(dve.scalar_tensor_tensor(h2[:, j], k.psum[0:C, 4 * j:4 * j + 2].rearrange("p a n -> p (a n)"),
                                                      k.fcb[:, 1:2], nzT[:, j], ALU.add, ALU.mult))
                        link(dve.tensor_tensor(h2[:, j], h2[:, j], fT[:, j], ALU.add))
                        dve.sem_inc(s.h2_ready, 1)
                    for j in range(2):
                        dve.wait_ge(s.back, i * 2 + j + 1)
                        link(dve.tensor_copy(x[:, j], ps[4 * j + 2].rearrange("p (g d) -> p g d", d=D)))
                        normalize(dve, link, x[:, j], x[:, j], xc[:, j], sq[:, j], st[:, j], D, var[1], std[1], i * 2 + j)
                        link(dve.tensor_tensor(x[:, j], x[:, j], rows(k.lnp[:, 2], G), ALU.mult))
                        link(dve.tensor_tensor(x[:, j], x[:, j], rows(k.lnp[:, 3], G), ALU.add))
                        dve.sem_inc(s.o_ready, 1)
                    for j in range(2):
                        l, e, g = lg[:, j], eg[:, j], gm[:, j]
                        dve.wait_ge(s.gate, i * 2 + j + 1)
                        lg_in = ps[4 * j + 3][:, 0:T * NH].rearrange("p (t n) -> p t n", t=T)
                        link(dve.tensor_reduce(g[:, 0], lg_in, X, ALU.max))
                        dve.tensor_tensor(l, lg_in, wide(g[:, 0], NH), ALU.subtract).then_inc(s.lg_ready, 1)
                    for j in range(2):
                        e, g = eg[:, j], gm[:, j]
                        dve.wait_ge(s.eg_ready, i * 2 + j + 1)
                        link(dve.tensor_reduce(g[:, 1], e, X, ALU.add))
                        link(dve.reciprocal(g[:, 2], g[:, 1]))
                        link(dve.tensor_tensor(e, e, wide(g[:, 2], NH), ALU.mult))
                        link(dve.tensor_tensor(x[:, j], x[:, j], wide(e.rearrange("p t n -> p (t n)"), D), ALU.mult))
                        at = k.h[:, ds((i * 2 + j) * T, T)]
                        dve.tensor_tensor(at, at, x[:, j].rearrange("p (t n) d -> p t (n d)", t=T), ALU.add)\
                           .then_inc(s.y_ready, 1)
                        dve.wait_ge(s.y_ready, i * 2 + j + 1)
                    link.end()

            @block.sync
            def _(sp):
                with sp.Fori(0, NB) as b:
                    sp.wait_ge(s.y_ready, b + 1)
                    sp.dma_start(out[ds(b, 1)].rearrange("b (t p) c -> p (b t) c", p=P), k.h[:, ds(b * T, T)])\
                      .then_inc(s.stored, 16)
                sp.wait_ge(s.stored, 16 * NB)


_INS = ["x", "itok_BS_0_255", "itok_BS_0_511", "itok_BS_0_127", "itok_BS_0_63", "itok_BS_0_3"]


def tower(nc, NB, **t):
    k = Parts()
    k.NB = NB
    k.id_names = _INS
    k.ids = t
    a = {n.split("_", 2)[2]: v for n, v in t.items() if n[:3] in ("L0_", "L1_")}
    with ExitStack() as ctx:
        k.sb = lambda name, shape, dt: ctx.enter_context(nc.sbuf_tensor(name, shape, dt))
        k.sem = lambda name: ctx.enter_context(nc.semaphore(name))
        k.psum = ctx.enter_context(nc.psum_tensor("psum", [P, 8, 512], F32))
        k.bank = [k.psum[:, i] for i in range(8)]
        k.h = k.sb("h", [P, NB * T, C], F32)
        k.xa = k.sb("xa", [P, NB * S], FP16)
        k.seen = k.sem("seen")
        with ExitStack() as setup:
            k.tmp = lambda name, shape, dt: setup.enter_context(nc.sbuf_tensor(name, shape, dt))
            load_weights(k, nc, a)
            constants(k, nc)
            prepare(k, nc)
        layer0(k, nc, a)
        attention1(k, nc)
        normalize1(k, nc)
        residual1(k, nc)
        feedforward1(k, nc)
        finish1(k, nc, t["out"])


def kernel(**inputs):
    import numpy as _np
    import concourse.bacc as _bacc
    from concourse import mybir as _mybir
    from concourse.bass_utils import run_bass_kernel_spmd as _run

    nc = _bacc.Bacc("TRN2", target_bir_lowering=False, num_devices=1)
    arrays, args = {}, {}
    for name, value in inputs.items():
        a = _np.ascontiguousarray(value)
        arrays[f"in_{name}_dram"] = a
        args[name] = nc.dram_tensor(f"in_{name}_dram", a.shape, _mybir.dt.from_np(a.dtype), kind="ExternalInput").ap()
    NB = inputs["x"].shape[0]
    args["out"] = nc.dram_tensor("out_0_dram", (NB, S, C), _mybir.dt.float32, kind="ExternalOutput").ap()
    tower(nc, NB, **args)
    r = _run(nc, [arrays], core_ids=[0])
    return r.results[0]["out_0_dram"]
```
